# Optimizing a Trainium2 kernel written in Bass

```python
import numpy as np
import jax
import jax.numpy as jnp

def _softmax(x, axis=-1):
    return jax.nn.softmax(x, axis=axis)

def _gelu(x):
    return jax.nn.gelu(x, approximate=True)

def _silu(x):
    return jax.nn.silu(x)

def _sigmoid(x):
    return jax.nn.sigmoid(x)

def _layernorm(x, axis=-1, eps=1e-05):
    m = jnp.mean(x, axis=axis, keepdims=True)
    v = jnp.var(x, axis=axis, keepdims=True)
    return (x - m) / jnp.sqrt(v + eps)

def _scatter_add(tgt, idx, src, axis=0):
    return tgt.at[idx].add(src)

def _segment_sum(src, seg, n):
    return jax.ops.segment_sum(src, seg, n)
kernel_name = 'mk_perceiver_d1_seqx_r2_a02c39'

def setup_inputs(seed: int=0):
    np.random.seed(seed)
    _w = jnp.asarray

    def _rec_inputs():
        import jax
        import jax.numpy as jnp
        _rk = jax.random.key(seed)
        x = -0.0003929 + 0.9999 * jax.random.normal(jax.random.fold_in(_rk, 1), (32, 32, 512), jnp.float32)
        _lenS = 32 - jax.random.randint(jax.random.fold_in(_rk, 7), (32,), 0, max(1, 32 // 4) + 1, jnp.int32)
        _lenS2 = 257 - jax.random.randint(jax.random.fold_in(_rk, 8), (32,), 0, max(1, 257 // 4) + 1, jnp.int32)
        _ctx_1024P = jax.random.normal(jax.random.fold_in(_rk, 11), (32, 16, 512), jnp.float32)
        _ctx_1024c = jax.random.dirichlet(jax.random.fold_in(_rk, 511), 0.3 * jnp.ones((16,), jnp.float32), (32, 257))
        _ctx_1024t = jnp.einsum('bsk,bkd->bsd', _ctx_1024c, _ctx_1024P)
        _ctx_1024t = _ctx_1024t * jax.lax.rsqrt(jnp.mean(jnp.square(_ctx_1024t)) + 1e-12) * 0.953939
        ctx_1024 = -1.39393e-06 + 0.999914 * (_ctx_1024t + 0.3 * jax.random.normal(jax.random.fold_in(_rk, 611), (32, 257, 512), jnp.float32))
        _validS = jnp.arange(32)[None, :] < _lenS[:, None]
        _validS2 = jnp.arange(257)[None, :] < _lenS2[:, None]
        _causal = jnp.tril(jnp.ones((32, 32), dtype=bool))
        mask_BxS2_bf1 = jnp.ones((32, 257), dtype=bool)
        return (x, ctx_1024, mask_BxS2_bf1)
    x, ctx_1024, mask_BxS2_bf1 = _rec_inputs()

    def _L0_xattn_setup():
        import jax, jax.numpy as jnp
        import numpy as np
        GAMMA = 10.0
        BASE = 10000.0
        SCALE = 64 ** (-0.5)
        NUM_HEADS = 16

        def _larope(t, seq_len):
            B, H, L, D = t.shape
            inv_freq = 1.0 / BASE ** (jnp.arange(0, D, 2, dtype=jnp.float32) / D)
            pos = GAMMA * (jnp.arange(L, dtype=jnp.float32) / float(seq_len))
            ang = pos[:, None] * inv_freq
            cos = jnp.cos(ang)
            sin = jnp.sin(ang)
            te, to = (t[..., 0::2], t[..., 1::2])
            re = te * cos - to * sin
            ro = te * sin + to * cos
            return jnp.stack([re, ro], axis=-1).reshape(t.shape)
        key = jax.random.key(seed)
        ks = jax.random.split(key, 8)
        B, Lq, Lk, D = (8, 1024, 256, 512)
        s = D ** (-0.5)
        return {'x': jax.random.normal(ks[0], (B, Lq, D), jnp.float32), 'context': jax.random.normal(ks[1], (B, Lk, D), jnp.float32), 'context_mask': jnp.ones((B, Lk), dtype=bool), 'Wq': jax.random.normal(ks[2], (D, D), jnp.float32) * s, 'bq': jnp.zeros((D,), jnp.float32), 'Wkv': jax.random.normal(ks[3], (D, 2 * D), jnp.float32) * s, 'bkv': jnp.zeros((2 * D,), jnp.float32), 'Wo': jax.random.normal(ks[4], (D, D), jnp.float32) * s, 'bo': jnp.zeros((D,), jnp.float32)}
    _L0_xattn_all = _L0_xattn_setup()
    _L0_xattn_in = {k: v for k, v in _L0_xattn_all.items() if k in ('Wq', 'bq', 'Wkv', 'bkv', 'Wo', 'bo')}
    del _L0_xattn_all

    def _L0_attn_setup():
        import jax, jax.numpy as jnp
        import numpy as np
        B, S, D, H = (2, 1024, 512, 16)
        HD = D // H
        key = jax.random.key(seed)
        k1, k2, k3 = jax.random.split(key, 3)
        x = jax.random.normal(k1, (B, S, D), dtype=jnp.float32)
        c_attn_kernel = 0.02 * jax.random.normal(k2, (3 * D, D), dtype=jnp.float32)
        c_attn_bias = jnp.zeros((3 * D,), dtype=jnp.float32)
        c_proj_kernel = 0.02 * jax.random.normal(k3, (D, D), dtype=jnp.float32)
        c_proj_bias = jnp.zeros((D,), dtype=jnp.float32)
        return {'hidden_states': x, 'c_attn_kernel': c_attn_kernel, 'c_attn_bias': c_attn_bias, 'c_proj_kernel': c_proj_kernel, 'c_proj_bias': c_proj_bias}
    _L0_attn_all = _L0_attn_setup()
    _L0_attn_in = {k: v for k, v in _L0_attn_all.items() if k in ('c_attn_kernel', 'c_attn_bias', 'c_proj_kernel', 'c_proj_bias')}
    del _L0_attn_all

    def _L0_ffn_setup():
        import jax, jax.numpy as jnp
        import numpy as np
        B, S, D, O, E, K = (4, 1024, 512, 512, 8, 2)
        key = jax.random.key(seed)
        ks = jax.random.split(key, 5)
        scale_in = 1.0 / np.sqrt(D)
        x = jax.random.normal(ks[0], (B, S, D), dtype=jnp.float32)
        gate_w = jax.random.uniform(ks[1], (E, D), jnp.float32, -scale_in, scale_in)
        gate_b = jax.random.uniform(ks[2], (E,), jnp.float32, -scale_in, scale_in)
        expert_w = jax.random.uniform(ks[3], (E, D, O), jnp.float32, -scale_in, scale_in)
        expert_b = jax.random.uniform(ks[4], (E, O), jnp.float32, -scale_in, scale_in)
        return {'x': x, 'gate_w': gate_w, 'gate_b': gate_b, 'expert_w': expert_w, 'expert_b': expert_b}
    _L0_ffn_all = _L0_ffn_setup()
    _L0_ffn_in = {k: v for k, v in _L0_ffn_all.items() if k in ('gate_w', 'gate_b', 'expert_w', 'expert_b')}
    del _L0_ffn_all
    return {'x': x, 'ctx_1024': ctx_1024, 'mask_BxS2_bf1': mask_BxS2_bf1, 'L0_xattn_Wq': _L0_xattn_in['Wq'], 'L0_xattn_bq': _L0_xattn_in['bq'], 'L0_xattn_Wkv': _L0_xattn_in['Wkv'], 'L0_xattn_bkv': _L0_xattn_in['bkv'], 'L0_xattn_Wo': _L0_xattn_in['Wo'], 'L0_xattn_bo': _L0_xattn_in['bo'], 'L0_attn_c_attn_kernel': _L0_attn_in['c_attn_kernel'], 'L0_attn_c_attn_bias': _L0_attn_in['c_attn_bias'], 'L0_attn_c_proj_kernel': _L0_attn_in['c_proj_kernel'], 'L0_attn_c_proj_bias': _L0_attn_in['c_proj_bias'], 'L0_ffn_gate_w': _L0_ffn_in['gate_w'], 'L0_ffn_gate_b': _L0_ffn_in['gate_b'], 'L0_ffn_expert_w': _L0_ffn_in['expert_w'], 'L0_ffn_expert_b': _L0_ffn_in['expert_b']}

def reference(x, ctx_1024, mask_BxS2_bf1, L0_xattn_Wq, L0_xattn_bq, L0_xattn_Wkv, L0_xattn_bkv, L0_xattn_Wo, L0_xattn_bo, L0_attn_c_attn_kernel, L0_attn_c_attn_bias, L0_attn_c_proj_kernel, L0_attn_c_proj_bias, L0_ffn_gate_w, L0_ffn_gate_b, L0_ffn_expert_w, L0_ffn_expert_b):
    import jax
    import jax.numpy as jnp

    def _L0_xattn_ref(x, context, context_mask, Wq, bq, Wkv, bkv, Wo, bo):
        import jax, jax.numpy as jnp
        import numpy as np
        GAMMA = 10.0
        BASE = 10000.0
        SCALE = 64 ** (-0.5)
        NUM_HEADS = 16

        def _larope(t, seq_len):
            B, H, L, D = t.shape
            inv_freq = 1.0 / BASE ** (jnp.arange(0, D, 2, dtype=jnp.float32) / D)
            pos = GAMMA * (jnp.arange(L, dtype=jnp.float32) / float(seq_len))
            ang = pos[:, None] * inv_freq
            cos = jnp.cos(ang)
            sin = jnp.sin(ang)
            te, to = (t[..., 0::2], t[..., 1::2])
            re = te * cos - to * sin
            ro = te * sin + to * cos
            return jnp.stack([re, ro], axis=-1).reshape(t.shape)
        B, Lq, D = x.shape
        Lk = context.shape[1]
        H = NUM_HEADS
        hd = D // H
        q = x @ Wq + bq
        kv = context @ Wkv + bkv
        k, v = jnp.split(kv, 2, axis=-1)
        q = q.reshape(B, Lq, H, hd).transpose(0, 2, 1, 3)
        k = k.reshape(B, Lk, H, hd).transpose(0, 2, 1, 3)
        v = v.reshape(B, Lk, H, hd).transpose(0, 2, 1, 3)
        q = _larope(q, Lq)
        k = _larope(k, Lk)
        scores = jnp.einsum('bhqd,bhkd->bhqk', q, k) * SCALE
        scores = jnp.where(context_mask[:, None, None, :], scores, -jnp.inf)
        attn = jax.nn.softmax(scores, axis=-1)
        out = jnp.einsum('bhqk,bhkd->bhqd', attn, v)
        out = out.transpose(0, 2, 1, 3).reshape(B, Lq, H * hd)
        return out @ Wo + bo

    def _L0_attn_ref(hidden_states, c_attn_kernel, c_attn_bias, c_proj_kernel, c_proj_bias):
        import jax, jax.numpy as jnp
        import numpy as np
        B, S, D, H = (2, 1024, 512, 16)
        HD = D // H
        b, s, d = hidden_states.shape
        qkv = hidden_states @ c_attn_kernel.T + c_attn_bias
        q, k, v = jnp.split(qkv, 3, axis=2)
        q = q.reshape(b, s, H, HD)
        k = k.reshape(b, s, H, HD)
        v = v.reshape(b, s, H, HD)
        causal = jnp.tril(jnp.ones((s, s), dtype=bool))
        neg = jnp.finfo(jnp.float32).min
        bias = jnp.where(causal, 0.0, neg).astype(jnp.float32)
        scale = 1.0 / jnp.sqrt(jnp.float32(HD))
        scores = jnp.einsum('bqhd,bkhd->bhqk', q * scale, k) + bias
        attn_weights = jax.nn.softmax(scores, axis=-1)
        attn_output = jnp.einsum('bhqk,bkhd->bqhd', attn_weights, v)
        attn_output = attn_output.reshape(b, s, d)
        out = attn_output @ c_proj_kernel.T + c_proj_bias
        return out

    def _L0_ffn_ref(x, gate_w, gate_b, expert_w, expert_b):
        import jax, jax.numpy as jnp
        import numpy as np
        B, S, D, O, E, K = (4, 1024, 512, 512, 8, 2)
        logits = jnp.einsum('bsd,ed->bse', x, gate_w) + gate_b
        if K < E:
            topv, topi = jax.lax.top_k(logits, K)
            keep = jax.nn.one_hot(topi, E, dtype=jnp.float32).sum(axis=-2)
            logits = jnp.where(keep > 0, logits, -jnp.inf)
        gate_score = jax.nn.softmax(logits, axis=-1)
        expert_out = jnp.einsum('bsd,edo->bseo', x, expert_w) + expert_b
        out = jnp.einsum('bseo,bse->bso', expert_out, gate_score)
        return out
    x = x + _L0_xattn_ref(_layernorm(x, axis=-1), ctx_1024, mask_BxS2_bf1, L0_xattn_Wq, L0_xattn_bq, L0_xattn_Wkv, L0_xattn_bkv, L0_xattn_Wo, L0_xattn_bo)
    x = x + _L0_attn_ref(_layernorm(x, axis=-1), L0_attn_c_attn_kernel, L0_attn_c_attn_bias, L0_attn_c_proj_kernel, L0_attn_c_proj_bias)
    x = x + _L0_ffn_ref(_layernorm(x, axis=-1), L0_ffn_gate_w, L0_ffn_gate_b, L0_ffn_expert_w, L0_ffn_expert_b)
    return x

_drawn_inputs = setup_inputs


def setup_inputs(seed=0):
    import zlib

    import numpy as np

    out = dict(_drawn_inputs(seed))
    spreads = {'L0_xattn_bq': (0.0, 0.1),
     'L0_xattn_bkv': (0.0, 0.1),
     'L0_xattn_bo': (0.0, 0.1),
     'L0_attn_c_attn_bias': (0.0, 0.1),
     'L0_attn_c_proj_bias': (0.0, 0.1)}
    factors = {'L0_ffn_expert_b': 3.738}
    for name, (base, spread) in spreads.items():
        noise = np.random.default_rng([zlib.crc32(name.encode()), seed]).standard_normal(out[name].shape)
        drawn = base * np.exp(spread * noise) if base else spread * noise
        out[name] = jnp.asarray(drawn.astype(out[name].dtype))
    for name, factor in factors.items():
        out[name] = (out[name] * factor).astype(out[name].dtype)
    return out
```

```python
from contextlib import ExitStack

import numpy as np
import concourse.bass as bass
from concourse import mybir

F32 = mybir.dt.float32
F32R = mybir.dt.float32r
U8 = mybir.dt.uint8
U32 = mybir.dt.uint32
ALU = mybir.AluOpType
ACT = mybir.ActivationFunctionType
AX = mybir.AxisListType

P = 128
B, S, D, LK = 32, 32, 512, 257
H, HD = 16, 32
KC = D // P
G = H // 4
TILES = B * S // P
BT = P // S
NE = 8
LKP = LK + 1
EPS = 1e-5
X_SCALE = 64.0 ** -0.5
BLOW = 8.0
A_SCALE = float(np.float32(1.0) / np.sqrt(np.float32(HD)))
WQ, WK, WV, WO, AQ, AK, AV, AP_, E0 = range(9)
R_BQ, R_BV, R_BO, R_AQ, R_AK, R_AV, R_AP = range(7)

C_ID = 0
C_COSK = C_ID + P
C_SINK = C_COSK + LKP
C_COSQ = C_SINK + LKP
C_SINQ = C_COSQ + HD // 2
C_HMX = C_SINQ + HD // 2
C_HMS = C_HMX + 4
C_CAUSAL = C_HMS + 4
C_ALL = C_CAUSAL + S


def constants():
    inv = (1.0 / 10000.0 ** (np.arange(0, HD, 2, dtype=np.float32) / np.float32(HD))).astype(np.float32)

    def angles(n):
        pos = np.float32(10.0) * (np.arange(n, dtype=np.float32) / np.float32(n))
        return (pos[:, None] * inv).astype(np.float32).astype(np.float64)

    c = np.zeros((P, C_ALL), np.float32)
    row = np.arange(P)
    c[:, C_ID:C_ID + P] = np.eye(P)
    k = angles(LK)
    c[:, C_COSK:C_COSK + LK] = np.cos(k).T[row % 16]
    c[:, C_SINK:C_SINK + LK] = np.sin(k).T[row % 16]
    q = angles(S)
    c[:, C_COSQ:C_COSQ + 16] = np.cos(q).astype(np.float32)[row % S] * np.float32(X_SCALE / BLOW)
    c[:, C_SINQ:C_SINQ + 16] = np.sin(q).astype(np.float32)[row % S] * np.float32(X_SCALE / BLOW)
    c[:, C_HMX:C_HMX + 4] = (row % 64 // 16)[:, None] == np.arange(4)
    c[:, C_HMS:C_HMS + 4] = (row // 32)[:, None] == np.arange(4)
    c[:, C_CAUSAL:C_CAUSAL + S] = np.where(np.arange(S)[None, :] <= (row % S)[:, None], 0.0, np.finfo(np.float32).min)
    return c


def perceiver(nc, x_in, ctx_in, ctx_last_in, mask_in, w_in, bias_in, bias_k_in, gate_w_in, gate_b_in,
              expert_b_in, const_in, out):
    with ExitStack() as top:
        def sem(name):
            return top.enter_context(nc.semaphore(name))

        def sbuf(stack, name, shape, dt=F32):
            return stack.enter_context(nc.sbuf_tensor(name, shape, dt))

        vlast_d = nc.dram_tensor("vlast_scratch", [B, D], F32, kind="Internal").ap()

        const = sbuf(top, "const", [P, C_ALL])
        ident = const[:, C_ID:C_ID + P]
        x = sbuf(top, "x", [P, TILES, D])
        whi = [sbuf(top, f"whi{i}", [P, KC, D], F32R) for i in range(4)]
        wlo = [sbuf(top, f"wlo{i}", [P, KC, D], F32R) for i in range(4)]
        wraw = [sbuf(top, f"wraw{i}", [P, KC, D]) for i in range(2)]
        stats = sbuf(top, "stats", [P, 6])
        mv = sbuf(top, "mv", [P, 2])
        neghalf = sbuf(top, "neghalf", [P, 1])
        vareps = sbuf(top, "vareps", [P, 1])
        rstd = sbuf(top, "rstd", [P, 1])
        xn = sbuf(top, "xn", [P, D])
        tick = sbuf(top, "tick", [1, G + 1])

        bank = [top.enter_context(nc.psum_tensor(f"bank{i}", [P, 512], F32)) for i in range(4)]
        quad = top.enter_context(nc.psum_tensor("quad", [P, 4, 512], F32))

        s_const, s_x, s_bias, s_maskin, s_clast, s_biask = (sem(n) for n in (
            "const_in", "x_in", "bias_in", "mask_in", "ctx_last_in", "bias_k_in"))
        s_wraw = [sem(f"weight_raw_in{i}") for i in range(2)]
        s_whi, s_wlo = sem("weight_hi_done"), sem("weight_lo_done")
        s_stats, s_mv, s_var, s_rstd, s_xn = (sem(n) for n in (
            "ln_stats_done", "ln_mv_done", "ln_var_done", "ln_rstd_done", "ln_xn_done"))

        def mm3(pe, psum, ahi, alo, bhi, blo, chunks=KC):
            for c in range(chunks):
                pe.matmul(psum, ahi(c), bhi(c), start=(c == 0), stop=False)
                pe.matmul(psum, ahi(c), blo(c), start=False, stop=False)
                last = pe.matmul(psum, alo(c), bhi(c), start=False, stop=(c == chunks - 1))
            return last

        def ln_dve_stats(dve, n, xt):
            dve.bn_stats(stats[:], xt).then_inc(s_stats, 1)
            dve.wait_ge(s_stats, n + 1)
            dve.memset(tick[:, G:G + 1], 0.0)
            dve.bn_aggr(mv[:], stats[:]).then_inc(s_mv, 1)
            dve.wait_ge(s_mv, n + 1)
            dve.tensor_scalar(vareps[:], mv[:, 1:2], EPS, None, ALU.add).then_inc(s_var, 1)

        def ln_pool(pool, n):
            pool.wait_ge(s_var, n + 1)
            pool.tensor_tensor(rstd[:], vareps[:], neghalf[:], ALU.pow).then_inc(s_rstd, 1)

        with ExitStack() as ph:
            def sb(name, shape, dt=F32):
                return sbuf(ph, name, shape, dt)

            maskb8 = sb("maskb8", [P, B, LK], U8)
            bias = sb("bias_cross", [P, R_AQ, D])
            bias_k = sb("bias_k", [P, 4])
            craw = [sb(f"craw{i}", [P, KC, LKP]) for i in range(2)]
            chi = [sb(f"chi{i}", [P, KC, LKP], F32R) for i in range(2)]
            clo = [sb(f"clo{i}", [P, KC, LKP], F32R) for i in range(2)]
            kb = sb("kb", [P, 4, LKP])
            kcos = sb("kcos", [P, 4, LKP])
            ksin = sb("ksin", [P, 4, LKP])
            kr = [sb(f"kr{i}", [P, G, LKP]) for i in range(2)]
            v = [sb(f"v{i}", [P, 3, D]) for i in range(2)]
            mb = [sb(f"mb{i}", [P, LK]) for i in range(2)]
            xthi = sb("xthi", [P, KC, P], F32R)
            xtlo = sb("xtlo", [P, KC, P], F32R)
            qb = sb("qb", [P, D])
            qcos = sb("qcos", [P, D])
            qsin = sb("qsin", [P, D])
            qr = qb[:].rearrange("p (g n) -> p g n", g=G)
            qt = sb("qt", [P, G, P])
            qbd = [sb(f"qbd{i}", [P, G, P]) for i in range(2)]
            sm = [sb(f"sm{i}", [P, LK]) for i in range(2)]
            pr = sb("pr", [P, G, 3 * P])
            nmax = sb("nmax", [P, G])
            rsum = sb("rsum", [P, G])
            rinv = sb("rinv", [P, G])
            pt = [sb(f"pt{i}", [P, 3 * P]) for i in range(2)]
            othi = sb("othi", [P, G, P], F32R)
            otlo = sb("otlo", [P, G, P], F32R)

            proj = bank[0:3]
            score = [bank[3], quad[:, 0, :]]
            ptp = quad[:, 1, :]
            extra = quad[:, 2, :]
            av = quad[:, 3, :]

            s_zero = sem("zeroed")
            s_ctx = [sem(f"ctx_raw_in{i}") for i in range(2)]
            s_vx = [sem(f"v_extra_in{i}") for i in range(2)]
            (s_clhi, s_cllo, s_vl, s_vlsb, s_vlst, s_chi, s_clo, s_proj, s_kev, s_vev, s_kcos, s_ksin, s_kr, s_qbd,
             s_mb, s_sc, s_sm, s_exp, s_rinv, s_norm, s_ptp, s_pt, s_av, s_ohi, s_olo, s_wo, s_xwo, s_xb, s_xtp, s_xthi,
             s_xtlo, s_qmm, s_qb, s_qcos, s_qr, s_qtp, s_qt) = (sem(n) for n in (
                 "ctx_last_hi_done", "ctx_last_lo_done", "v_last_done", "v_last_in_sbuf", "v_last_stored",
                 "ctx_hi_done", "ctx_lo_done", "proj_done", "k_evacuated", "v_evacuated", "k_cos_done", "k_sin_done",
                 "k_rotated", "q_blocks_done", "mask_bias_done", "scores_done", "scores_masked", "exp_done",
                 "rsum_inverted", "probs_normed", "probs_t_done", "probs_t_in_sbuf", "attn_done", "attn_hi_done",
                 "attn_lo_done", "out_proj_done", "x_with_out_proj", "x_with_bias", "xn_t_done", "xn_t_hi_done",
                 "xn_t_lo_done", "q_done", "q_in_sbuf", "q_trig_done", "q_rotated", "q_t_done", "q_t_in_sbuf"))

            cosk = const[:, C_COSK:C_COSK + LKP].unsqueeze(1).to_broadcast([P, 4, LKP])
            sink = const[:, C_SINK:C_SINK + LKP].unsqueeze(1).to_broadcast([P, 4, LKP])
            cosq = const[:, C_COSQ:C_COSQ + 16].unsqueeze(1).to_broadcast([P, 2 * H, 16])
            sinq = const[:, C_SINQ:C_SINQ + 16].unsqueeze(1).to_broadcast([P, 2 * H, 16])
            hmx = const[:, C_HMX:C_HMX + 4].unsqueeze(1).unsqueeze(3).to_broadcast([P, G, 4, S])

            block = ph.enter_context(nc.Block())

            @block.sync
            def _(sp):
                def weight(n):
                    if n >= 2:
                        sp.wait_ge(s_wlo, n - 1)
                    sp.dma_start(wraw[n % 2][:], w_in[n]).then_inc(s_wraw[n % 2], 16)

                def ctx(b, j):
                    sp.dma_start(craw[j % 2][:], ctx_in[b]).then_inc(s_ctx[j % 2], 16)

                def v_extra(b, j):
                    sp.dma_start(v[j % 2][0:1, 2, :], vlast_d[bass.ds(b, 1), :]).then_inc(s_vx[j % 2], 16)

                sp.dma_start(const[:], const_in).then_inc(s_const, 16)
                for t in range(TILES):
                    sp.dma_start(x[:, t, :], x_in[t * P:(t + 1) * P, :]).then_inc(s_x, 16)
                weight(WQ)
                weight(WK)
                sp.dma_start(bias[:], bias_in[0:R_AQ, :].partition_broadcast(P)).then_inc(s_bias, 16)
                sp.dma_start(bias_k[:], bias_k_in).then_inc(s_biask, 16)
                sp.dma_start(craw[1][:, :, 0:P], ctx_last_in).then_inc(s_clast, 16)
                ctx(0, 0)
                sp.dma_start(maskb8[:], mask_in.partition_broadcast(P)).then_inc(s_maskin, 16)
                weight(WV)
                weight(WO)
                sp.wait_ge(s_cllo, 1)
                ctx(1, 1)
                sp.wait_ge(s_vlsb, 1)
                sp.dma_start(vlast_d, xn[0:B, :]).then_inc(s_vlst, 16)
                sp.wait_ge(s_vlst, 16)
                sp.wait_ge(s_zero, 3)
                v_extra(0, 0)

                def step(t, j, last):
                    b = t * BT + j
                    if not (last and j == BT - 1):
                        if not (isinstance(t, int) and b == 0):
                            sp.wait_ge(s_av, b * G)
                        v_extra(b + 1, j + 1)
                    if not (last and j >= BT - 2):
                        sp.wait_ge(s_clo, b + 1)
                        ctx(b + 2, j)

                def body(t, last=False):
                    for j in range(BT):
                        step(t, j, last)

                body(0)
                weight(AQ)
                weight(AK)
                with sp.Fori(1, TILES - 1) as t:
                    body(t)
                body(TILES - 1, last=True)

            @block.gpsimd
            def _(pool):
                pool.memset(neghalf[:], -0.5).then_inc(s_zero, 1)
                pool.memset(v[0][:, 2, :], 0.0).then_inc(s_zero, 1)
                pool.memset(v[1][:, 2, :], 0.0).then_inc(s_zero, 1)
                pool.memset(pr[:], 0.0).then_inc(s_zero, 1)
                pool.wait_ge(s_zero, 4)

                def k_sin(b):
                    pool.wait_ge(s_kev, (b + 1) * 4)
                    if not (isinstance(b, int) and b == 0):
                        pool.wait_ge(s_kr, b)
                    pool.tensor_tensor(ksin[:], kb[:], sink, ALU.mult).then_inc(s_ksin, 1)

                def q_blocks(b, t, j):
                    pool.wait_ge(s_qt, t + 1)
                    if not (isinstance(b, int) and b < 2):
                        pool.wait_ge(s_sc, (b - 1) * G)
                    q = qt[:, :, j * S:(j + 1) * S].unsqueeze(2).to_broadcast([P, G, 4, S])
                    pool.tensor_tensor(qbd[j % 2][:].rearrange("p g (h q) -> p g h q", h=4), q, hmx,
                                       ALU.mult).then_inc(s_qbd, 1)

                pool.wait_ge(s_const, 16)
                ln_pool(pool, 0)
                q_blocks(0, 0, 0)
                k_sin(0)

                def body(t, last=False):
                    for j in range(BT):
                        if not (last and j == BT - 1):
                            if j < BT - 1:
                                q_blocks(t * BT + j + 1, t, j + 1)
                            else:
                                q_blocks(t * BT + BT, t + 1, 0)
                            k_sin(t * BT + j + 1)
                        if j == 0 and not last:
                            ln_pool(pool, t + 1)

                body(0)
                with pool.Fori(1, TILES - 1) as t:
                    body(t)
                body(TILES - 1, last=True)

            @block.scalar
            def _(act):
                def w_hi(n):
                    act.wait_ge(s_wraw[n % 2], 16 * (n // 2 + 1))
                    act.activation(whi[n % 4][:], wraw[n % 2][:], ACT.Copy).then_inc(s_whi, 1)

                def ctx_hi_at(t, j2):
                    b = t * BT + j2
                    act.wait_ge(s_ctx[j2 % 2], (t * 2 + j2 // 2 + 1) * 16)
                    if not (isinstance(b, int) and b < 2):
                        act.wait_ge(s_proj, (b - 1) * 6)
                    act.activation(chi[j2 % 2][:], craw[j2 % 2][:], ACT.Copy).then_inc(s_chi, 1)

                def k_evac(b, m):
                    act.wait_ge(s_proj, b * 6 + m + 1)
                    if m == 0 and not (isinstance(b, int) and b == 0):
                        act.wait_ge(s_kcos, b)
                        act.wait_ge(s_ksin, b)
                    act.activation(kb[:, m, :], proj[m % 3][:, 0:LKP], ACT.Identity,
                                   bias=bias_k[:, m:m + 1]).then_inc(s_kev, 1)

                def exp(b, g):
                    n = b * G + g
                    act.wait_ge(s_sm, n + 1)
                    if not (isinstance(b, int) and b == 0):
                        act.wait_ge(s_ptp, n - G + 1)
                    act.activation(pr[:, g, 0:LK], sm[g % 2][:], ACT.Exp, bias=nmax[:, g:g + 1], scale=-1.0,
                                   accum_out=rsum[:, g:g + 1]).then_inc(s_exp, 1)

                def pt_evac(b, g):
                    n = b * G + g
                    act.wait_ge(s_ptp, n + 1)
                    if not (isinstance(b, int) and n < 2):
                        act.wait_ge(s_av, n - 1)
                    act.activation(pt[g % 2][:], ptp[:, 0:3 * P], ACT.Copy).then_inc(s_pt, 1)

                def o_hi(b, t, j):
                    act.wait_ge(s_av, b * G + G)
                    if j == 0 and not (isinstance(t, int) and t == 0):
                        act.wait_ge(s_wo, t)
                    for h in range(4):
                        rows = slice(h * 32, h * 32 + 32)
                        last = act.activation(
                            othi[rows, :, j * S:(j + 1) * S],
                            av[rows, :].rearrange("p (g h q) -> p g h q", g=G, h=4)[:, :, h, :], ACT.Copy)
                    last.then_inc(s_ohi, 1)

                def mask_bias(b, j):
                    if not (isinstance(b, int) and b < 2):
                        act.wait_ge(s_sm, (b - 1) * G)
                    act.activation(mb[j % 2][:], maskb8[:, b, :], ACT.Copy, bias=-3e38, scale=3e38).then_inc(s_mb, 1)

                def xt_hi(t):
                    act.wait_ge(s_xtp, t + 1)
                    if not (isinstance(t, int) and t == 0):
                        act.wait_ge(s_qmm, t)
                    act.activation(xthi[:], extra.rearrange("p (c n) -> p c n", c=KC), ACT.Copy).then_inc(s_xthi, 1)

                def qt_evac(t):
                    act.wait_ge(s_qtp, t + 1)
                    if not (isinstance(t, int) and t == 0):
                        act.wait_ge(s_qbd, t * BT)
                    act.activation(qt[:], extra.rearrange("p (g n) -> p g n", g=G), ACT.Copy).then_inc(s_qt, 1)

                act.wait_ge(s_const, 16)
                w_hi(WQ)
                w_hi(WK)
                xt_hi(0)
                act.wait_ge(s_clast, 16)
                act.activation(chi[1][:, :, 0:P], craw[1][:, :, 0:P], ACT.Copy).then_inc(s_clhi, 1)
                ctx_hi_at(0, 0)
                w_hi(WV)
                qt_evac(0)
                act.wait_ge(s_biask, 16)
                for m in range(4):
                    k_evac(0, m)
                w_hi(WO)
                act.wait_ge(s_maskin, 16)
                mask_bias(0, 0)
                act.wait_ge(s_vl, 1)
                ctx_hi_at(0, 1)
                act.wait_ge(s_zero, 4)

                def body(t, last=False):
                    for j in range(BT):
                        b = t * BT + j
                        more = not (last and j == BT - 1)
                        if more:
                            k_evac(b + 1, 0)
                        if j == 3 and not last:
                            qt_evac(t + 1)
                        if j == 1 and not last:
                            xt_hi(t + 1)
                        exp(b, 0)
                        if more:
                            k_evac(b + 1, 1)
                        exp(b, 1)
                        if more:
                            k_evac(b + 1, 2)
                        pt_evac(b, 0)
                        exp(b, 2)
                        if more:
                            k_evac(b + 1, 3)
                            mask_bias(b + 1, j + 1)
                        pt_evac(b, 1)
                        exp(b, 3)
                        if not (last and j >= BT - 2):
                            ctx_hi_at(t, j + 2)
                        pt_evac(b, 2)
                        pt_evac(b, 3)
                        o_hi(b, t, j)

                body(0)
                with act.Fori(1, TILES - 1) as t:
                    body(t)
                body(TILES - 1, last=True)

            @block.vector
            def _(dve):
                def w_lo(n):
                    dve.wait_ge(s_whi, n + 1)
                    dve.tensor_tensor(wlo[n % 4][:], wraw[n % 2][:], whi[n % 4][:].bitcast(F32),
                                      ALU.subtract).then_inc(s_wlo, 1)

                def ctx_lo(b, j):
                    dve.wait_ge(s_chi, b + 1)
                    dve.tensor_tensor(clo[j % 2][:], craw[j % 2][:], chi[j % 2][:].bitcast(F32),
                                      ALU.subtract).then_inc(s_clo, 1)

                def ln(t):
                    ln_dve_stats(dve, t, x[:, t, :])
                    dve.wait_ge(s_rstd, t + 1)
                    if not (isinstance(t, int) and t == 0):
                        dve.wait_ge(s_xtp, t)
                    dve.tensor_scalar(xn[:], x[:, t, :], mv[:, 0:1], rstd[:, 0:1], ALU.subtract,
                                      ALU.mult).then_inc(s_xn, 1)

                def xt_lo(t):
                    dve.wait_ge(s_xthi, t + 1)
                    dve.tensor_tensor(xtlo[:], extra.rearrange("p (c n) -> p c n", c=KC), xthi[:].bitcast(F32),
                                      ALU.subtract).then_inc(s_xtlo, 1)

                def q_rope(t):
                    dve.wait_ge(s_qmm, t + 1)
                    if not (isinstance(t, int) and t == 0):
                        dve.wait_ge(s_qtp, t)
                    dve.tensor_tensor(qb[:], extra, bias[:, R_BQ, :], ALU.add).then_inc(s_qb, 1)
                    dve.wait_ge(s_qb, t + 1)
                    qv = qb[:].rearrange("p (a i) -> p a i", i=16)
                    dve.tensor_tensor(qcos[:].rearrange("p (a i) -> p a i", i=16), qv, cosq, ALU.mult)
                    dve.tensor_tensor(qsin[:].rearrange("p (a i) -> p a i", i=16), qv, sinq,
                                      ALU.mult).then_inc(s_qcos, 1)
                    dve.wait_ge(s_qcos, t + 1)
                    ev, od = slice(0, D // 2), slice(D // 2, D)
                    dve.tensor_tensor(qr[:, :, 0:64], qcos[:, ev].rearrange("p (g n) -> p g n", g=G),
                                      qsin[:, od].rearrange("p (g n) -> p g n", g=G), ALU.subtract)
                    dve.tensor_tensor(qr[:, :, 64:128], qsin[:, ev].rearrange("p (g n) -> p g n", g=G),
                                      qcos[:, od].rearrange("p (g n) -> p g n", g=G), ALU.add).then_inc(s_qr, 1)

                def k_cos(b):
                    dve.wait_ge(s_kev, (b + 1) * 4)
                    dve.tensor_tensor(kcos[:], kb[:], cosk, ALU.mult).then_inc(s_kcos, 1)

                def k_rotate(b, j):
                    dve.wait_ge(s_kcos, b + 1)
                    dve.wait_ge(s_ksin, b + 1)
                    if not (isinstance(b, int) and b < 2):
                        dve.wait_ge(s_sc, (b - 1) * G)
                    pairs = kr[j % 2][:].rearrange("p (a two) n -> p a two n", two=2)
                    for half in range(2):
                        rows = slice(half * 64, half * 64 + 64)
                        dve.tensor_tensor(pairs[0:64, :, half, :], kcos[rows, 0:2, :], ksin[rows, 2:4, :], ALU.subtract)
                        last = dve.tensor_tensor(pairs[64:128, :, half, :], ksin[rows, 0:2, :], kcos[rows, 2:4, :], ALU.add)
                    last.then_inc(s_kr, 1)

                def v_evac(b, j, c):
                    dve.wait_ge(s_proj, b * 6 + 4 + c + 1)
                    if c == 0 and not (isinstance(b, int) and b < 2):
                        dve.wait_ge(s_av, (b - 1) * G)
                    dve.tensor_tensor(v[j % 2][:, c, :], proj[(4 + c) % 3][:], bias[:, R_BV, :],
                                      ALU.add).then_inc(s_vev, 1)

                def masked(b, j, g):
                    n = b * G + g
                    dve.wait_ge(s_sc, n + 1)
                    if g == 0:
                        dve.wait_ge(s_mb, b + 1)
                    if not (isinstance(b, int) and n < 2):
                        dve.wait_ge(s_exp, n - 1)
                    dve.memset(tick[:, g:g + 1], 0.0)
                    dve.tensor_tensor_reduce(sm[g % 2][:], score[g % 2][:, 0:LK], mb[j % 2][:], -BLOW, 3.4e38,
                                             ALU.add, ALU.min, nmax[:, g:g + 1]).then_inc(s_sm, 1)

                def norm(b, g):
                    n = b * G + g
                    dve.wait_ge(s_exp, n + 1)
                    dve.reciprocal(rinv[:, g:g + 1], rsum[:, g:g + 1]).then_inc(s_rinv, 1)
                    dve.wait_ge(s_rinv, n + 1)
                    dve.tensor_scalar(pr[:, g, 0:LK], pr[:, g, 0:LK], rinv[:, g:g + 1], None,
                                      ALU.mult).then_inc(s_norm, 1)

                def o_lo(b, j):
                    dve.wait_ge(s_ohi, b + 1)
                    for h in range(4):
                        rows = slice(h * 32, h * 32 + 32)
                        last = dve.tensor_tensor(
                            otlo[rows, :, j * S:(j + 1) * S],
                            av[rows, :].rearrange("p (g h q) -> p g h q", g=G, h=4)[:, :, h, :],
                            othi[rows, :, j * S:(j + 1) * S].bitcast(F32), ALU.subtract)
                    last.then_inc(s_olo, 1)

                def add_out(t):
                    dve.wait_ge(s_wo, t + 1)
                    dve.tensor_tensor(x[:, t, :], extra, x[:, t, :], ALU.add).then_inc(s_xwo, 1)
                    dve.wait_ge(s_xwo, t + 1)
                    dve.tensor_tensor(x[:, t, :], x[:, t, :], bias[:, R_BO, :], ALU.add).then_inc(s_xb, 1)

                dve.wait_ge(s_x, 16 * TILES)
                dve.wait_ge(s_zero, 1)
                ln(0)
                w_lo(WQ)
                w_lo(WK)
                xt_lo(0)
                dve.wait_ge(s_clhi, 1)
                dve.tensor_tensor(clo[1][:, :, 0:P], craw[1][:, :, 0:P], chi[1][:, :, 0:P].bitcast(F32),
                                  ALU.subtract).then_inc(s_cllo, 1)
                ctx_lo(0, 0)
                dve.wait_ge(s_bias, 16)
                q_rope(0)
                w_lo(WV)
                k_cos(0)
                k_rotate(0, 0)
                dve.wait_ge(s_vl, 1)
                dve.wait_ge(s_xtp, 1)
                dve.tensor_tensor(xn[0:B, :], extra[0:B, :], bias[0:B, R_BV, :], ALU.add).then_inc(s_vlsb, 1)
                dve.wait_ge(s_vlst, 16)
                v_evac(0, 0, 0)
                v_evac(0, 0, 1)
                w_lo(WO)
                ctx_lo(1, 1)

                def body(t, first=False, last=False):
                    for j in range(BT):
                        b = t * BT + j
                        more = not (last and j == BT - 1)
                        if j == 1 and not last:
                            xt_lo(t + 1)
                        masked(b, j, 0)
                        masked(b, j, 1)
                        if j == 0 and not first:
                            add_out(t - 1)
                        norm(b, 0)
                        masked(b, j, 2)
                        norm(b, 1)
                        masked(b, j, 3)
                        if more:
                            k_cos(b + 1)
                        norm(b, 2)
                        norm(b, 3)
                        if more:
                            k_rotate(b + 1, j + 1)
                            v_evac(b + 1, j + 1, 0)
                        if not (last and j >= BT - 2):
                            ctx_lo(b + 2, j)
                        if j == 0 and not last:
                            ln(t + 1)
                        if j == 2 and not last:
                            q_rope(t + 1)
                        if more:
                            v_evac(b + 1, j + 1, 1)
                        o_lo(b, j)

                body(0, first=True)
                with dve.Fori(1, TILES - 1) as t:
                    body(t)
                body(TILES - 1, last=True)
                add_out(TILES - 1)

            @block.tensor
            def _(pe):
                def xn_transposed(t):
                    pe.wait_ge(s_xn, t + 1)
                    if not (isinstance(t, int) and t == 0):
                        pe.wait_ge(s_qt, t)
                    if not (isinstance(t, int) and t <= 1):
                        pe.wait_ge(s_xwo, t - 1)
                    for c in range(KC):
                        last = pe.transpose(extra[:, c * P:(c + 1) * P], xn[:, c * P:(c + 1) * P], ident)
                    last.then_inc(s_xtp, 1)

                def q_product(t):
                    pe.wait_ge(s_xtlo, t + 1)
                    mm3(pe, extra, lambda c: xthi[:, c, :], lambda c: xtlo[:, c, :],
                        lambda c: whi[WQ][:, c, :], lambda c: wlo[WQ][:, c, :]).then_inc(s_qmm, 1)

                def q_transposed(t):
                    pe.wait_ge(s_qr, t + 1)
                    for g in range(G):
                        last = pe.transpose(extra[:, g * P:(g + 1) * P], qr[:, g, :], ident)
                    last.then_inc(s_qtp, 1)

                def k_product(b, j, m):
                    if m == 0:
                        pe.wait_ge(s_clo, b + 1)
                    if not (isinstance(b, int) and b == 0 and m < 3):
                        if m == 0:
                            pe.wait_ge(s_kev, b * 4)
                        elif m < 3:
                            pe.wait_ge(s_vev, b * 2 - 2 + m)
                        else:
                            pe.wait_ge(s_kev, b * 4 + 1)
                    mm3(pe, proj[m % 3][:, 0:LKP],
                        lambda c: whi[WK][:, c, m * P:(m + 1) * P], lambda c: wlo[WK][:, c, m * P:(m + 1) * P],
                        lambda c: chi[j % 2][:, c, :], lambda c: clo[j % 2][:, c, :]).then_inc(s_proj, 1)

                def v_product(b, j, u, part):
                    psum = proj[(4 + u) % 3][:]
                    if part == 0:
                        pe.wait_ge(s_kev, b * 4 + 2 + u)
                    for c in (0, 1) if part == 0 else (2, 3):
                        hi, lo = (a[j % 2][:, c, u * P:(u + 1) * P] for a in (chi, clo))
                        pe.matmul(psum, hi, whi[WV][:, c, :], start=(c == 0), stop=False)
                        pe.matmul(psum, hi, wlo[WV][:, c, :], start=False, stop=False)
                        last = pe.matmul(psum, lo, whi[WV][:, c, :], start=False, stop=(c == KC - 1))
                    if part == 1:
                        last.then_inc(s_proj, 1)

                def scores(b, j, g):
                    n = b * G + g
                    if g == 0:
                        pe.wait_ge(s_kr, b + 1)
                        pe.wait_ge(s_qbd, b + 1)
                    if not (isinstance(b, int) and n < 2):
                        pe.wait_ge(s_sm, n - 1)
                    pe.matmul(score[g % 2][:, 0:LK], qbd[j % 2][:, g, :], kr[j % 2][:, g, 0:LK],
                              start=True, stop=True).then_inc(s_sc, 1)

                def probs_transposed(b, g):
                    n = b * G + g
                    pe.wait_ge(s_norm, n + 1)
                    if not (isinstance(b, int) and n == 0):
                        pe.wait_ge(s_pt, n)
                    for c in range(3):
                        last = pe.transpose(ptp[:, c * P:(c + 1) * P], pr[:, g, c * P:(c + 1) * P], ident)
                    last.then_inc(s_ptp, 1)

                def attend(b, t, j, g):
                    n = b * G + g
                    pe.wait_ge(s_pt, n + 1)
                    if g == 0:
                        pe.wait_ge(s_vev, b * 2 + 2)
                        pe.wait_ge(s_vx[j % 2], (t * 2 + j // 2 + 1) * 16)
                        if not (isinstance(b, int) and b == 0):
                            pe.wait_ge(s_olo, b)
                    for c in range(3):
                        last = pe.matmul(av[:, g * P:(g + 1) * P], v[j % 2][:, c, g * P:(g + 1) * P],
                                         pt[g % 2][:, c * P:(c + 1) * P], start=(c == 0), stop=(c == 2))
                    last.then_inc(s_av, 1)

                def out_product(t):
                    pe.wait_ge(s_olo, t * BT + BT)
                    pe.wait_ge(s_qt, t + 2 if not (isinstance(t, int) and t == TILES - 1) else TILES)
                    mm3(pe, extra, lambda c: othi[:, c, :], lambda c: otlo[:, c, :],
                        lambda c: whi[WO][:, c, :], lambda c: wlo[WO][:, c, :]).then_inc(s_wo, 1)

                pe.wait_ge(s_const, 16)
                xn_transposed(0)
                pe.wait_ge(s_wlo, WQ + 1)
                q_product(0)
                pe.wait_ge(s_wlo, WK + 1)
                for m in range(3):
                    k_product(0, 0, m)
                q_transposed(0)
                k_product(0, 0, 3)
                pe.wait_ge(s_wlo, WV + 1)
                pe.wait_ge(s_cllo, 1)
                pe.wait_ge(s_qt, 1)
                mm3(pe, extra, lambda c: chi[1][:, c, 0:P], lambda c: clo[1][:, c, 0:P],
                    lambda c: whi[WV][:, c, :], lambda c: wlo[WV][:, c, :]).then_inc(s_vl, 1)
                for u in range(2):
                    v_product(0, 0, u, 0)
                    v_product(0, 0, u, 1)
                pe.wait_ge(s_wlo, WO + 1)
                pe.wait_ge(s_vlsb, 1)

                def body(t, first=False, last=False):
                    for j in range(BT):
                        b = t * BT + j
                        more = not (last and j == BT - 1)
                        if more:
                            k_product(b + 1, j + 1, 0)
                        scores(b, j, 0)
                        if j == 0 and not first:
                            out_product(t - 1)
                        if j == 1 and not last:
                            xn_transposed(t + 1)
                        if j == 3 and not last:
                            q_transposed(t + 1)
                        if more:
                            k_product(b + 1, j + 1, 1)
                        scores(b, j, 1)
                        if more:
                            k_product(b + 1, j + 1, 2)
                        probs_transposed(b, 0)
                        scores(b, j, 2)
                        if more:
                            k_product(b + 1, j + 1, 3)
                        probs_transposed(b, 1)
                        scores(b, j, 3)
                        if more:
                            v_product(b + 1, j + 1, 0, 0)
                        attend(b, t, j, 0)
                        probs_transposed(b, 2)
                        if more:
                            v_product(b + 1, j + 1, 0, 1)
                        attend(b, t, j, 1)
                        probs_transposed(b, 3)
                        if more:
                            v_product(b + 1, j + 1, 1, 0)
                        attend(b, t, j, 2)
                        if more:
                            v_product(b + 1, j + 1, 1, 1)
                        if j == 1 and not last:
                            q_product(t + 1)
                        attend(b, t, j, 3)

                body(0, first=True)
                with pe.Fori(1, TILES - 1) as t:
                    body(t)
                body(TILES - 1, last=True)
                out_product(TILES - 1)

        with ExitStack() as ph:
            def sb(name, shape, dt=F32):
                return sbuf(ph, name, shape, dt)

            bias = sb("bias_self", [P, 7 - R_AQ, D])
            xthi = sb("xthi2", [P, KC, P], F32R)
            xtlo = sb("xtlo2", [P, KC, P], F32R)
            qsb = sb("qsb", [P, D])
            ksb = sb("ksb", [P, D])
            vsb = sb("vsb", [P, D])
            qbd = sb("qbd2", [P, G, BT, P])
            kt = sb("kt", [P, G, P])
            sm = sb("sm2", [P, G * BT, S])
            pr = sb("pr2", [P, G * BT, S])
            smax = sb("smax2", [P, G * BT])
            ssum = sb("ssum2", [P, G * BT])
            sinv = sb("sinv2", [P, G * BT])
            pt = sb("pt2", [P, G, P])
            othi = sb("othi2", [P, G, P], F32R)
            otlo = sb("otlo2", [P, G, P], F32R)
            x3hi = sb("x3hi", [P, KC, B * S], F32R)
            x3lo = sb("x3lo", [P, KC, B * S], F32R)
            gate_w = sb("gate_w", [P, KC, NE])
            gwhi = sb("gwhi", [P, KC, NE], F32R)
            gwlo = sb("gwlo", [P, KC, NE], F32R)
            gate_b = sb("gate_b", [P, NE])
            expert_b = sb("expert_b", [NE, D])
            iota = sb("iota", [P, NE])
            logits = sb("logits", [P, TILES, NE])
            top8 = sb("top8", [P, TILES, 8])
            idx8 = sb("idx8", [P, TILES, 8], U32)
            idxf = sb("idxf", [P, TILES, 2])
            gap = sb("gap", [P, TILES])
            gexp = sb("gexp", [P, TILES])
            gden = sb("gden", [P, TILES])
            gtop = sb("gtop", [P, 2, TILES])
            pick = sb("pick", [P, 2, TILES, NE])
            gates = sb("gates", [P, TILES, NE])
            gt = sb("gt", [NE, TILES, P])

            (s_bias2, s_gw, s_gb, s_eb, s_xtp, s_xthi, s_xtlo, s_qkvp, s_qkv, s_qtp, s_ktp, s_qbd, s_kt, s_sc, s_m, s_exp,
             s_nm, s_norm, s_ptp, s_pt, s_av, s_ohi, s_olo, s_cp, s_xo1, s_xo) = (sem(n) for n in (
                 "bias_self_in", "gate_w_in", "gate_b_in", "expert_b_in", "self_xn_t_done", "self_xn_t_hi_done", "self_xn_t_lo_done",
                 "qkv_done", "qkv_in_sbuf", "self_q_t_done", "self_k_t_done", "self_q_blocks_done", "self_k_t_in_sbuf",
                 "self_scores_done", "self_max_steps", "self_exp_done", "self_norm_steps", "self_probs_normed",
                 "self_probs_t_done", "self_probs_t_in_sbuf", "self_attn_done", "self_attn_hi_done",
                 "self_attn_lo_done", "self_out_proj_done", "self_x_with_out_proj", "self_x_with_bias"))
            (s_iota, s_gwhi, s_gwlo, s_ntp, s_x3hi, s_x3lo, s_lgp, s_lg, s_top, s_idx, s_gst, s_gexp, s_gates, s_gtp,
             s_gt, s_mm, s_acc, s_out) = (sem(n) for n in (
                 "iota_done", "gate_w_hi_done", "gate_w_lo_done", "ffn_xn_t_done", "ffn_xn_t_hi_done",
                 "ffn_xn_t_lo_done", "logits_done", "logits_in_sbuf", "top_found", "top_index_found",
                 "gate_steps", "gate_exp_done", "gates_done", "gates_t_done", "gates_t_in_sbuf", "expert_products",
                 "expert_outputs_added", "out_stored"))

            hms = const[:, C_HMS:C_HMS + 4].unsqueeze(1).unsqueeze(3).to_broadcast([P, BT, 4, S])
            causal = const[:, C_CAUSAL:C_CAUSAL + S].unsqueeze(1).to_broadcast([P, G * BT, S])

            def over_k(a):
                return a.unsqueeze(2).to_broadcast([P, G * BT, S])

            ring = [bank[i][:] for i in range(4)] + [quad[:, i, :] for i in range(4)]
            block = ph.enter_context(nc.Block())

            @block.sync
            def _(sp):
                sp.dma_start(bias[:], bias_in[R_AQ:7, :].partition_broadcast(P)).then_inc(s_bias2, 16)
                sp.dma_start(gate_w[:], gate_w_in).then_inc(s_gw, 16)
                sp.dma_start(gate_b[:], gate_b_in.unsqueeze(0).partition_broadcast(P)).then_inc(s_gb, 16)
                sp.dma_start(expert_b[:], expert_b_in).then_inc(s_eb, 16)

                def weight(n, slot, turn):
                    sp.wait_ge(s_wlo, n - 1)
                    sp.dma_start(wraw[slot][:], w_in[n]).then_inc(s_wraw[slot], 16)

                weight(AV, 0, 0)
                weight(AP_, 1, 0)
                with sp.Fori(0, NE // 2) as i:
                    for s in range(2):
                        weight(E0 + i * 2 + s, s, i)
                for t in range(TILES):
                    sp.wait_ge(s_acc, TILES * NE + t + 1)
                    sp.dma_start(out[t * P:(t + 1) * P, :], x[:, t, :]).then_inc(s_out, 16)
                sp.wait_ge(s_out, 16 * TILES)

            @block.gpsimd
            def _(pool):
                pool.iota(iota[:], [[1, NE]], base=0, channel_multiplier=0,
                          allow_small_or_imprecise_dtypes=True).then_inc(s_iota, 1)
                with pool.Fori(TILES, 3 * TILES) as n:
                    ln_pool(pool, n)

            @block.scalar
            def _(act):
                def w_hi(n, slot, raw, uses):
                    act.wait_ge(s_wraw[raw], uses)
                    act.activation(whi[slot][:], wraw[raw][:], ACT.Copy).then_inc(s_whi, 1)

                def xt_hi(t):
                    act.wait_ge(s_xtp, t + 1)
                    if not (isinstance(t, int) and t == 0):
                        act.wait_ge(s_qkvp, t * 3)
                    act.activation(xthi[:], bank[0][:].rearrange("p (c n) -> p c n", c=KC), ACT.Copy).then_inc(s_xthi, 1)

                def kt_evac(t):
                    act.wait_ge(s_ktp, t + 1)
                    if not (isinstance(t, int) and t == 0):
                        act.wait_ge(s_sc, t)
                    act.activation(kt[:], bank[1][:].rearrange("p (g n) -> p g n", g=G), ACT.Copy).then_inc(s_kt, 1)

                def exp(t):
                    act.wait_ge(s_m, t * 3 + 3)
                    if not (isinstance(t, int) and t == 0):
                        act.wait_ge(s_ptp, t)
                    act.activation(pr[:], sm[:], ACT.Exp, scale=A_SCALE).then_inc(s_exp, 1)

                def pt_evac(t):
                    act.wait_ge(s_ptp, t + 1)
                    if not (isinstance(t, int) and t == 0):
                        act.wait_ge(s_av, t)
                    act.activation(pt[:], quad[:, 1, :].rearrange("p (g n) -> p g n", g=G), ACT.Copy).then_inc(s_pt, 1)

                def o_hi(t):
                    act.wait_ge(s_av, t + 1)
                    if not (isinstance(t, int) and t == 0):
                        act.wait_ge(s_cp, t)
                    for h in range(4):
                        r = slice(h * 32, h * 32 + 32)
                        last = act.activation(
                            othi[r, :, :].rearrange("p g (b q) -> p b g q", b=BT),
                            quad[r, :, :].rearrange("p b (g h q) -> p b g h q", g=G, h=4)[:, :, :, h, :], ACT.Copy)
                    last.then_inc(s_ohi, 1)

                w_hi(AQ, 0, 0, 48)
                xt_hi(0)
                w_hi(AK, 1, 1, 48)
                w_hi(AV, 2, 0, 64)
                act.wait_ge(s_gw, 16)
                act.activation(gwhi[:], gate_w[:], ACT.Copy).then_inc(s_gwhi, 1)
                kt_evac(0)
                w_hi(AP_, 3, 1, 64)

                def body(t):
                    xt_hi(t)
                    exp(t - 1)
                    pt_evac(t - 1)
                    o_hi(t - 1)
                    kt_evac(t)

                with act.Fori(1, TILES) as t:
                    body(t)
                exp(TILES - 1)
                pt_evac(TILES - 1)
                o_hi(TILES - 1)

                for t in range(TILES):
                    act.wait_ge(s_ntp, t + 1)
                    act.activation(x3hi[:, :, t * P:(t + 1) * P], ring[t].rearrange("p (c n) -> p c n", c=KC),
                                   ACT.Copy).then_inc(s_x3hi, 1)
                act.wait_ge(s_gst, 1)
                act.activation(gexp[:], gap[:], ACT.Exp).then_inc(s_gexp, 1)
                for t in range(TILES):
                    act.wait_ge(s_gtp, t + 1)
                    act.activation(gt[:, t, :], ring[t][0:NE, 0:P], ACT.Copy).then_inc(s_gt, 1)
                act.wait_ge(s_cp, TILES)
                w_hi(E0, 0, 0, 80)
                w_hi(E0 + 1, 1, 1, 80)

                def pair(i):
                    for s in range(2):
                        act.wait_ge(s_mm, (i * 2 + s + 2) * TILES)
                        w_hi(E0 + i * 2 + 2 + s, s, s, i * 16 + 96)

                with act.Fori(0, NE // 2 - 1) as i:
                    pair(i)

            @block.vector
            def _(dve):
                def w_lo(n, slot, raw):
                    dve.wait_ge(s_whi, n + 1)
                    dve.tensor_tensor(wlo[slot][:], wraw[raw][:], whi[slot][:].bitcast(F32),
                                      ALU.subtract).then_inc(s_wlo, 1)

                def ln(n, xt, read, reads):
                    ln_dve_stats(dve, n, xt)
                    dve.wait_ge(s_rstd, n + 1)
                    if read is not None:
                        dve.wait_ge(read, reads)
                    dve.tensor_scalar(xn[:], xt, mv[:, 0:1], rstd[:, 0:1], ALU.subtract, ALU.mult).then_inc(s_xn, 1)

                def xt_lo(t):
                    dve.wait_ge(s_xthi, t + 1)
                    dve.tensor_tensor(xtlo[:], bank[0][:].rearrange("p (c n) -> p c n", c=KC), xthi[:].bitcast(F32),
                                      ALU.subtract).then_inc(s_xtlo, 1)

                def evac(t, u):
                    dve.wait_ge(s_qkvp, t * 3 + u + 1)
                    if not (isinstance(t, int) and t == 0):
                        dve.wait_ge((s_qtp, s_ktp, s_av)[u], t)
                    dve.tensor_tensor((qsb, ksb, vsb)[u][:], bank[1 + u][:], bias[:, u, :],
                                      ALU.add).then_inc(s_qkv, 1)

                def q_blocks(t):
                    dve.wait_ge(s_qtp, t + 1)
                    if not (isinstance(t, int) and t == 0):
                        dve.wait_ge(s_sc, t)
                    for g in range(G):
                        q = bank[0][:, g * P:(g + 1) * P].rearrange("p (b q) -> p b q", b=BT)
                        last = dve.tensor_tensor(qbd[:, g, :, :].rearrange("p b (h q) -> p b h q", h=4),
                                                 q.unsqueeze(2).to_broadcast([P, BT, 4, S]), hms, ALU.mult)
                    last.then_inc(s_qbd, 1)

                def less_max(t):
                    dve.wait_ge(s_sc, t + 1)
                    if not (isinstance(t, int) and t == 0):
                        dve.wait_ge(s_exp, t)
                    dve.tensor_tensor(sm[:], quad[:, 0, :].rearrange("p (a k) -> p a k", k=S), causal,
                                      ALU.add).then_inc(s_m, 1)
                    dve.wait_ge(s_m, t * 3 + 1)
                    dve.tensor_reduce(smax[:], sm[:], AX.X, ALU.max).then_inc(s_m, 1)
                    dve.wait_ge(s_m, t * 3 + 2)
                    dve.tensor_tensor(sm[:], sm[:], over_k(smax[:]), ALU.subtract).then_inc(s_m, 1)

                def norm(t):
                    dve.wait_ge(s_exp, t + 1)
                    dve.tensor_reduce(ssum[:], pr[:], AX.X, ALU.add).then_inc(s_nm, 1)
                    dve.wait_ge(s_nm, t * 2 + 1)
                    dve.reciprocal(sinv[:], ssum[:]).then_inc(s_nm, 1)
                    dve.wait_ge(s_nm, t * 2 + 2)
                    dve.tensor_tensor(pr[:], pr[:], over_k(sinv[:]), ALU.mult).then_inc(s_norm, 1)

                def o_lo(t):
                    dve.wait_ge(s_ohi, t + 1)
                    for h in range(4):
                        r = slice(h * 32, h * 32 + 32)
                        for b in range(BT):
                            last = dve.tensor_tensor(
                                otlo[r, :, b * S:(b + 1) * S],
                                quad[r, b, :].rearrange("p (g h q) -> p g h q", g=G, h=4)[:, :, h, :],
                                othi[r, :, b * S:(b + 1) * S].bitcast(F32), ALU.subtract)
                    last.then_inc(s_olo, 1)

                def add_out(t):
                    dve.wait_ge(s_cp, t + 1)
                    dve.tensor_tensor(x[:, t, :], bank[2][:], x[:, t, :], ALU.add).then_inc(s_xo1, 1)
                    dve.wait_ge(s_xo1, t + 1)
                    dve.tensor_tensor(x[:, t, :], x[:, t, :], bias[:, R_AP - R_AQ, :], ALU.add).then_inc(s_xo, 1)

                ln(TILES, x[:, 0, :], None, 0)
                w_lo(AQ, 0, 0)
                xt_lo(0)
                w_lo(AK, 1, 1)
                w_lo(AV, 2, 0)
                dve.wait_ge(s_bias2, 16)
                evac(0, 0)
                evac(0, 1)
                evac(0, 2)
                dve.wait_ge(s_gwhi, 1)
                dve.tensor_tensor(gwlo[:], gate_w[:], gwhi[:].bitcast(F32), ALU.subtract).then_inc(s_gwlo, 1)
                ln(TILES + 1, x[:, 1, :], s_xtp, 1)
                q_blocks(0)
                w_lo(AP_, 3, 1)

                def body(t, last=False):
                    xt_lo(t)
                    less_max(t - 1)
                    evac(t, 0)
                    norm(t - 1)
                    evac(t, 1)
                    o_lo(t - 1)
                    evac(t, 2)
                    if not last:
                        ln(t + TILES + 1, x[:, t + 1, :], s_xtp, t + 1)
                    q_blocks(t)
                    add_out(t - 1)

                with dve.Fori(1, TILES - 1) as t:
                    body(t)
                body(TILES - 1, last=True)
                less_max(TILES - 1)
                norm(TILES - 1)
                o_lo(TILES - 1)
                add_out(TILES - 1)

                def x3_lo(t):
                    dve.wait_ge(s_x3hi, t + 1)
                    cols = slice(t * P, (t + 1) * P)
                    dve.tensor_tensor(x3lo[:, :, cols], ring[t].rearrange("p (c n) -> p c n", c=KC),
                                      x3hi[:, :, cols].bitcast(F32), ALU.subtract).then_inc(s_x3lo, 1)

                def top(t):
                    dve.wait_ge(s_lgp, t + 1)
                    dve.tensor_tensor(logits[:, t, :], ring[t][:, 0:NE], gate_b[:], ALU.add).then_inc(s_lg, 1)
                    dve.wait_ge(s_lg, t + 1)
                    dve.max(top8[:, t, :], logits[:, t, :]).then_inc(s_top, 1)
                    dve.wait_ge(s_top, t + 1)
                    dve.max_index(idx8[:, t, :], top8[:, t, :], logits[:, t, :]).then_inc(s_idx, 1)

                dve.wait_ge(s_gb, 16)
                for t in range(TILES):
                    dve.wait_ge(s_xo, t + 1)
                    if t == 0:
                        ln(2 * TILES, x[:, 0, :], s_xtp, TILES)
                    else:
                        ln(2 * TILES + t, x[:, t, :], s_ntp, t)
                    x3_lo(t)
                    if t >= 1:
                        top(t - 1)
                top(TILES - 1)

                dve.wait_ge(s_idx, TILES)
                dve.tensor_tensor(gap[:], top8[:, :, 1], top8[:, :, 0], ALU.subtract).then_inc(s_gst, 1)
                dve.tensor_copy(idxf[:], idx8[:, :, 0:2]).then_inc(s_gst, 1)
                dve.wait_ge(s_gexp, 1)
                dve.tensor_scalar(gden[:], gexp[:], 1.0, None, ALU.add).then_inc(s_gst, 1)
                dve.wait_ge(s_gst, 3)
                dve.reciprocal(gtop[:, 0, :], gden[:]).then_inc(s_gst, 1)
                dve.wait_ge(s_gst, 4)
                dve.tensor_tensor(gtop[:, 1, :], gexp[:], gtop[:, 0, :], ALU.mult).then_inc(s_gst, 1)
                dve.wait_ge(s_iota, 1)
                over_t = [P, TILES, NE]
                for k in range(2):
                    dve.tensor_tensor(pick[:, k, :, :], iota[:].unsqueeze(1).to_broadcast(over_t),
                                      idxf[:, :, k].unsqueeze(2).to_broadcast(over_t), ALU.is_equal).then_inc(s_gst, 1)
                dve.wait_ge(s_gst, 7)
                for k in range(2):
                    dve.tensor_tensor(pick[:, k, :, :], pick[:, k, :, :],
                                      gtop[:, k, :].unsqueeze(2).to_broadcast(over_t), ALU.mult).then_inc(s_gst, 1)
                dve.wait_ge(s_gst, 9)
                dve.tensor_tensor(gates[:], pick[:, 0, :, :], pick[:, 1, :, :], ALU.add).then_inc(s_gates, 1)
                dve.wait_ge(s_gates, 1)

                for t in range(TILES):
                    dve.wait_ge(s_mm, t + 1)
                    dve.tensor_tensor(x[:, t, :], ring[t], x[:, t, :], ALU.add).then_inc(s_acc, 1)
                w_lo(E0, 0, 0)
                w_lo(E0 + 1, 1, 1)

                def add_expert(e, t):
                    dve.wait_ge(s_mm, e * TILES + TILES + t + 1)
                    dve.wait_ge(s_acc, e * TILES + t + 1)
                    dve.scalar_tensor_tensor(x[:, t, :], ring[t], gates[:, t, bass.ds(e, 1)], x[:, t, :], ALU.mult,
                                             ALU.add).then_inc(s_acc, 1)

                def pair(i, last=False):
                    for s in range(2):
                        for t in range(TILES):
                            add_expert(i * 2 + s, t)
                        if not last:
                            w_lo(E0 + i * 2 + 2 + s, s, s)

                with dve.Fori(0, NE // 2 - 1) as i:
                    pair(i)
                pair(NE // 2 - 1, last=True)

            @block.tensor
            def _(pe):
                def xn_transposed(t):
                    pe.wait_ge(s_xn, t + TILES + 1)
                    if not (isinstance(t, int) and t == 0):
                        pe.wait_ge(s_qbd, t)
                    for c in range(KC):
                        last = pe.transpose(bank[0][:, c * P:(c + 1) * P], xn[:, c * P:(c + 1) * P], ident)
                    last.then_inc(s_xtp, 1)

                def qkv_product(t, u):
                    if u == 0:
                        pe.wait_ge(s_xtlo, t + 1)
                    if isinstance(t, int) and t == 0:
                        pe.wait_ge(s_wlo, AQ + u + 1)
                    elif u == 0:
                        pe.wait_ge(s_kt, t)
                    elif u == 1:
                        pe.wait_ge(s_qkv, t * 3 - 1)
                        if not (isinstance(t, int) and t <= 1):
                            pe.wait_ge(s_xo1, t - 1)
                    else:
                        pe.wait_ge(s_qkv, t * 3)
                    w = u
                    mm3(pe, bank[1 + u][:], lambda c: xthi[:, c, :], lambda c: xtlo[:, c, :],
                        lambda c: whi[w][:, c, :], lambda c: wlo[w][:, c, :]).then_inc(s_qkvp, 1)

                def qk_transposed(t):
                    pe.wait_ge(s_qkv, t * 3 + 1)
                    for g in range(G):
                        last = pe.transpose(bank[0][:, g * P:(g + 1) * P], qsb[:, g * P:(g + 1) * P], ident)
                    last.then_inc(s_qtp, 1)
                    pe.wait_ge(s_qkv, t * 3 + 2)
                    for g in range(G):
                        last = pe.transpose(bank[1][:, g * P:(g + 1) * P], ksb[:, g * P:(g + 1) * P], ident)
                    last.then_inc(s_ktp, 1)

                def scores(t):
                    pe.wait_ge(s_qbd, t + 1)
                    pe.wait_ge(s_kt, t + 1)
                    if not (isinstance(t, int) and t == 0):
                        pe.wait_ge(s_olo, t)
                    for g in range(G):
                        for b in range(BT):
                            at = (g * BT + b) * S
                            last = pe.matmul(quad[:, 0, at:at + S], qbd[:, g, b, :], kt[:, g, b * S:(b + 1) * S],
                                             start=True, stop=True)
                    last.then_inc(s_sc, 1)

                def probs_transposed(t):
                    pe.wait_ge(s_norm, t + 1)
                    for g in range(G):
                        last = pe.transpose(quad[:, 1, g * P:(g + 1) * P],
                                            pr[:, g * BT:(g + 1) * BT, :].rearrange("p b k -> p (b k)"), ident)
                    last.then_inc(s_ptp, 1)

                def attend(t):
                    pe.wait_ge(s_pt, t + 1)
                    pe.wait_ge(s_qkv, t * 3 + 3)
                    for g in range(G):
                        for b in range(BT):
                            rows = slice(b * S, (b + 1) * S)
                            last = pe.matmul(quad[:, b, g * P:(g + 1) * P], vsb[rows, g * P:(g + 1) * P],
                                             pt[rows, g, :], start=True, stop=True)
                    last.then_inc(s_av, 1)

                def out_product(t):
                    pe.wait_ge(s_olo, t + 1)
                    pe.wait_ge(s_qkv, t * 3 + 5 if not (isinstance(t, int) and t == TILES - 1) else 3 * TILES)
                    if isinstance(t, int):
                        pe.wait_ge(s_wlo, AP_ + 1)
                    mm3(pe, bank[2][:], lambda c: othi[:, c, :], lambda c: otlo[:, c, :],
                        lambda c: whi[3][:, c, :], lambda c: wlo[3][:, c, :]).then_inc(s_cp, 1)

                xn_transposed(0)
                for u in range(3):
                    qkv_product(0, u)
                qk_transposed(0)
                pe.wait_ge(s_wlo, AP_ + 1)

                def body(t):
                    xn_transposed(t)
                    scores(t - 1)
                    qkv_product(t, 0)
                    probs_transposed(t - 1)
                    qkv_product(t, 1)
                    attend(t - 1)
                    qkv_product(t, 2)
                    qk_transposed(t)
                    out_product(t - 1)

                body(1)
                with pe.Fori(2, TILES) as t:
                    body(t)
                scores(TILES - 1)
                probs_transposed(TILES - 1)
                attend(TILES - 1)
                out_product(TILES - 1)

                def x3_transposed(t):
                    pe.wait_ge(s_xn, 2 * TILES + t + 1)
                    if t == 0:
                        pe.wait_ge(s_xo1, TILES)
                    for c in range(KC):
                        last = pe.transpose(ring[t][:, c * P:(c + 1) * P], xn[:, c * P:(c + 1) * P], ident)
                    last.then_inc(s_ntp, 1)

                def gate_logits(t):
                    pe.wait_ge(s_x3lo, t + 1)
                    cols = slice(t * P, (t + 1) * P)
                    mm3(pe, ring[t][:, 0:NE], lambda c: x3hi[:, c, cols], lambda c: x3lo[:, c, cols],
                        lambda c: gwhi[:, c, :], lambda c: gwlo[:, c, :]).then_inc(s_lgp, 1)

                pe.wait_ge(s_gwlo, 1)
                for t in range(TILES):
                    x3_transposed(t)
                    if t >= 1:
                        gate_logits(t - 1)
                gate_logits(TILES - 1)
                pe.wait_ge(s_gates, 1)
                for t in range(TILES):
                    pe.transpose(ring[t][0:NE, 0:P], gates[:, t, :], ident).then_inc(s_gtp, 1)
                pe.wait_ge(s_eb, 16)
                for t in range(TILES):
                    pe.wait_ge(s_gt, t + 1)
                    pe.matmul(ring[t], gt[:, t, :], expert_b[:], start=True, stop=True).then_inc(s_mm, 1)

                def pair(i):
                    for s in range(2):
                        pe.wait_ge(s_wlo, i * 2 + E0 + s + 1)
                        for t in range(TILES):
                            pe.wait_ge(s_acc, (i * 2 + s) * TILES + t + 1)
                            cols = slice(t * P, (t + 1) * P)
                            mm3(pe, ring[t], lambda c: x3hi[:, c, cols], lambda c: x3lo[:, c, cols],
                                lambda c: whi[s][:, c, :], lambda c: wlo[s][:, c, :]).then_inc(s_mm, 1)

                with pe.Fori(0, NE // 2) as i:
                    pair(i)


def kernel(**inputs):
    import numpy as _np
    import concourse.bacc as _bacc
    from concourse import mybir as _mybir
    from concourse.bass_utils import run_bass_kernel_spmd as _run

    a = {k: _np.asarray(v) for k, v in inputs.items()}

    def chunks(w):
        return w.reshape(KC, P, -1).transpose(1, 0, 2)

    def even_odd(w):
        return w.reshape(-1, H, HD // 2, 2).transpose(0, 3, 1, 2).reshape(w.shape)

    wkv, bkv = a["L0_xattn_Wkv"], a["L0_xattn_bkv"]
    wa, ba = a["L0_attn_c_attn_kernel"], a["L0_attn_c_attn_bias"]
    mats = [even_odd(a["L0_xattn_Wq"]), even_odd(wkv[:, :D]), wkv[:, D:], a["L0_xattn_Wo"],
            wa[:D].T, wa[D:2 * D].T, wa[2 * D:].T, a["L0_attn_c_proj_kernel"].T, *a["L0_ffn_expert_w"]]
    ctx = a["ctx_1024"]
    ctx_t = _np.zeros((B, P, KC, LKP), _np.float32)
    ctx_t[:, :, :, :LK] = ctx.reshape(B, LK, KC, P).transpose(0, 3, 2, 1)
    ctx_last = _np.zeros((P, KC, P), _np.float32)
    ctx_last[:, :, :B] = ctx[:, LK - 1, :].reshape(B, KC, P).transpose(2, 1, 0)
    arrays = {
        "x": a["x"].reshape(B * S, D),
        "ctx_t": ctx_t,
        "ctx_last": ctx_last,
        "mask": a["mask_BxS2_bf1"].view(_np.uint8),
        "weights": _np.stack([chunks(m) for m in mats]),
        "biases": _np.stack([even_odd(a["L0_xattn_bq"][None])[0], bkv[D:], a["L0_xattn_bo"], ba[:D], ba[D:2 * D],
                             ba[2 * D:], a["L0_attn_c_proj_bias"]]),
        "bias_k": even_odd(bkv[None, :D])[0].reshape(4, P).T,
        "gate_w": chunks(a["L0_ffn_gate_w"].T),
        "gate_b": a["L0_ffn_gate_b"],
        "expert_b": a["L0_ffn_expert_b"],
        "constants": constants(),
    }
    arrays = {f"{k}_dram": _np.ascontiguousarray(v) for k, v in arrays.items()}
    nc = _bacc.Bacc("TRN2", target_bir_lowering=False, num_devices=1)
    args = [nc.dram_tensor(k, v.shape, _mybir.dt.from_np(v.dtype), kind="ExternalInput").ap() for k, v in arrays.items()]
    out = nc.dram_tensor("out_dram", [B * S, D], _mybir.dt.float32, kind="ExternalOutput").ap()
    perceiver(nc, *args, out)
    r = _run(nc, [arrays], core_ids=[0])
    return r.results[0]["out_dram"].reshape(B, S, D)
```

```python
from contextlib import ExitStack

import numpy as np
import concourse.bass as bass
from concourse import mybir

F32 = mybir.dt.float32
F32R = mybir.dt.float32r
U8 = mybir.dt.uint8
U32 = mybir.dt.uint32
ALU = mybir.AluOpType
ACT = mybir.ActivationFunctionType
AX = mybir.AxisListType

P = 128
B, S, D, LK = 32, 32, 512, 257
H, HD = 16, 32
KC = D // P
G = H // 4
TILES = B * S // P
BT = P // S
NE = 8
LKP = LK + 1
EPS = 1e-5
X_SCALE = 64.0 ** -0.5
BLOW = 8.0
A_SCALE = float(np.float32(1.0) / np.sqrt(np.float32(HD)))
WK, WQ, WV, WO, AQ, AK, AV, AP_, E0 = range(9)
SLOT = (0, 1, 2, 3, 1, 0, 2, 3)
R_BQ, R_BV, R_BO, R_AQ, R_AK, R_AV, R_AP = range(7)

C_ID = 0
C_COSK = C_ID + P
C_SINK = C_COSK + LKP
C_COSQ = C_SINK + LKP
C_SINQ = C_COSQ + HD // 2
C_HMX = C_SINQ + HD // 2
C_HMS = C_HMX + 4
C_CAUSAL = C_HMS + 4
C_EYE = C_CAUSAL + S
C_SAME = C_EYE + S
C_ALL = C_SAME + P


def constants():
    inv = (1.0 / 10000.0 ** (np.arange(0, HD, 2, dtype=np.float32) / np.float32(HD))).astype(np.float32)

    def angles(n):
        pos = np.float32(10.0) * (np.arange(n, dtype=np.float32) / np.float32(n))
        return (pos[:, None] * inv).astype(np.float32).astype(np.float64)

    c = np.zeros((P, C_ALL), np.float32)
    row = np.arange(P)
    c[:, C_ID:C_ID + P] = np.eye(P)
    k = angles(LK)
    c[:, C_COSK:C_COSK + LK] = np.cos(k).T[row % 16]
    c[:, C_SINK:C_SINK + LK] = np.sin(k).T[row % 16]
    q = angles(S)
    c[:, C_COSQ:C_COSQ + 16] = np.cos(q).astype(np.float32)[row % S] * np.float32(X_SCALE / BLOW)
    c[:, C_SINQ:C_SINQ + 16] = np.sin(q).astype(np.float32)[row % S] * np.float32(X_SCALE / BLOW)
    c[:, C_HMX:C_HMX + 4] = (row % 64 // 16)[:, None] == np.arange(4)
    c[:, C_HMS:C_HMS + 4] = (row // 32)[:, None] == np.arange(4)
    c[:, C_CAUSAL:C_CAUSAL + S] = np.where(np.arange(S)[None, :] <= (row % S)[:, None], 0.0, np.finfo(np.float32).min)
    c[:, C_EYE:C_EYE + S] = (row % S)[:, None] == np.arange(S)
    c[:, C_SAME:C_SAME + P] = (row // S)[:, None] == (row // S)[None, :]
    return c


def perceiver(nc, x_in, ctx_in, ctx_last_in, mask_in, w_in, bias_in, bias_cols_in, gate_w_in, gate_b_in,
              expert_b_in, const_in, out):
    with ExitStack() as top:
        def sem(name):
            return top.enter_context(nc.semaphore(name))

        def sbuf(stack, name, shape, dt=F32):
            return stack.enter_context(nc.sbuf_tensor(name, shape, dt))

        const = sbuf(top, "const", [P, C_ALL])
        ident = const[:, C_ID:C_ID + P]
        x = sbuf(top, "x", [P, TILES, D])
        whi = [sbuf(top, f"whi{i}", [P, KC, D], F32R) for i in range(4)]
        wlo = [sbuf(top, f"wlo{i}", [P, KC, D], F32R) for i in range(4)]
        wraw = [sbuf(top, f"wraw{i}", [P, KC, D]) for i in range(2)]
        craw = [sbuf(top, f"craw{i}", [P, KC, LKP]) for i in range(2)]
        xthi = sbuf(top, "xthi", [P, KC, P], F32R)
        xtlo = sbuf(top, "xtlo", [P, KC, P], F32R)
        stats = sbuf(top, "stats", [P, 6])
        mv = sbuf(top, "mv", [P, 2])
        neghalf = sbuf(top, "neghalf", [P, 1])
        vareps = sbuf(top, "vareps", [P, 1])
        rstd = sbuf(top, "rstd", [P, 1])
        xn = sbuf(top, "xn", [P, D])
        tick = sbuf(top, "tick", [1, G + 1])

        bank = [top.enter_context(nc.psum_tensor(f"bank{i}", [P, 512], F32)) for i in range(4)]
        quad = top.enter_context(nc.psum_tensor("quad", [P, 4, 512], F32))

        s_const, s_x0, s_x, s_bias, s_maskin, s_clast, s_biask = (sem(n) for n in (
            "const_in", "x_first_tile_in", "x_in", "bias_in", "mask_in", "ctx_last_in", "bias_k_in"))
        s_wk = [sem(f"first_weight_chunk{c}_in") for c in range(KC)]
        s_wraw = [sem(f"weight_raw_in{i}") for i in range(2)]
        s_whi, s_wlo = sem("weight_hi_done"), sem("weight_lo_done")
        s_bias2 = sem("bias_self_in")
        s_stats, s_mv, s_var, s_rstd, s_xn, s_xtp, s_xthi, s_xtlo = (sem(n) for n in (
            "ln_stats_done", "ln_mv_done", "ln_var_done", "ln_rstd_done", "ln_xn_done", "xn_t_done", "xn_t_hi_done",
            "xn_t_lo_done"))
        s_qp, s_kp, s_vp = sem("self_q_done"), sem("self_k_done"), sem("self_v_done")

        def mm3(pe, psum, ahi, alo, bhi, blo, chunks=KC, before=None):
            for c in range(chunks):
                if before is not None:
                    before(c)
                pe.matmul(psum, ahi(c), bhi(c), start=(c == 0), stop=False)
                pe.matmul(psum, ahi(c), blo(c), start=False, stop=False)
                last = pe.matmul(psum, alo(c), bhi(c), start=False, stop=(c == chunks - 1))
            return last

        def raw_count(n):
            return 16 * (n // 2 + n % 2)

        def ln_dve_stats(dve, n, xt):
            dve.bn_stats(stats[:], xt).then_inc(s_stats, 1)
            dve.wait_ge(s_stats, n + 1)
            dve.memset(tick[:, G:G + 1], 0.0)
            dve.bn_aggr(mv[:], stats[:]).then_inc(s_mv, 1)
            dve.wait_ge(s_mv, n + 1)
            dve.tensor_scalar(vareps[:], mv[:, 1:2], EPS, None, ALU.add).then_inc(s_var, 1)

        def ln_pool(pool, n):
            pool.wait_ge(s_var, n + 1)
            pool.tensor_tensor(rstd[:], vareps[:], neghalf[:], ALU.pow).then_inc(s_rstd, 1)

        with ExitStack() as ph:
            def sb(name, shape, dt=F32):
                return sbuf(ph, name, shape, dt)

            maskb8 = sb("maskb8", [P, B, LK], U8)
            bias = sb("bias_cross", [P, R_AQ, D])
            bias_cols = sb("bias_cols", [P, 4 + G])
            chi = [sb(f"chi{i}", [P, KC, LKP], F32R) for i in range(2)]
            clo = [sb(f"clo{i}", [P, KC, LKP], F32R) for i in range(2)]
            kb = sb("kb", [P, 4, LKP])
            kcos = sb("kcos", [P, 4, LKP])
            ksin = sb("ksin", [P, 4, LKP])
            kr = [sb(f"kr{i}", [P, G, LKP]) for i in range(2)]
            v = [sb(f"v{i}", [P, 2, D]) for i in range(2)]
            mb = [sb(f"mb{i}", [P, LK]) for i in range(2)]
            qb = sb("qb", [P, D])
            qcos = sb("qcos", [P, D])
            qsin = sb("qsin", [P, D])
            qr = qb[:].rearrange("p (g n) -> p g n", g=G)
            qt = sb("qt", [P, G, P])
            qbd = [sb(f"qbd{i}", [P, G, P]) for i in range(2)]
            sm = [sb(f"sm{i}", [P, LK]) for i in range(2)]
            pr = sb("pr", [P, G, LKP])
            vlast = sb("vlast", [P, G, B])
            pdiag = sb("pdiag", [P, G, S])
            olast = sb("olast", [P, G, S])
            osum = sb("osum", [P, G, S])
            nmax = sb("nmax", [P, G])
            rsum = sb("rsum", [P, G])
            rinv = sb("rinv", [P, G])
            pt = [sb(f"pt{i}", [P, 2 * P]) for i in range(2)]
            othi = sb("othi", [P, G, P], F32R)
            otlo = sb("otlo", [P, G, P], F32R)

            proj = bank[0:3]
            score = [bank[3], quad[:, 0, :]]
            ptp = quad[:, 1, :]
            extra = quad[:, 2, :]
            av = quad[:, 3, 0:P]
            plast = quad[:, 3, P:2 * P]

            s_zero, s_wkhi, s_wklo = sem("zeroed"), sem("first_weight_hi_chunks"), sem("first_weight_lo_chunks")
            s_ctx = [sem(f"ctx_raw_in{i}") for i in range(2)]
            s_pdiag, s_last, s_olast, s_osum = (sem(n) for n in (
                "p_last_diagonal_done", "p_last_spread", "o_last_done", "o_sum_done"))
            (s_clhi, s_cllo, s_vl, s_vlsb, s_chi, s_clo, s_proj, s_kev, s_vev, s_kcos, s_ksin, s_kr, s_qbd,
             s_mb, s_sc, s_sm, s_exp, s_rinv, s_norm, s_ptp, s_pt, s_av, s_ohi, s_olo, s_wo, s_xwo, s_xb,
             s_qmm, s_qb, s_qcos, s_qr, s_qtp, s_qt) = (sem(n) for n in (
                 "ctx_last_hi_done", "ctx_last_lo_done", "v_last_done", "v_last_in_sbuf",
                 "ctx_hi_done", "ctx_lo_done", "proj_done", "k_evacuated", "v_evacuated", "k_cos_done", "k_sin_done",
                 "k_rotated", "q_blocks_done", "mask_bias_done", "scores_done", "scores_masked", "exp_done",
                 "rsum_inverted", "probs_normed", "probs_t_done", "probs_t_in_sbuf", "attn_done", "attn_hi_done",
                 "attn_lo_done", "out_proj_done", "x_with_out_proj", "x_with_bias",
                 "q_done", "q_in_sbuf", "q_trig_done", "q_rotated", "q_t_done", "q_t_in_sbuf"))

            cosk = const[:, C_COSK:C_COSK + LKP].unsqueeze(1).to_broadcast([P, 4, LKP])
            sink = const[:, C_SINK:C_SINK + LKP].unsqueeze(1).to_broadcast([P, 4, LKP])
            cosq = const[:, C_COSQ:C_COSQ + 16].unsqueeze(1).to_broadcast([P, 2 * H, 16])
            sinq = const[:, C_SINQ:C_SINQ + 16].unsqueeze(1).to_broadcast([P, 2 * H, 16])
            eye = const[:, C_EYE:C_EYE + S].unsqueeze(1).to_broadcast([P, G, S])
            hmx = const[:, C_HMX:C_HMX + 4].unsqueeze(1).unsqueeze(3).to_broadcast([P, G, 4, S])

            block = ph.enter_context(nc.Block())

            @block.sync
            def _(sp):
                def weight(n):
                    if n == WK + 2:
                        sp.wait_ge(s_wklo, KC)
                    elif n > WK + 2:
                        sp.wait_ge(s_wlo, n - 2)
                    sp.dma_start(wraw[n % 2][:], w_in[n]).then_inc(s_wraw[n % 2], 16)

                def ctx(b, j):
                    sp.dma_start(craw[j % 2][:], ctx_in[b]).then_inc(s_ctx[j % 2], 16)

                ctx(0, 0)
                for c in range(KC):
                    sp.dma_start(wraw[0][:, c, :], w_in[WK][:, c, :]).then_inc(s_wk[c], 16)
                sp.dma_start(x[:, 0, :], x_in[0:P, :]).then_inc(s_x0, 16)
                sp.dma_start(const[:], const_in).then_inc(s_const, 16)
                sp.dma_start(bias_cols[:], bias_cols_in).then_inc(s_biask, 16)
                weight(WQ)
                sp.dma_start(bias[:], bias_in[0:R_AQ, :].partition_broadcast(P)).then_inc(s_bias, 16)
                sp.dma_start(craw[1][:, :, 0:B], ctx_last_in).then_inc(s_clast, 16)
                weight(WV)
                sp.dma_start(maskb8[:], mask_in.partition_broadcast(P)).then_inc(s_maskin, 16)
                weight(WO)
                sp.wait_ge(s_cllo, 1)
                ctx(1, 1)
                for t in range(1, TILES):
                    sp.dma_start(x[:, t, :], x_in[t * P:(t + 1) * P, :]).then_inc(s_x, 16)

                def step(t, j, last):
                    b = t * BT + j
                    if not (last and j >= BT - 2):
                        sp.wait_ge(s_clo, b + 1)
                        ctx(b + 2, j)

                def body(t, last=False):
                    for j in range(BT):
                        step(t, j, last)

                body(0)
                weight(AQ)
                weight(AK)
                with sp.Fori(1, TILES - 1) as t:
                    body(t)
                body(TILES - 1, last=True)
                weight(AV)
                for i in range(2):
                    sp.wait_ge(s_clo, B - 1 + i)
                    rows = bias_in[R_AQ + 2 * i:R_AQ + 2 * i + 2, :].partition_broadcast(P)
                    sp.dma_start(craw[i][:].rearrange("p c n -> p (c n)")[:, 0:2 * D].rearrange("p (r n) -> p r n", r=2),
                                 rows).then_inc(s_bias2, 16)
                weight(AP_)

            @block.gpsimd
            def _(pool):
                pool.memset(neghalf[:], -0.5).then_inc(s_zero, 1)
                def k_sin(b):
                    pool.wait_ge(s_kev, (b + 1) * 4)
                    if not (isinstance(b, int) and b == 0):
                        pool.wait_ge(s_kr, b)
                    pool.tensor_tensor(ksin[:], kb[:], sink, ALU.mult).then_inc(s_ksin, 1)

                def p_last(b):
                    pool.wait_ge(s_norm, (b + 1) * G)
                    if not (isinstance(b, int) and b == 0):
                        pool.wait_ge(s_last, b)
                    pool.tensor_tensor(pdiag[:], pr[:, :, LK - 1].unsqueeze(2).to_broadcast([P, G, S]), eye,
                                       ALU.mult).then_inc(s_pdiag, 1)

                def q_blocks(b, t, j):
                    pool.wait_ge(s_qt, t + 1)
                    if not (isinstance(b, int) and b < 2):
                        pool.wait_ge(s_sc, (b - 1) * G)
                    q = qt[:, :, j * S:(j + 1) * S].unsqueeze(2).to_broadcast([P, G, 4, S])
                    pool.tensor_tensor(qbd[j % 2][:].rearrange("p g (h q) -> p g h q", h=4), q, hmx,
                                       ALU.mult).then_inc(s_qbd, 1)

                pool.wait_ge(s_const, 16)
                ln_pool(pool, 0)
                k_sin(0)
                q_blocks(0, 0, 0)

                def wo_lo():
                    pool.wait_ge(s_whi, WO)
                    pool.wait_ge(s_wlo, WO - 1)
                    pool.tensor_tensor(wlo[WO][:], wraw[WO % 2][:], whi[WO][:].bitcast(F32),
                                       ALU.subtract).then_inc(s_wlo, 1)

                def body(t, last=False):
                    for j in range(BT):
                        if not (last and j == BT - 1):
                            if j < BT - 1:
                                q_blocks(t * BT + j + 1, t, j + 1)
                            else:
                                q_blocks(t * BT + BT, t + 1, 0)
                            k_sin(t * BT + j + 1)
                        p_last(t * BT + j)
                        if j == 0:
                            ln_pool(pool, t + 1)
                        if j == 0 and isinstance(t, int) and t == 0:
                            wo_lo()

                body(0)
                with pool.Fori(1, TILES - 1) as t:
                    body(t)
                body(TILES - 1, last=True)
                ln_pool(pool, TILES + 1)

            @block.scalar
            def _(act):
                def w_hi(n):
                    act.wait_ge(s_wraw[n % 2], raw_count(n))
                    act.activation(whi[SLOT[n]][:], wraw[n % 2][:], ACT.Copy).then_inc(s_whi, 1)

                def ctx_hi_at(t, j2):
                    b = t * BT + j2
                    act.wait_ge(s_ctx[j2 % 2], (t * 2 + j2 // 2 + 1) * 16)
                    if not (isinstance(b, int) and b < 2):
                        act.wait_ge(s_proj, (b - 1) * 6)
                    act.activation(chi[j2 % 2][:], craw[j2 % 2][:], ACT.Copy).then_inc(s_chi, 1)

                def k_evac(b, m):
                    act.wait_ge(s_proj, b * 6 + m + 1)
                    if m == 0 and not (isinstance(b, int) and b == 0):
                        act.wait_ge(s_kcos, b)
                        act.wait_ge(s_ksin, b)
                    act.activation(kb[:, m, :], proj[m % 3][:, 0:LKP], ACT.Identity,
                                   bias=bias_cols[:, m:m + 1]).then_inc(s_kev, 1)

                def exp(b, g):
                    n = b * G + g
                    act.wait_ge(s_sm, n + 1)
                    if not (isinstance(b, int) and b == 0):
                        act.wait_ge(s_ptp, n - G + 1)
                        if g == 0:
                            act.wait_ge(s_pdiag, b)
                    act.activation(pr[:, g, 0:LK], sm[g % 2][:], ACT.Exp, bias=nmax[:, g:g + 1], scale=-1.0,
                                   accum_out=rsum[:, g:g + 1]).then_inc(s_exp, 1)

                def pt_evac(b, g):
                    n = b * G + g
                    act.wait_ge(s_ptp, n + 1)
                    if not (isinstance(b, int) and n < 2):
                        act.wait_ge(s_av, n - 1)
                    act.activation(pt[g % 2][:], ptp[:, 0:2 * P], ACT.Copy).then_inc(s_pt, 1)

                def o_hi(b, t, j):
                    act.wait_ge(s_osum, b + 1)
                    if j == 0 and not (isinstance(t, int) and t == 0):
                        act.wait_ge(s_wo, t)
                    act.activation(othi[:, :, j * S:(j + 1) * S], osum[:], ACT.Copy).then_inc(s_ohi, 1)

                def mask_bias(b, j):
                    if not (isinstance(b, int) and b < 2):
                        act.wait_ge(s_sm, (b - 1) * G)
                    act.activation(mb[j % 2][:], maskb8[:, b, :], ACT.Copy, bias=-3e38, scale=3e38).then_inc(s_mb, 1)

                def xt_hi(t):
                    act.wait_ge(s_xtp, t + 1)
                    if not (isinstance(t, int) and t == 0):
                        act.wait_ge(s_qmm, t)
                    act.activation(xthi[:], extra.rearrange("p (c n) -> p c n", c=KC), ACT.Copy).then_inc(s_xthi, 1)

                def qt_evac(t):
                    act.wait_ge(s_qtp, t + 1)
                    if not (isinstance(t, int) and t == 0):
                        act.wait_ge(s_qbd, t * BT)
                    act.activation(qt[:], extra.rearrange("p (g n) -> p g n", g=G), ACT.Copy).then_inc(s_qt, 1)

                ctx_hi_at(0, 0)
                for c in range(KC):
                    act.wait_ge(s_wk[c], 16)
                    act.activation(whi[WK][:, c, :], wraw[0][:, c, :], ACT.Copy).then_inc(s_wkhi, 1)
                act.wait_ge(s_biask, 16)
                k_evac(0, 0)
                w_hi(WQ)
                for m in range(1, 4):
                    k_evac(0, m)
                xt_hi(0)
                act.wait_ge(s_clast, 16)
                act.activation(chi[1][:, :, 0:B], craw[1][:, :, 0:B], ACT.Copy).then_inc(s_clhi, 1)
                w_hi(WV)
                act.wait_ge(s_vl, 1)
                ctx_hi_at(0, 1)
                w_hi(WO)
                qt_evac(0)
                act.wait_ge(s_maskin, 16)
                mask_bias(0, 0)

                def body(t, last=False):
                    for j in range(BT):
                        b = t * BT + j
                        more = not (last and j == BT - 1)
                        if more:
                            k_evac(b + 1, 0)
                        if j == 3 and not last:
                            qt_evac(t + 1)
                        if j == 1:
                            xt_hi(t + 1)
                        exp(b, 0)
                        if not (j == 0 and isinstance(t, int) and t == 0):
                            o_hi(b - 1, t if j > 0 else t - 1, (j + BT - 1) % BT)
                        if more:
                            k_evac(b + 1, 1)
                        exp(b, 1)
                        if more:
                            k_evac(b + 1, 2)
                        pt_evac(b, 0)
                        exp(b, 2)
                        if more:
                            k_evac(b + 1, 3)
                            mask_bias(b + 1, j + 1)
                        pt_evac(b, 1)
                        exp(b, 3)
                        if not (last and j >= BT - 2):
                            ctx_hi_at(t, j + 2)
                        pt_evac(b, 2)
                        pt_evac(b, 3)
                        if last and j == 0:
                            act.wait_ge(s_qmm, TILES)
                            w_hi(AQ)
                        if last and j == 2:
                            act.wait_ge(s_proj, B * 6)
                            w_hi(AK)
                            w_hi(AV)

                body(0)
                with act.Fori(1, TILES - 1) as t:
                    body(t)
                body(TILES - 1, last=True)
                o_hi(B - 1, TILES - 1, BT - 1)

            @block.vector
            def _(dve):
                def w_lo(n):
                    dve.wait_ge(s_whi, n)
                    dve.tensor_tensor(wlo[SLOT[n]][:], wraw[n % 2][:], whi[SLOT[n]][:].bitcast(F32),
                                      ALU.subtract).then_inc(s_wlo, 1)

                def ctx_lo(b, j):
                    dve.wait_ge(s_chi, b + 1)
                    dve.tensor_tensor(clo[j % 2][:], craw[j % 2][:], chi[j % 2][:].bitcast(F32),
                                      ALU.subtract).then_inc(s_clo, 1)

                def ln(t, xt):
                    ln_dve_stats(dve, t, xt)
                    dve.wait_ge(s_rstd, t + 1)
                    if not (isinstance(t, int) and t == 0):
                        dve.wait_ge(s_xtp, t)
                    dve.tensor_scalar(xn[:], xt, mv[:, 0:1], rstd[:, 0:1], ALU.subtract,
                                      ALU.mult).then_inc(s_xn, 1)

                def xt_lo(t):
                    dve.wait_ge(s_xthi, t + 1)
                    dve.tensor_tensor(xtlo[:], extra.rearrange("p (c n) -> p c n", c=KC), xthi[:].bitcast(F32),
                                      ALU.subtract).then_inc(s_xtlo, 1)

                def q_rope(t):
                    dve.wait_ge(s_qmm, t + 1)
                    if not (isinstance(t, int) and t == 0):
                        dve.wait_ge(s_qtp, t)
                    dve.tensor_tensor(qb[:], extra, bias[:, R_BQ, :], ALU.add).then_inc(s_qb, 1)
                    dve.wait_ge(s_qb, t + 1)
                    qv = qb[:].rearrange("p (a i) -> p a i", i=16)
                    dve.tensor_tensor(qcos[:].rearrange("p (a i) -> p a i", i=16), qv, cosq, ALU.mult)
                    dve.tensor_tensor(qsin[:].rearrange("p (a i) -> p a i", i=16), qv, sinq,
                                      ALU.mult).then_inc(s_qcos, 1)
                    dve.wait_ge(s_qcos, t + 1)
                    ev, od = slice(0, D // 2), slice(D // 2, D)
                    dve.tensor_tensor(qr[:, :, 0:64], qcos[:, ev].rearrange("p (g n) -> p g n", g=G),
                                      qsin[:, od].rearrange("p (g n) -> p g n", g=G), ALU.subtract)
                    dve.tensor_tensor(qr[:, :, 64:128], qsin[:, ev].rearrange("p (g n) -> p g n", g=G),
                                      qcos[:, od].rearrange("p (g n) -> p g n", g=G), ALU.add).then_inc(s_qr, 1)

                def k_cos(b):
                    dve.wait_ge(s_kev, (b + 1) * 4)
                    dve.tensor_tensor(kcos[:], kb[:], cosk, ALU.mult).then_inc(s_kcos, 1)

                def k_rotate(b, j):
                    dve.wait_ge(s_kcos, b + 1)
                    dve.wait_ge(s_ksin, b + 1)
                    if not (isinstance(b, int) and b < 2):
                        dve.wait_ge(s_sc, (b - 1) * G)
                    pairs = kr[j % 2][:].rearrange("p (a two) n -> p a two n", two=2)
                    for half in range(2):
                        rows = slice(half * 64, half * 64 + 64)
                        dve.tensor_tensor(pairs[0:64, :, half, :], kcos[rows, 0:2, :], ksin[rows, 2:4, :], ALU.subtract)
                        last = dve.tensor_tensor(pairs[64:128, :, half, :], ksin[rows, 0:2, :], kcos[rows, 2:4, :], ALU.add)
                    last.then_inc(s_kr, 1)

                def v_evac(b, j, c):
                    dve.wait_ge(s_proj, b * 6 + 4 + c + 1)
                    if c == 0 and not (isinstance(b, int) and b < 2):
                        dve.wait_ge(s_av, (b - 1) * G)
                    dve.tensor_tensor(v[j % 2][:, c, :], proj[(4 + c) % 3][:], bias[:, R_BV, :],
                                      ALU.add).then_inc(s_vev, 1)

                def masked(b, j, g):
                    n = b * G + g
                    dve.wait_ge(s_sc, n + 1)
                    if g == 0:
                        dve.wait_ge(s_mb, b + 1)
                    if not (isinstance(b, int) and n < 2):
                        dve.wait_ge(s_exp, n - 1)
                    dve.memset(tick[:, g:g + 1], 0.0)
                    dve.tensor_tensor_reduce(sm[g % 2][:], score[g % 2][:, 0:LK], mb[j % 2][:], -BLOW, 3.4e38,
                                             ALU.add, ALU.min, nmax[:, g:g + 1]).then_inc(s_sm, 1)

                def norm(b, g):
                    n = b * G + g
                    dve.wait_ge(s_exp, n + 1)
                    dve.reciprocal(rinv[:, g:g + 1], rsum[:, g:g + 1]).then_inc(s_rinv, 1)
                    dve.wait_ge(s_rinv, n + 1)
                    dve.tensor_scalar(pr[:, g, 0:LK], pr[:, g, 0:LK], rinv[:, g:g + 1], None,
                                      ALU.mult).then_inc(s_norm, 1)

                def o_sum(b):
                    dve.wait_ge(s_last, b + 1)
                    dve.tensor_tensor(olast[:], plast.rearrange("p (g q) -> p g q", g=G),
                                      vlast[:, :, b].unsqueeze(2).to_broadcast([P, G, S]), ALU.mult).then_inc(s_olast, 1)
                    dve.wait_ge(s_olast, b + 1)
                    dve.tensor_tensor(osum[:], av.rearrange("p (g q) -> p g q", g=G), olast[:], ALU.add).then_inc(s_osum, 1)

                def o_lo(b, j):
                    dve.wait_ge(s_ohi, b + 1)
                    dve.tensor_tensor(otlo[:, :, j * S:(j + 1) * S], osum[:],
                                      othi[:, :, j * S:(j + 1) * S].bitcast(F32), ALU.subtract).then_inc(s_olo, 1)

                def add_out(t):
                    dve.wait_ge(s_wo, t + 1)
                    dve.tensor_tensor(x[:, t, :], extra, x[:, t, :], ALU.add).then_inc(s_xwo, 1)
                    dve.wait_ge(s_xwo, t + 1)
                    dve.tensor_tensor(x[:, t, :], x[:, t, :], bias[:, R_BO, :], ALU.add).then_inc(s_xb, 1)

                ctx_lo(0, 0)
                for c in range(KC):
                    dve.wait_ge(s_wkhi, c + 1)
                    dve.tensor_tensor(wlo[WK][:, c, :], wraw[0][:, c, :], whi[WK][:, c, :].bitcast(F32),
                                      ALU.subtract).then_inc(s_wklo, 1)
                dve.wait_ge(s_x0, 16)
                dve.wait_ge(s_zero, 1)
                ln(0, x[:, 0, :])
                w_lo(WQ)
                dve.wait_ge(s_const, 16)
                xt_lo(0)
                k_cos(0)
                dve.wait_ge(s_clhi, 1)
                dve.tensor_tensor(clo[1][:, :, 0:B], craw[1][:, :, 0:B], chi[1][:, :, 0:B].bitcast(F32),
                                  ALU.subtract).then_inc(s_cllo, 1)
                w_lo(WV)
                dve.wait_ge(s_bias, 16)
                q_rope(0)
                dve.wait_ge(s_vl, 1)
                dve.wait_ge(s_biask, 16)
                dve.tensor_tensor(vlast[:], ptp[:, 0:G * B].rearrange("p (g b) -> p g b", g=G),
                                  bias_cols[:, 4:4 + G].unsqueeze(2).to_broadcast([P, G, B]), ALU.add).then_inc(s_vlsb, 1)
                ctx_lo(1, 1)
                k_rotate(0, 0)
                v_evac(0, 0, 0)
                v_evac(0, 0, 1)
                dve.wait_ge(s_x, 16 * (TILES - 1))

                def body(t, first=False, last=False):
                    for j in range(BT):
                        b = t * BT + j
                        more = not (last and j == BT - 1)
                        if j == 1:
                            xt_lo(t + 1)
                        masked(b, j, 0)
                        if not (first and j == 0):
                            o_sum(b - 1)
                        masked(b, j, 1)
                        if not (first and j == 0):
                            o_lo(b - 1, (j + BT - 1) % BT)
                        norm(b, 0)
                        masked(b, j, 2)
                        norm(b, 1)
                        if j == 0 and not first:
                            add_out(t - 1)
                        masked(b, j, 3)
                        norm(b, 2)
                        if more:
                            k_cos(b + 1)
                        norm(b, 3)
                        if more:
                            k_rotate(b + 1, j + 1)
                            v_evac(b + 1, j + 1, 0)
                        if not (last and j >= BT - 2):
                            ctx_lo(b + 2, j)
                        if j == 0:
                            ln(t + 1, x[:, 0 if last else t + 1, :])
                        if j == 2 and not last:
                            q_rope(t + 1)
                        if more:
                            v_evac(b + 1, j + 1, 1)
                        if last and j == 0:
                            w_lo(AQ)
                        if last and j == 2:
                            w_lo(AK)
                            w_lo(AV)
                        if last and j == 3:
                            ln(TILES + 1, x[:, 1, :])

                body(0, first=True)
                with dve.Fori(1, TILES - 1) as t:
                    body(t)
                body(TILES - 1, last=True)
                o_sum(B - 1)
                o_lo(B - 1, BT - 1)
                add_out(TILES - 1)

            @block.tensor
            def _(pe):
                def xn_transposed(t):
                    pe.wait_ge(s_xn, t + 1)
                    if not (isinstance(t, int) and t == 0):
                        pe.wait_ge(s_qt, t)
                    if not (isinstance(t, int) and t <= 1):
                        pe.wait_ge(s_xwo, t - 1)
                    for c in range(KC):
                        last = pe.transpose(extra[:, c * P:(c + 1) * P], xn[:, c * P:(c + 1) * P], ident)
                    last.then_inc(s_xtp, 1)

                def q_product(t):
                    pe.wait_ge(s_xtlo, t + 1)
                    mm3(pe, extra, lambda c: xthi[:, c, :], lambda c: xtlo[:, c, :],
                        lambda c: whi[WQ][:, c, :], lambda c: wlo[WQ][:, c, :]).then_inc(s_qmm, 1)

                def q_transposed(t):
                    pe.wait_ge(s_qr, t + 1)
                    for g in range(G):
                        last = pe.transpose(extra[:, g * P:(g + 1) * P], qr[:, g, :], ident)
                    last.then_inc(s_qtp, 1)

                def wk_chunk(c):
                    pe.wait_ge(s_wklo, c + 1)

                def k_product(b, j, m):
                    if m == 0:
                        pe.wait_ge(s_clo, b + 1)
                    if not (isinstance(b, int) and b == 0 and m < 3):
                        if m == 0:
                            pe.wait_ge(s_kev, b * 4)
                        elif m < 3:
                            pe.wait_ge(s_vev, b * 2 - 2 + m)
                        else:
                            pe.wait_ge(s_kev, b * 4 + 1)
                    mm3(pe, proj[m % 3][:, 0:LKP],
                        lambda c: whi[WK][:, c, m * P:(m + 1) * P], lambda c: wlo[WK][:, c, m * P:(m + 1) * P],
                        lambda c: chi[j % 2][:, c, :], lambda c: clo[j % 2][:, c, :],
                        before=wk_chunk if isinstance(b, int) and b == 0 and m == 0 else None).then_inc(s_proj, 1)

                def v_product(b, j, u, part):
                    psum = proj[(4 + u) % 3][:]
                    if part == 0:
                        pe.wait_ge(s_kev, b * 4 + 2 + u)
                    for c in (0, 1) if part == 0 else (2, 3):
                        hi, lo = (a[j % 2][:, c, u * P:(u + 1) * P] for a in (chi, clo))
                        pe.matmul(psum, hi, whi[WV][:, c, :], start=(c == 0), stop=False)
                        pe.matmul(psum, hi, wlo[WV][:, c, :], start=False, stop=False)
                        last = pe.matmul(psum, lo, whi[WV][:, c, :], start=False, stop=(c == KC - 1))
                    if part == 1:
                        last.then_inc(s_proj, 1)

                def scores(b, j, g):
                    n = b * G + g
                    if g == 0:
                        pe.wait_ge(s_kr, b + 1)
                        pe.wait_ge(s_qbd, b + 1)
                    if not (isinstance(b, int) and n < 2):
                        pe.wait_ge(s_sm, n - 1)
                    pe.matmul(score[g % 2][:, 0:LK], qbd[j % 2][:, g, :], kr[j % 2][:, g, 0:LK],
                              start=True, stop=True).then_inc(s_sc, 1)

                def probs_transposed(b, g):
                    n = b * G + g
                    pe.wait_ge(s_norm, n + 1)
                    if not (isinstance(b, int) and n == 0):
                        pe.wait_ge(s_pt, n)
                    for c in range(2):
                        last = pe.transpose(ptp[:, c * P:(c + 1) * P], pr[:, g, c * P:(c + 1) * P], ident)
                    last.then_inc(s_ptp, 1)

                def attend(b, t, j, g):
                    n = b * G + g
                    pe.wait_ge(s_pt, n + 1)
                    if g == 0:
                        pe.wait_ge(s_vev, b * 2 + 2)
                        if not (isinstance(b, int) and b == 0):
                            pe.wait_ge(s_osum, b)
                    for c in range(2):
                        for h in range(4):
                            cols = slice(h * HD, h * HD + HD)
                            last = pe.matmul(av[cols, g * S:(g + 1) * S],
                                             v[j % 2][:, c, g * P + h * HD:g * P + h * HD + HD],
                                             pt[g % 2][:, c * P + h * S:c * P + h * S + S], start=(c == 0), stop=(c == 1))
                    last.then_inc(s_av, 1)

                def last_spread(b):
                    pe.wait_ge(s_pdiag, b + 1)
                    pe.matmul(plast, const[:, C_SAME:C_SAME + P], pdiag[:].rearrange("p g q -> p (g q)"),
                              start=True, stop=True).then_inc(s_last, 1)

                def self_product(u):
                    if u == 0:
                        pe.wait_ge(s_xtlo, TILES + 1)
                    pe.wait_ge(s_wlo, AQ + u)
                    if u == 0:
                        pe.wait_ge(s_kev, B * 4)
                    else:
                        pe.wait_ge(s_vev, B * 2 - 2 + u)
                    w = SLOT[AQ + u]
                    mm3(pe, bank[u][:], lambda c: xthi[:, c, :], lambda c: xtlo[:, c, :],
                        lambda c: whi[w][:, c, :], lambda c: wlo[w][:, c, :]).then_inc((s_qp, s_kp, s_vp)[u], 1)

                def out_product(t):
                    pe.wait_ge(s_olo, t * BT + BT)
                    if isinstance(t, int) and t == TILES - 1:
                        pe.wait_ge(s_xtlo, TILES + 1)
                    else:
                        pe.wait_ge(s_qt, t + 2)
                    pe.wait_ge(s_wlo, WO)
                    mm3(pe, extra, lambda c: othi[:, c, :], lambda c: otlo[:, c, :],
                        lambda c: whi[WO][:, c, :], lambda c: wlo[WO][:, c, :]).then_inc(s_wo, 1)

                for m in range(4):
                    k_product(0, 0, m)
                pe.wait_ge(s_const, 16)
                xn_transposed(0)
                pe.wait_ge(s_wlo, WQ)
                q_product(0)
                pe.wait_ge(s_wlo, WV)
                pe.wait_ge(s_cllo, 1)
                for g in range(G):
                    last = mm3(pe, ptp[:, g * B:(g + 1) * B],
                               lambda c: whi[WV][:, c, g * P:(g + 1) * P], lambda c: wlo[WV][:, c, g * P:(g + 1) * P],
                               lambda c: chi[1][:, c, 0:B], lambda c: clo[1][:, c, 0:B])
                last.then_inc(s_vl, 1)
                v_product(0, 0, 0, 0)
                v_product(0, 0, 0, 1)
                q_transposed(0)
                v_product(0, 0, 1, 0)
                v_product(0, 0, 1, 1)
                pe.wait_ge(s_vlsb, 1)

                def body(t, first=False, last=False):
                    for j in range(BT):
                        b = t * BT + j
                        more = not (last and j == BT - 1)
                        if more:
                            k_product(b + 1, j + 1, 0)
                        scores(b, j, 0)
                        if not (first and j == 0):
                            last_spread(b - 1)
                        if j == 1:
                            xn_transposed(t + 1)
                        if j == 3 and not last:
                            q_transposed(t + 1)
                        if more:
                            k_product(b + 1, j + 1, 1)
                        scores(b, j, 1)
                        if more:
                            k_product(b + 1, j + 1, 2)
                        else:
                            self_product(0)
                        probs_transposed(b, 0)
                        if j == 0 and not first:
                            out_product(t - 1)
                        scores(b, j, 2)
                        if more:
                            k_product(b + 1, j + 1, 3)
                        probs_transposed(b, 1)
                        scores(b, j, 3)
                        if more:
                            v_product(b + 1, j + 1, 0, 0)
                        else:
                            self_product(1)
                        attend(b, t, j, 0)
                        if more:
                            v_product(b + 1, j + 1, 0, 1)
                        probs_transposed(b, 2)
                        attend(b, t, j, 1)
                        if more:
                            v_product(b + 1, j + 1, 1, 0)
                        else:
                            self_product(2)
                        probs_transposed(b, 3)
                        attend(b, t, j, 2)
                        if more:
                            v_product(b + 1, j + 1, 1, 1)
                        if j == 1 and not last:
                            q_product(t + 1)
                        attend(b, t, j, 3)

                body(0, first=True)
                with pe.Fori(1, TILES - 1) as t:
                    body(t)
                body(TILES - 1, last=True)
                last_spread(B - 1)
                out_product(TILES - 1)

        with ExitStack() as ph:
            def sb(name, shape, dt=F32):
                return sbuf(ph, name, shape, dt)

            bias = [craw[r // 2][:].rearrange("p c n -> p (c n)")[:, r % 2 * D:(r % 2 + 1) * D] for r in range(4)]
            qkv = [sb(f"{n}_self", [P, D]) for n in "qkv"]
            qt = sb("qt2", [P, H, S])
            kt = sb("kt2", [P, H, S])
            kbd = sb("kbd", [P, H, P])
            pbd = sb("pbd", [P, H, P])
            sm = sb("sm2", [P, G * BT, S])
            smax = sb("smax2", [P, G * BT])
            ssum = sb("ssum2", [P, G * BT])
            sinv = sb("sinv2", [P, G * BT])
            othi = sb("othi2", [P, G, P], F32R)
            otlo = sb("otlo2", [P, G, P], F32R)
            stats3 = sb("stats3", [P, 6])
            mv3 = sb("mv3", [P, 2])
            vareps3 = sb("vareps3", [P, 1])
            rstd3 = sb("rstd3", [P, 1])
            xn3 = sb("xn3", [P, D])
            x3hi = sb("x3hi", [P, KC, B * S], F32R)
            x3lo = sb("x3lo", [P, KC, B * S], F32R)
            gate_w = sb("gate_w", [P, KC, NE])
            x3t = sb("x3t", [P, KC, P])
            gate_b = sb("gate_b", [P, NE])
            expert_b = sb("expert_b", [NE, D])
            iota = sb("iota", [P, NE])
            logits = sb("logits", [P, TILES, NE])
            top8 = sb("top8", [P, TILES, 8])
            idx8 = sb("idx8", [P, TILES, 8], U32)
            idxf = sb("idxf", [P, TILES, 2])
            gap = sb("gap", [P, TILES])
            gexp = sb("gexp", [P, TILES])
            gden = sb("gden", [P, TILES])
            gtop = sb("gtop", [P, 2, TILES])
            pick = sb("pick", [P, 2, TILES, NE])
            gates = sb("gates", [P, TILES, NE])
            gt = sb("gt", [NE, TILES, P])

            (s_gw, s_gb, s_eb, s_qsb, s_ksb, s_vsb,
             s_qt, s_kt, s_kbd, s_sc, s_causal, s_max, s_msub, s_exp, s_sum, s_sinv, s_norm, s_ptp, s_pbd, s_av, s_ohi,
             s_olo, s_cp, s_xpb, s_xo) = (sem(n) for n in (
                 "gate_w_in", "gate_b_in", "expert_b_in", "self_q_in_sbuf", "self_k_in_sbuf",
                 "self_v_in_sbuf", "self_q_by_batch_d", "self_k_by_batch_d", "self_k_blocks_done", "self_scores_done",
                 "self_scores_masked", "self_max_done", "self_less_max", "self_exp_done", "self_sum_done",
                 "self_sum_inverted", "self_probs_normed", "self_probs_t_done", "self_probs_blocks_done",
                 "self_attn_done",
                 "self_attn_hi_done", "self_attn_lo_done", "self_out_proj_done", "self_x_with_bias",
                 "self_x_with_out_proj"))
            (s_stats3, s_mv3, s_var3, s_rstd3, s_xn3, s_iota, s_x3t, s_ntp, s_x3hi, s_x3lo, s_lgp, s_lg, s_top,
             s_idx, s_gst, s_gexp, s_gates, s_gtp, s_gt, s_mm, s_acc, s_out) = (sem(n) for n in (
                 "ffn_ln_stats_done", "ffn_ln_mv_done", "ffn_ln_var_done", "ffn_ln_rstd_done", "ffn_ln_xn_done",
                 "iota_done", "ffn_xn_t_in_sbuf", "ffn_xn_t_done", "ffn_xn_t_hi_done",
                 "ffn_xn_t_lo_done", "logits_done", "logits_in_sbuf", "top_found", "top_index_found",
                 "gate_steps", "gate_exp_done", "gates_done", "gates_t_done", "gates_t_in_sbuf", "expert_products",
                 "expert_outputs_added", "out_stored"))

            causal = const[:, C_CAUSAL:C_CAUSAL + S].unsqueeze(1).to_broadcast([P, G * BT, S])

            def over_k(a):
                return a.unsqueeze(2).to_broadcast([P, G * BT, S])

            def first(t):
                return isinstance(t, int) and t == 0

            ring = [bank[i][:] for i in range(4)] + [quad[:, i, :] for i in range(4)]
            b_q, b_k, b_v, b_xt, b_score, b_av, b_cp, b_x3 = ring
            block = ph.enter_context(nc.Block())

            @block.sync
            def _(sp):
                sp.dma_start(gate_w[:], gate_w_in).then_inc(s_gw, 16)
                sp.dma_start(gate_b[:], gate_b_in.unsqueeze(0).partition_broadcast(P)).then_inc(s_gb, 16)
                sp.dma_start(expert_b[:], expert_b_in).then_inc(s_eb, 16)

                def weight(n, slot):
                    sp.wait_ge(s_wlo, n - 2)
                    sp.dma_start(wraw[slot][:], w_in[n]).then_inc(s_wraw[slot], 16)

                with sp.Fori(0, NE // 2) as i:
                    for s in range(2):
                        weight(E0 + i * 2 + s, s)
                for t in range(TILES):
                    sp.wait_ge(s_acc, TILES * NE + t + 1)
                    sp.dma_start(out[t * P:(t + 1) * P, :], x[:, t, :]).then_inc(s_out, 16)
                sp.wait_ge(s_out, 16 * TILES)

            @block.gpsimd
            def _(pool):
                pool.iota(iota[:], [[1, NE]], base=0, channel_multiplier=0,
                          allow_small_or_imprecise_dtypes=True).then_inc(s_iota, 1)

                def less_max(t):
                    pool.wait_ge(s_max, t + 1)
                    pool.tensor_tensor(sm[:], sm[:], over_k(smax[:]), ALU.subtract).then_inc(s_msub, 1)

                def norm(t):
                    pool.wait_ge(s_sinv, t + 1)
                    pool.tensor_tensor(sm[:], sm[:], over_k(sinv[:]), ALU.mult).then_inc(s_norm, 1)

                def ffn_ln(t):
                    pool.wait_ge(s_var3, t + 1)
                    pool.tensor_tensor(rstd3[:], vareps3[:], neghalf[:], ALU.pow).then_inc(s_rstd3, 1)

                def proj_bias(t):
                    pool.wait_ge(s_xn, TILES + t + 1)
                    pool.tensor_tensor(x[:, t, :], x[:, t, :], bias[R_AP - R_AQ], ALU.add).then_inc(s_xpb, 1)

                def body(t, depth=2, last=False):
                    if depth >= 1:
                        norm(t - 1)
                    if depth >= 2:
                        ffn_ln(t - 2)
                    if depth >= 1 and not last:
                        ln_pool(pool, TILES + t + 1)
                    proj_bias(t)
                    less_max(t)

                pool.wait_ge(s_whi, AP_)
                pool.wait_ge(s_wlo, AP_ - 1)
                pool.tensor_tensor(wlo[SLOT[AP_]][:], wraw[AP_ % 2][:], whi[SLOT[AP_]][:].bitcast(F32),
                                   ALU.subtract).then_inc(s_wlo, 1)
                pool.wait_ge(s_bias2, 32)
                body(0, depth=0)
                body(1, depth=1)
                with pool.Fori(2, TILES - 1) as t:
                    body(t)
                body(TILES - 1, last=True)
                norm(TILES - 1)
                ffn_ln(TILES - 2)
                ffn_ln(TILES - 1)

            @block.scalar
            def _(act):
                def w_hi(n, slot, raw, uses):
                    act.wait_ge(s_wraw[raw], uses)
                    act.activation(whi[slot][:], wraw[raw][:], ACT.Copy).then_inc(s_whi, 1)

                def xt_hi(t):
                    act.wait_ge(s_xtp, TILES + t + 1)
                    act.wait_ge(s_vp, t)
                    act.activation(xthi[:], b_xt.rearrange("p (c n) -> p c n", c=KC), ACT.Copy).then_inc(s_xthi, 1)

                def blocks(dst, src):
                    for b in range(BT):
                        last = act.activation(dst[:].rearrange("p h (b n) -> p h b n", b=BT)[:, :, b, :], src, ACT.Copy,
                                              scale=const[:, C_HMS + b:C_HMS + b + 1])
                    return last

                def k_blocks(t):
                    act.wait_ge(s_kt, t + 1)
                    if not first(t):
                        act.wait_ge(s_sc, t)
                    blocks(kbd, kt[:]).then_inc(s_kbd, 1)

                def p_blocks(t):
                    act.wait_ge(s_ptp, t + 1)
                    if not first(t):
                        act.wait_ge(s_av, t)
                    blocks(pbd, b_xt.rearrange("p (h q) -> p h q", h=H)).then_inc(s_pbd, 1)

                def exp(t):
                    act.wait_ge(s_msub, t + 1)
                    act.activation(sm[:], sm[:], ACT.Exp, scale=A_SCALE).then_inc(s_exp, 1)

                def o_hi(t):
                    act.wait_ge(s_av, t + 1)
                    if not first(t):
                        act.wait_ge(s_cp, t)
                    act.activation(othi[:], b_av.rearrange("p (g n) -> p g n", g=G), ACT.Copy).then_inc(s_ohi, 1)

                def x3_hi(t):
                    act.wait_ge(s_ntp, t + 1)
                    if not first(t):
                        act.wait_ge(s_lgp, t)
                    act.activation(x3t[:], b_x3.rearrange("p (c n) -> p c n", c=KC), ACT.Copy).then_inc(s_x3t, 1)
                    cols = bass.ds(t * P, P)
                    act.activation(x3hi[:, :, cols], b_x3.rearrange("p (c n) -> p c n", c=KC),
                                   ACT.Copy).then_inc(s_x3hi, 1)

                w_hi(AP_, SLOT[AP_], 1, raw_count(AP_))

                def body(t, depth=2, last=False):
                    if depth >= 1:
                        exp(t - 1)
                        p_blocks(t - 1)
                    if depth == 0:
                        xt_hi(t + 1)
                    k_blocks(t)
                    if depth >= 1:
                        o_hi(t - 1)
                    if depth >= 1 and not last:
                        xt_hi(t + 1)
                    if depth >= 2:
                        x3_hi(t - 2)

                body(0, depth=0)
                body(1, depth=1)
                with act.Fori(2, TILES - 1) as t:
                    body(t)
                body(TILES - 1, last=True)
                exp(TILES - 1)
                p_blocks(TILES - 1)
                w_hi(E0, 0, 0, raw_count(E0))
                o_hi(TILES - 1)
                x3_hi(TILES - 2)
                w_hi(E0 + 1, 1, 1, raw_count(E0 + 1))
                x3_hi(TILES - 1)

                act.wait_ge(s_gst, 1)
                act.activation(gexp[:], gap[:], ACT.Exp).then_inc(s_gexp, 1)
                for t in range(TILES):
                    act.wait_ge(s_gtp, t + 1)
                    act.activation(gt[:, t, :], ring[t][0:NE, 0:P], ACT.Copy).then_inc(s_gt, 1)

                def pair(i):
                    for s in range(2):
                        act.wait_ge(s_mm, (i * 2 + s + 2) * TILES)
                        w_hi(E0 + i * 2 + 2 + s, s, s, i * 16 + raw_count(E0 + 2 + s))

                with act.Fori(0, NE // 2 - 1) as i:
                    pair(i)

            @block.vector
            def _(dve):
                def w_lo(n, slot, raw):
                    dve.wait_ge(s_whi, n)
                    dve.tensor_tensor(wlo[slot][:], wraw[raw][:], whi[slot][:].bitcast(F32),
                                      ALU.subtract).then_inc(s_wlo, 1)

                def ln_apply(t):
                    dve.wait_ge(s_rstd, TILES + t + 1)
                    dve.wait_ge(s_xtp, TILES + t)
                    dve.tensor_scalar(xn[:], x[:, t, :], mv[:, 0:1], rstd[:, 0:1], ALU.subtract,
                                      ALU.mult).then_inc(s_xn, 1)

                def ffn_ln_stats(t):
                    dve.wait_ge(s_xo, t + 1)
                    dve.memset(tick[:, 0:1], 0.0)
                    dve.bn_stats(stats3[:], x[:, t, :]).then_inc(s_stats3, 1)
                    dve.wait_ge(s_stats3, t + 1)
                    dve.memset(tick[:, 1:2], 0.0)
                    dve.bn_aggr(mv3[:], stats3[:]).then_inc(s_mv3, 1)
                    dve.wait_ge(s_mv3, t + 1)
                    dve.tensor_scalar(vareps3[:], mv3[:, 1:2], EPS, None, ALU.add).then_inc(s_var3, 1)

                def ffn_ln_apply(t):
                    dve.wait_ge(s_rstd3, t + 1)
                    if not first(t):
                        dve.wait_ge(s_ntp, t)
                    dve.tensor_scalar(xn3[:], x[:, t, :], mv3[:, 0:1], rstd3[:, 0:1], ALU.subtract,
                                      ALU.mult).then_inc(s_xn3, 1)

                def xt_lo(t):
                    dve.wait_ge(s_xthi, TILES + t + 1)
                    dve.tensor_tensor(xtlo[:], b_xt.rearrange("p (c n) -> p c n", c=KC), xthi[:].bitcast(F32),
                                      ALU.subtract).then_inc(s_xtlo, 1)

                def evac(t, u):
                    dve.wait_ge((s_qp, s_kp, s_vp)[u], t + 1)
                    if not first(t):
                        dve.wait_ge((s_qt, s_kt, s_av)[u], t)
                    dve.tensor_tensor(qkv[u][:], (b_q, b_k, b_v)[u], bias[u],
                                      ALU.add).then_inc((s_qsb, s_ksb, s_vsb)[u], 1)

                def q_by_batch(t):
                    dve.wait_ge(s_qsb, t + 1)
                    if not first(t):
                        dve.wait_ge(s_sc, t)
                    dve.transpose(qt[:].rearrange("p h q -> p (h q)"), qkv[0][:]).then_inc(s_qt, 1)

                def k_by_batch(t):
                    dve.wait_ge(s_ksb, t + 1)
                    if not first(t):
                        dve.wait_ge(s_kbd, t)
                    dve.transpose(kt[:].rearrange("p h k -> p (h k)"), qkv[1][:]).then_inc(s_kt, 1)

                def mask_and_max(t):
                    dve.wait_ge(s_sc, t + 1)
                    if not first(t):
                        dve.wait_ge(s_ptp, t)
                    dve.tensor_tensor(sm[:], b_score.rearrange("p (a k) -> p a k", k=S), causal,
                                      ALU.add).then_inc(s_causal, 1)
                    dve.wait_ge(s_causal, t + 1)
                    dve.tensor_reduce(smax[:], sm[:], AX.X, ALU.max).then_inc(s_max, 1)

                def inverse_sum(t):
                    dve.wait_ge(s_exp, t + 1)
                    dve.tensor_reduce(ssum[:], sm[:], AX.X, ALU.add).then_inc(s_sum, 1)
                    dve.wait_ge(s_sum, t + 1)
                    dve.reciprocal(sinv[:], ssum[:]).then_inc(s_sinv, 1)

                def o_lo(t):
                    dve.wait_ge(s_ohi, t + 1)
                    dve.tensor_tensor(otlo[:], b_av.rearrange("p (g n) -> p g n", g=G), othi[:].bitcast(F32),
                                      ALU.subtract).then_inc(s_olo, 1)

                def add_out(t):
                    dve.wait_ge(s_cp, t + 1)
                    dve.wait_ge(s_xpb, t + 1)
                    dve.tensor_tensor(x[:, t, :], b_cp, x[:, t, :], ALU.add).then_inc(s_xo, 1)

                def x3_lo(t):
                    dve.wait_ge(s_x3hi, t + 1)
                    cols = bass.ds(t * P, P)
                    dve.tensor_tensor(x3lo[:, :, cols], b_x3.rearrange("p (c n) -> p c n", c=KC),
                                      x3hi[:, :, cols].bitcast(F32), ALU.subtract).then_inc(s_x3lo, 1)

                def logits_evac(t):
                    dve.wait_ge(s_lgp, t + 1)
                    dve.tensor_tensor(logits[:, t, :], b_x3[:, 0:NE], gate_b[:], ALU.add).then_inc(s_lg, 1)

                dve.wait_ge(s_bias2, 32)
                dve.wait_ge(s_gb, 16)

                def body(t, depth=2, last=False):
                    if depth >= 2:
                        add_out(t - 2)
                    if depth >= 1:
                        inverse_sum(t - 1)
                    if depth >= 2:
                        ffn_ln_stats(t - 2)
                    if depth >= 3:
                        logits_evac(t - 3)
                    evac(t, 0)
                    q_by_batch(t)
                    if depth >= 2:
                        ffn_ln_apply(t - 2)
                    if depth >= 1 and not last:
                        ln_dve_stats(dve, TILES + t + 1, x[:, t + 1, :])
                    evac(t, 1)
                    k_by_batch(t)
                    if depth >= 1 and not last:
                        ln_apply(t + 1)
                    evac(t, 2)
                    if depth >= 1:
                        o_lo(t - 1)
                    if depth == 0:
                        xt_lo(t + 1)
                    mask_and_max(t)
                    if depth >= 1 and not last:
                        xt_lo(t + 1)
                    if depth >= 2:
                        x3_lo(t - 2)

                body(0, depth=0)
                body(1, depth=1)
                body(2, depth=2)
                with dve.Fori(3, TILES - 1) as t:
                    body(t, depth=3)
                body(TILES - 1, depth=3, last=True)
                T = TILES - 1
                inverse_sum(T)
                add_out(T - 1)
                ffn_ln_stats(T - 1)
                logits_evac(T - 2)
                ffn_ln_apply(T - 1)
                w_lo(E0, 0, 0)
                o_lo(T)
                x3_lo(T - 1)
                logits_evac(T - 1)
                add_out(T)
                ffn_ln_stats(T)
                ffn_ln_apply(T)
                w_lo(E0 + 1, 1, 1)
                x3_lo(T)
                logits_evac(T)

                dve.wait_ge(s_lg, TILES)
                for t in range(TILES):
                    dve.max(top8[:, t, :], logits[:, t, :]).then_inc(s_top, 1)
                dve.wait_ge(s_top, TILES)
                dve.tensor_tensor(gap[:], top8[:, :, 1], top8[:, :, 0], ALU.subtract).then_inc(s_gst, 1)
                for t in range(TILES):
                    dve.max_index(idx8[:, t, :], top8[:, t, :], logits[:, t, :]).then_inc(s_idx, 1)
                dve.wait_ge(s_idx, TILES)
                dve.tensor_copy(idxf[:], idx8[:, :, 0:2]).then_inc(s_gst, 1)
                dve.wait_ge(s_gexp, 1)
                dve.tensor_scalar(gden[:], gexp[:], 1.0, None, ALU.add).then_inc(s_gst, 1)
                dve.wait_ge(s_gst, 3)
                dve.reciprocal(gtop[:, 0, :], gden[:]).then_inc(s_gst, 1)
                dve.wait_ge(s_gst, 4)
                dve.tensor_tensor(gtop[:, 1, :], gexp[:], gtop[:, 0, :], ALU.mult).then_inc(s_gst, 1)
                dve.wait_ge(s_iota, 1)
                over_t = [P, TILES, NE]
                for k in range(2):
                    dve.tensor_tensor(pick[:, k, :, :], iota[:].unsqueeze(1).to_broadcast(over_t),
                                      idxf[:, :, k].unsqueeze(2).to_broadcast(over_t), ALU.is_equal).then_inc(s_gst, 1)
                dve.wait_ge(s_gst, 7)
                for k in range(2):
                    dve.tensor_tensor(pick[:, k, :, :], pick[:, k, :, :],
                                      gtop[:, k, :].unsqueeze(2).to_broadcast(over_t), ALU.mult).then_inc(s_gst, 1)
                dve.wait_ge(s_gst, 9)
                dve.tensor_tensor(gates[:], pick[:, 0, :, :], pick[:, 1, :, :], ALU.add).then_inc(s_gates, 1)
                dve.wait_ge(s_gates, 1)

                for t in range(TILES):
                    dve.wait_ge(s_mm, t + 1)
                    dve.tensor_tensor(x[:, t, :], ring[t], x[:, t, :], ALU.add).then_inc(s_acc, 1)

                def add_expert(e, t):
                    dve.wait_ge(s_mm, e * TILES + TILES + t + 1)
                    dve.wait_ge(s_acc, e * TILES + t + 1)
                    dve.scalar_tensor_tensor(x[:, t, :], ring[t], gates[:, t, bass.ds(e, 1)], x[:, t, :], ALU.mult,
                                             ALU.add).then_inc(s_acc, 1)

                def pair(i, last=False):
                    for s in range(2):
                        for t in range(TILES):
                            add_expert(i * 2 + s, t)
                        if not last:
                            w_lo(E0 + i * 2 + 2 + s, s, s)

                with dve.Fori(0, NE // 2 - 1) as i:
                    pair(i)
                pair(NE // 2 - 1, last=True)

            @block.tensor
            def _(pe):
                def four_transposes(dst, src):
                    for c in range(KC):
                        last = pe.transpose(dst[:, c * P:(c + 1) * P], src[:, c * P:(c + 1) * P], ident)
                    return last

                def xn_transposed(t):
                    pe.wait_ge(s_xn, TILES + t + 1)
                    if not (isinstance(t, int) and t <= 1):
                        pe.wait_ge(s_pbd, t - 1)
                    four_transposes(b_xt, xn).then_inc(s_xtp, 1)

                def qkv_product(t, u):
                    if u == 0:
                        pe.wait_ge(s_xtlo, TILES + t + 1)
                    pe.wait_ge((s_qsb, s_ksb, s_vsb)[u], t)
                    w = SLOT[AQ + u]
                    mm3(pe, (b_q, b_k, b_v)[u], lambda c: xthi[:, c, :], lambda c: xtlo[:, c, :],
                        lambda c: whi[w][:, c, :], lambda c: wlo[w][:, c, :]).then_inc((s_qp, s_kp, s_vp)[u], 1)

                def scores(t):
                    pe.wait_ge(s_kbd, t + 1)
                    pe.wait_ge(s_qt, t + 1)
                    if not first(t):
                        pe.wait_ge(s_causal, t)
                    for h in range(H):
                        rows, cols = slice(h % 4 * S, h % 4 * S + S), slice(h // 4 * P, h // 4 * P + P)
                        last = pe.matmul(b_score[rows, cols], qt[:, h, :], kbd[:, h, :], start=True, stop=True)
                    last.then_inc(s_sc, 1)

                def probs_transposed(t):
                    pe.wait_ge(s_norm, t + 1)
                    four_transposes(b_xt, sm[:].rearrange("p a k -> p (a k)")).then_inc(s_ptp, 1)

                def attend(t):
                    pe.wait_ge(s_pbd, t + 1)
                    pe.wait_ge(s_vsb, t + 1)
                    if not first(t):
                        pe.wait_ge(s_olo, t)
                    for h in range(H):
                        rows, cols = slice(h % 4 * HD, h % 4 * HD + HD), slice(h // 4 * P, h // 4 * P + P)
                        last = pe.matmul(b_av[rows, cols], qkv[2][:, h * HD:(h + 1) * HD], pbd[:, h, :],
                                         start=True, stop=True)
                    last.then_inc(s_av, 1)

                def out_product(t):
                    pe.wait_ge(s_olo, t + 1)
                    if first(t):
                        pe.wait_ge(s_wlo, AP_)
                    else:
                        pe.wait_ge(s_xo, t)
                    mm3(pe, b_cp, lambda c: othi[:, c, :], lambda c: otlo[:, c, :],
                        lambda c: whi[3][:, c, :], lambda c: wlo[3][:, c, :]).then_inc(s_cp, 1)

                def x3_transposed(t):
                    pe.wait_ge(s_xn3, t + 1)
                    if not first(t):
                        pe.wait_ge(s_lg, t)
                    four_transposes(b_x3, xn3).then_inc(s_ntp, 1)

                def gate_logits(t):
                    pe.wait_ge(s_x3t, t + 1)
                    pe.wait_ge(s_x3lo, t + 1)
                    if first(t):
                        pe.wait_ge(s_gw, 16)
                    for c in range(KC):
                        last = pe.matmul(b_x3[:, 0:NE], x3t[:, c, :], gate_w[:, c, :], start=(c == 0),
                                         stop=(c == KC - 1))
                    last.then_inc(s_lgp, 1)

                def body(t, depth=2, last=False):
                    qkv_product(t, 0)
                    if depth >= 2:
                        probs_transposed(t - 1)
                    qkv_product(t, 1)
                    if depth == 1:
                        scores(t - 1)
                    qkv_product(t, 2)
                    if depth == 1:
                        probs_transposed(t - 1)
                    attend(t - 1)
                    scores(t)
                    if not last:
                        xn_transposed(t + 1)
                    if depth >= 2:
                        x3_transposed(t - 2)
                    out_product(t - 1)
                    if depth >= 2:
                        gate_logits(t - 2)

                xn_transposed(1)
                body(1, depth=1)
                body(2, depth=2)
                with pe.Fori(3, TILES - 1) as t:
                    body(t)
                body(TILES - 1, last=True)
                T = TILES - 1
                probs_transposed(T)
                x3_transposed(T - 1)
                attend(T)
                out_product(T)
                gate_logits(T - 1)
                x3_transposed(T)
                gate_logits(T)

                pe.wait_ge(s_lg, TILES)
                pe.wait_ge(s_gates, 1)
                for t in range(TILES):
                    pe.transpose(ring[t][0:NE, 0:P], gates[:, t, :], ident).then_inc(s_gtp, 1)
                pe.wait_ge(s_eb, 16)
                for t in range(TILES):
                    pe.wait_ge(s_gt, t + 1)
                    pe.matmul(ring[t], gt[:, t, :], expert_b[:], start=True, stop=True).then_inc(s_mm, 1)

                def pair(i):
                    for s in range(2):
                        pe.wait_ge(s_wlo, i * 2 + E0 + s)
                        for t in range(TILES):
                            pe.wait_ge(s_acc, (i * 2 + s) * TILES + t + 1)
                            cols = slice(t * P, (t + 1) * P)
                            mm3(pe, ring[t], lambda c: x3hi[:, c, cols], lambda c: x3lo[:, c, cols],
                                lambda c: whi[s][:, c, :], lambda c: wlo[s][:, c, :]).then_inc(s_mm, 1)

                with pe.Fori(0, NE // 2) as i:
                    pair(i)


def kernel(**inputs):
    import numpy as _np
    import concourse.bacc as _bacc
    from concourse import mybir as _mybir
    from concourse.bass_utils import run_bass_kernel_spmd as _run

    a = {k: _np.asarray(v) for k, v in inputs.items()}

    def chunks(w):
        return w.reshape(KC, P, -1).transpose(1, 0, 2)

    def even_odd(w):
        return w.reshape(-1, H, HD // 2, 2).transpose(0, 3, 1, 2).reshape(w.shape)

    wkv, bkv = a["L0_xattn_Wkv"], a["L0_xattn_bkv"]
    wa, ba = a["L0_attn_c_attn_kernel"], a["L0_attn_c_attn_bias"]
    mats = [even_odd(wkv[:, :D]), even_odd(a["L0_xattn_Wq"]), wkv[:, D:], a["L0_xattn_Wo"],
            wa[:D].T, wa[D:2 * D].T, wa[2 * D:].T, a["L0_attn_c_proj_kernel"].T, *a["L0_ffn_expert_w"]]
    ctx = a["ctx_1024"]
    ctx_t = _np.zeros((B, P, KC, LKP), _np.float32)
    ctx_t[:, :, :, :LK] = ctx.reshape(B, LK, KC, P).transpose(0, 3, 2, 1)
    ctx_last = ctx[:, LK - 1, :].reshape(B, KC, P).transpose(2, 1, 0)
    arrays = {
        "x": a["x"].reshape(B * S, D),
        "ctx_t": ctx_t,
        "ctx_last": ctx_last,
        "mask": a["mask_BxS2_bf1"].view(_np.uint8),
        "weights": _np.stack([chunks(m) for m in mats]),
        "biases": _np.stack([even_odd(a["L0_xattn_bq"][None])[0], bkv[D:], a["L0_xattn_bo"], ba[:D], ba[D:2 * D],
                             ba[2 * D:], a["L0_attn_c_proj_bias"]]),
        "bias_cols": _np.concatenate([even_odd(bkv[None, :D])[0].reshape(4, P).T, bkv[D:].reshape(G, P).T], 1),
        "gate_w": chunks(a["L0_ffn_gate_w"].T),
        "gate_b": a["L0_ffn_gate_b"],
        "expert_b": a["L0_ffn_expert_b"],
        "constants": constants(),
    }
    arrays = {f"{k}_dram": _np.ascontiguousarray(v) for k, v in arrays.items()}
    nc = _bacc.Bacc("TRN2", target_bir_lowering=False, num_devices=1)
    args = [nc.dram_tensor(k, v.shape, _mybir.dt.from_np(v.dtype), kind="ExternalInput").ap() for k, v in arrays.items()]
    out = nc.dram_tensor("out_dram", [B * S, D], _mybir.dt.float32, kind="ExternalOutput").ap()
    perceiver(nc, *args, out)
    r = _run(nc, [arrays], core_ids=[0])
    return r.results[0]["out_dram"].reshape(B, S, D)
```

```python
from contextlib import ExitStack

import numpy as np
import concourse.bass as bass
from concourse import mybir

F32 = mybir.dt.float32
F32R = mybir.dt.float32r
U8 = mybir.dt.uint8
U32 = mybir.dt.uint32
I32 = mybir.dt.int32
ALU = mybir.AluOpType
ACT = mybir.ActivationFunctionType
AX = mybir.AxisListType

P = 128
B, S, D, LK = 32, 32, 512, 257
H, HD = 16, 32
KC = D // P
G = H // 4
TILES = B * S // P
BT = P // S
NE = 8
LKP = LK + 1
EPS = 1e-5
X_SCALE = 64.0 ** -0.5
BLOW = 8.0
A_SCALE = float(np.float32(1.0) / np.sqrt(np.float32(HD)))
WK, WQ, WV, WO, AQ, AK, AV, AP_, E0 = range(9)
SLOT = (0, 1, 2, 3, 1, 0, 2, 3)
R_BQ, R_BV, R_BO, R_AQ, R_AK, R_AV, R_AP = range(7)

C_ID = 0
C_COSK = C_ID + P
C_SINK = C_COSK + LKP
C_COSQ = C_SINK + LKP
C_SINQ = C_COSQ + HD // 2
C_HMX = C_SINQ + HD // 2
C_HMS = C_HMX + 4
C_CAUSAL = C_HMS + 4
C_EYE = C_CAUSAL + S
C_SAME = C_EYE + S
C_ALL = C_SAME + P

SLOTS = 2 * B * S // P + NE - 1
AHEAD = 4
LAST_ROUND = (SLOTS - AHEAD + 1) // AHEAD
POOL_EXPERTS = range(2, 7)

R_BEFORE = 0
R_ONES = R_BEFORE + P
R_IOTA = R_ONES + P
R_TILE = R_IOTA + P
R_UPTO = R_TILE + NE
R_TOKEN = R_UPTO + NE * NE
R_SPARE = R_TOKEN + TILES
R_ALL = R_SPARE + 1


def route_constants():
    c = np.zeros((P, R_ALL), np.float32)
    row, col = np.arange(P)[:, None], np.arange(P)[None, :]
    c[:, R_BEFORE:R_BEFORE + P] = row < col
    c[:, R_ONES:R_ONES + P] = 1.0
    c[:, R_IOTA:R_IOTA + P] = col
    c[:, R_TILE:R_TILE + NE] = np.arange(NE) * P
    c[:, R_UPTO:R_UPTO + NE * NE] = (np.arange(NE)[None, :] <= np.arange(NE)[:, None]).reshape(1, -1)
    c[:, R_TOKEN:R_TOKEN + TILES] = np.arange(TILES)[None, :] * P + row + 1
    c[:, R_SPARE] = B * S + np.arange(P) + 1
    return c


def constants():
    inv = (1.0 / 10000.0 ** (np.arange(0, HD, 2, dtype=np.float32) / np.float32(HD))).astype(np.float32)

    def angles(n):
        pos = np.float32(10.0) * (np.arange(n, dtype=np.float32) / np.float32(n))
        return (pos[:, None] * inv).astype(np.float32).astype(np.float64)

    c = np.zeros((P, C_ALL), np.float32)
    row = np.arange(P)
    c[:, C_ID:C_ID + P] = np.eye(P)
    k = angles(LK)
    c[:, C_COSK:C_COSK + LK] = np.cos(k).T[row % 16]
    c[:, C_SINK:C_SINK + LK] = np.sin(k).T[row % 16]
    q = angles(S)
    c[:, C_COSQ:C_COSQ + 16] = np.cos(q).astype(np.float32)[row % S] * np.float32(X_SCALE / BLOW)
    c[:, C_SINQ:C_SINQ + 16] = np.sin(q).astype(np.float32)[row % S] * np.float32(X_SCALE / BLOW)
    c[:, C_HMX:C_HMX + 4] = (row % 64 // 16)[:, None] == np.arange(4)
    c[:, C_HMS:C_HMS + 4] = (row // 32)[:, None] == np.arange(4)
    c[:, C_CAUSAL:C_CAUSAL + S] = np.where(np.arange(S)[None, :] <= (row % S)[:, None], 0.0, np.finfo(np.float32).min)
    c[:, C_EYE:C_EYE + S] = (row % S)[:, None] == np.arange(S)
    c[:, C_SAME:C_SAME + P] = (row // S)[:, None] == (row // S)[None, :]
    return c


def perceiver(nc, x_in, ctx_in, ctx_last_in, mask_in, w_in, bias_in, bias_cols_in, gate_w_in, gate_b_in,
              expert_b_in, const_in, route_in, out):
    with ExitStack() as top:
        def sem(name):
            return top.enter_context(nc.semaphore(name))

        def sbuf(stack, name, shape, dt=F32):
            return stack.enter_context(nc.sbuf_tensor(name, shape, dt))

        const = sbuf(top, "const", [P, C_ALL])
        ident = const[:, C_ID:C_ID + P]
        x = sbuf(top, "x", [P, TILES, D])
        wparts = sbuf(top, "wparts", [P, 2 * 4, KC, D], F32R)
        whi = [wparts[:, i, :, :] for i in (0, 1, 2, 6)]
        wlo = [wparts[:, i, :, :] for i in (3, 4, 5, 7)]
        wraw = [sbuf(top, f"wraw{i}", [P, KC, D]) for i in range(2)]
        craw = [sbuf(top, f"craw{i}", [P, KC, LKP]) for i in range(2)]
        xthi = sbuf(top, "xthi", [P, KC, P], F32R)
        xtlo = sbuf(top, "xtlo", [P, KC, P], F32R)
        stats = sbuf(top, "stats", [P, 6])
        mv = sbuf(top, "mv", [P, 2])
        neghalf = sbuf(top, "neghalf", [P, 1])
        vareps = sbuf(top, "vareps", [P, 1])
        rstd = sbuf(top, "rstd", [P, 1])
        xn = sbuf(top, "xn", [P, D])
        tick = sbuf(top, "tick", [1, G + 1])

        bank = [top.enter_context(nc.psum_tensor(f"bank{i}", [P, 512], F32)) for i in range(4)]
        quad = top.enter_context(nc.psum_tensor("quad", [P, 4, 512], F32))

        s_const, s_x0, s_x, s_bias, s_maskin, s_clast, s_biask = (sem(n) for n in (
            "const_in", "x_first_tile_in", "x_in", "bias_in", "mask_in", "ctx_last_in", "bias_k_in"))
        s_wk = [sem(f"first_weight_chunk{c}_in") for c in range(KC)]
        s_wraw = [sem(f"weight_raw_in{i}") for i in range(2)]
        s_whi_chunk = sem("weight_hi_chunk_done")
        s_whi, s_wlo = sem("weight_hi_done"), sem("weight_lo_done")
        s_bias2 = sem("bias_self_in")
        s_stats, s_mv, s_var, s_rstd, s_xn, s_xtp, s_xthi, s_xtlo = (sem(n) for n in (
            "ln_stats_done", "ln_mv_done", "ln_var_done", "ln_rstd_done", "ln_xn_done", "xn_t_done", "xn_t_hi_done",
            "xn_t_lo_done"))
        s_qp, s_kp, s_vp = sem("self_q_done"), sem("self_k_done"), sem("self_v_done")

        def mm3(pe, psum, ahi, alo, bhi, blo, chunks=KC, before=None):
            for c in range(chunks):
                if before is not None:
                    before(c)
                pe.matmul(psum, ahi(c), bhi(c), start=(c == 0), stop=False)
                pe.matmul(psum, ahi(c), blo(c), start=False, stop=False)
                last = pe.matmul(psum, alo(c), bhi(c), start=False, stop=(c == chunks - 1))
            return last

        def raw_count(n):
            return 16 * (n // 2 + n % 2)

        def ln_dve_stats(dve, n, xt):
            dve.bn_stats(stats[:], xt).then_inc(s_stats, 1)
            dve.wait_ge(s_stats, n + 1)
            dve.memset(tick[:, G:G + 1], 0.0)
            dve.bn_aggr(mv[:], stats[:]).then_inc(s_mv, 1)
            dve.wait_ge(s_mv, n + 1)
            dve.tensor_scalar(vareps[:], mv[:, 1:2], EPS, None, ALU.add).then_inc(s_var, 1)

        def ln_pool(pool, n):
            pool.wait_ge(s_var, n + 1)
            pool.tensor_tensor(rstd[:], vareps[:], neghalf[:], ALU.pow).then_inc(s_rstd, 1)

        with ExitStack() as ph:
            def sb(name, shape, dt=F32):
                return sbuf(ph, name, shape, dt)

            maskb8 = sb("maskb8", [P, B, LK], U8)
            bias = sb("bias_cross", [P, R_AQ, D])
            bias_cols = sb("bias_cols", [P, 4 + G])
            chi = [sb(f"chi{i}", [P, KC, LKP], F32R) for i in range(2)]
            clo = [sb(f"clo{i}", [P, KC, LKP], F32R) for i in range(2)]
            kb = sb("kb", [P, 4, LKP])
            kcos = sb("kcos", [P, 4, LKP])
            ksin = sb("ksin", [P, 4, LKP])
            kr = [sb(f"kr{i}", [P, G, LKP]) for i in range(2)]
            v = [sb(f"v{i}", [P, 2, D]) for i in range(2)]
            mb = [sb(f"mb{i}", [P, LK]) for i in range(2)]
            qb = sb("qb", [P, D])
            qcos = sb("qcos", [P, D])
            qsin = sb("qsin", [P, D])
            qr = qb[:].rearrange("p (g n) -> p g n", g=G)
            qt = sb("qt", [P, G, P])
            qbd = [sb(f"qbd{i}", [P, G, P]) for i in range(2)]
            sm = [sb(f"sm{i}", [P, LK]) for i in range(2)]
            pr = sb("pr", [P, G, LKP])
            vlast = sb("vlast", [P, G, B])
            pdiag = sb("pdiag", [P, G, S])
            olast = sb("olast", [P, G, S])
            osum = sb("osum", [P, G, S])
            nmax = sb("nmax", [P, G])
            rsum = sb("rsum", [P, G])
            rinv = sb("rinv", [P, G])
            pt = [sb(f"pt{i}", [P, 2 * P]) for i in range(2)]
            othi = sb("othi", [P, G, P], F32R)
            otlo = sb("otlo", [P, G, P], F32R)

            proj = bank[0:3]
            score = [bank[3], quad[:, 0, :]]
            ptp = quad[:, 1, :]
            extra = quad[:, 2, :]
            av = quad[:, 3, 0:P]
            plast = quad[:, 3, P:2 * P]

            s_zero, s_wkhi, s_wklo = sem("zeroed"), sem("first_weight_hi_chunks"), sem("first_weight_lo_chunks")
            s_ctx = [sem(f"ctx_raw_in{i}") for i in range(2)]
            s_pdiag, s_last, s_olast, s_osum = (sem(n) for n in (
                "p_last_diagonal_done", "p_last_spread", "o_last_done", "o_sum_done"))
            (s_clhi, s_cllo, s_vl, s_vlsb, s_chi, s_clo, s_proj, s_kev, s_vev, s_kcos, s_ksin, s_kr, s_qbd,
             s_mb, s_sc, s_sm, s_exp, s_rinv, s_norm, s_ptp, s_pt, s_av, s_ohi, s_olo, s_wo, s_xwo, s_xb,
             s_qmm, s_qb, s_qcos, s_qr, s_qtp, s_qt) = (sem(n) for n in (
                 "ctx_last_hi_done", "ctx_last_lo_done", "v_last_done", "v_last_in_sbuf",
                 "ctx_hi_done", "ctx_lo_done", "proj_done", "k_evacuated", "v_evacuated", "k_cos_done", "k_sin_done",
                 "k_rotated", "q_blocks_done", "mask_bias_done", "scores_done", "scores_masked", "exp_done",
                 "rsum_inverted", "probs_normed", "probs_t_done", "probs_t_in_sbuf", "attn_done", "attn_hi_done",
                 "attn_lo_done", "out_proj_done", "x_with_out_proj", "x_with_bias",
                 "q_done", "q_in_sbuf", "q_trig_done", "q_rotated", "q_t_done", "q_t_in_sbuf"))

            cosk = const[:, C_COSK:C_COSK + LKP].unsqueeze(1).to_broadcast([P, 4, LKP])
            sink = const[:, C_SINK:C_SINK + LKP].unsqueeze(1).to_broadcast([P, 4, LKP])
            cosq = const[:, C_COSQ:C_COSQ + 16].unsqueeze(1).to_broadcast([P, 2 * H, 16])
            sinq = const[:, C_SINQ:C_SINQ + 16].unsqueeze(1).to_broadcast([P, 2 * H, 16])
            eye = const[:, C_EYE:C_EYE + S].unsqueeze(1).to_broadcast([P, G, S])
            hmx = const[:, C_HMX:C_HMX + 4].unsqueeze(1).unsqueeze(3).to_broadcast([P, G, 4, S])

            block = ph.enter_context(nc.Block())

            @block.sync
            def _(sp):
                def weight(n):
                    if n == WK + 2:
                        sp.wait_ge(s_wklo, KC)
                    elif n > WK + 2:
                        sp.wait_ge(s_wlo, n - 2)
                    sp.dma_start(wraw[n % 2][:], w_in[n]).then_inc(s_wraw[n % 2], 16)

                def ctx(b, j):
                    sp.dma_start(craw[j % 2][:], ctx_in[b]).then_inc(s_ctx[j % 2], 16)

                ctx(0, 0)
                for c in range(KC):
                    sp.dma_start(wraw[0][:, c, :], w_in[WK][:, c, :]).then_inc(s_wk[c], 16)
                sp.dma_start(x[:, 0, :], x_in[0:P, :]).then_inc(s_x0, 16)
                sp.dma_start(const[:], const_in).then_inc(s_const, 16)
                sp.dma_start(bias_cols[:], bias_cols_in).then_inc(s_biask, 16)
                weight(WQ)
                sp.dma_start(craw[1][:, :, 0:B], ctx_last_in).then_inc(s_clast, 16)
                weight(WV)
                sp.dma_start(bias[:], bias_in[0:R_AQ, :].partition_broadcast(P)).then_inc(s_bias, 16)
                sp.dma_start(maskb8[:], mask_in.partition_broadcast(P)).then_inc(s_maskin, 16)
                weight(WO)
                sp.wait_ge(s_cllo, 1)
                ctx(1, 1)
                for t in range(1, TILES):
                    sp.dma_start(x[:, t, :], x_in[t * P:(t + 1) * P, :]).then_inc(s_x, 16)

                def step(t, j, last):
                    b = t * BT + j
                    if not (last and j >= BT - 2):
                        sp.wait_ge(s_clo, b + 1)
                        ctx(b + 2, j)

                def body(t, last=False):
                    for j in range(BT):
                        step(t, j, last)

                body(0)
                weight(AQ)
                weight(AK)
                with sp.Fori(1, TILES - 1) as t:
                    body(t)
                body(TILES - 1, last=True)
                weight(AV)
                for i in range(2):
                    sp.wait_ge(s_clo, B - 1 + i)
                    rows = bias_in[R_AQ + 2 * i:R_AQ + 2 * i + 2, :].partition_broadcast(P)
                    sp.dma_start(craw[i][:].rearrange("p c n -> p (c n)")[:, 0:2 * D].rearrange("p (r n) -> p r n", r=2),
                                 rows).then_inc(s_bias2, 16)
                weight(AP_)

            @block.gpsimd
            def _(pool):
                pool.memset(neghalf[:], -0.5).then_inc(s_zero, 1)
                def k_sin(b):
                    pool.wait_ge(s_kev, (b + 1) * 4)
                    if not (isinstance(b, int) and b == 0):
                        pool.wait_ge(s_kr, b)
                    pool.tensor_tensor(ksin[:], kb[:], sink, ALU.mult).then_inc(s_ksin, 1)

                def p_last(b):
                    pool.wait_ge(s_norm, (b + 1) * G)
                    if not (isinstance(b, int) and b == 0):
                        pool.wait_ge(s_last, b)
                    pool.tensor_tensor(pdiag[:], pr[:, :, LK - 1].unsqueeze(2).to_broadcast([P, G, S]), eye,
                                       ALU.mult).then_inc(s_pdiag, 1)

                def q_blocks(b, t, j):
                    pool.wait_ge(s_qt, t + 1)
                    if not (isinstance(b, int) and b < 2):
                        pool.wait_ge(s_sc, (b - 1) * G)
                    q = qt[:, :, j * S:(j + 1) * S].unsqueeze(2).to_broadcast([P, G, 4, S])
                    pool.tensor_tensor(qbd[j % 2][:].rearrange("p g (h q) -> p g h q", h=4), q, hmx,
                                       ALU.mult).then_inc(s_qbd, 1)

                pool.wait_ge(s_const, 16)
                ln_pool(pool, 0)
                k_sin(0)
                q_blocks(0, 0, 0)

                def wo_lo():
                    pool.wait_ge(s_whi, WO)
                    pool.wait_ge(s_wlo, WO - 1)
                    pool.tensor_tensor(wlo[WO][:], wraw[WO % 2][:], whi[WO][:].bitcast(F32),
                                       ALU.subtract).then_inc(s_wlo, 1)

                def body(t, last=False):
                    for j in range(BT):
                        if not (last and j == BT - 1):
                            if j < BT - 1:
                                q_blocks(t * BT + j + 1, t, j + 1)
                            else:
                                q_blocks(t * BT + BT, t + 1, 0)
                            k_sin(t * BT + j + 1)
                        p_last(t * BT + j)
                        if j == 0:
                            ln_pool(pool, t + 1)
                        if j == 0 and isinstance(t, int) and t == 0:
                            wo_lo()

                body(0)
                with pool.Fori(1, TILES - 1) as t:
                    body(t)
                body(TILES - 1, last=True)
                ln_pool(pool, TILES + 1)

            @block.scalar
            def _(act):
                def w_hi(n):
                    act.wait_ge(s_wraw[n % 2], raw_count(n))
                    act.activation(whi[SLOT[n]][:], wraw[n % 2][:], ACT.Copy).then_inc(s_whi, 1)

                def ctx_hi_at(t, j2):
                    b = t * BT + j2
                    act.wait_ge(s_ctx[j2 % 2], (t * 2 + j2 // 2 + 1) * 16)
                    if not (isinstance(b, int) and b < 2):
                        act.wait_ge(s_proj, (b - 1) * 6)
                    act.activation(chi[j2 % 2][:], craw[j2 % 2][:], ACT.Copy).then_inc(s_chi, 1)

                def k_evac(b, m):
                    act.wait_ge(s_proj, b * 6 + m + 1)
                    if m == 0 and not (isinstance(b, int) and b == 0):
                        act.wait_ge(s_kcos, b)
                        act.wait_ge(s_ksin, b)
                    act.activation(kb[:, m, :], proj[m % 3][:, 0:LKP], ACT.Identity,
                                   bias=bias_cols[:, m:m + 1]).then_inc(s_kev, 1)

                def exp(b, g):
                    n = b * G + g
                    act.wait_ge(s_sm, n + 1)
                    if not (isinstance(b, int) and b == 0):
                        act.wait_ge(s_ptp, n - G + 1)
                        if g == 0:
                            act.wait_ge(s_pdiag, b)
                    act.activation(pr[:, g, 0:LK], sm[g % 2][:], ACT.Exp, bias=nmax[:, g:g + 1], scale=-1.0,
                                   accum_out=rsum[:, g:g + 1]).then_inc(s_exp, 1)

                def pt_evac(b, g):
                    n = b * G + g
                    act.wait_ge(s_ptp, n + 1)
                    if not (isinstance(b, int) and n < 2):
                        act.wait_ge(s_av, n - 1)
                    act.activation(pt[g % 2][:], ptp[:, 0:2 * P], ACT.Copy).then_inc(s_pt, 1)

                def o_hi(b, t, j):
                    act.wait_ge(s_osum, b + 1)
                    if j == 0 and not (isinstance(t, int) and t == 0):
                        act.wait_ge(s_wo, t)
                    act.activation(othi[:, :, j * S:(j + 1) * S], osum[:], ACT.Copy).then_inc(s_ohi, 1)

                def mask_bias(b, j):
                    if not (isinstance(b, int) and b < 2):
                        act.wait_ge(s_sm, (b - 1) * G)
                    act.activation(mb[j % 2][:], maskb8[:, b, :], ACT.Copy, bias=-3e38, scale=3e38).then_inc(s_mb, 1)

                def xt_hi(t):
                    act.wait_ge(s_xtp, t + 1)
                    if not (isinstance(t, int) and t == 0):
                        act.wait_ge(s_qmm, t)
                    act.activation(xthi[:], extra.rearrange("p (c n) -> p c n", c=KC), ACT.Copy).then_inc(s_xthi, 1)

                def qt_evac(t):
                    act.wait_ge(s_qtp, t + 1)
                    if not (isinstance(t, int) and t == 0):
                        act.wait_ge(s_qbd, t * BT)
                    act.activation(qt[:], extra.rearrange("p (g n) -> p g n", g=G), ACT.Copy).then_inc(s_qt, 1)

                def w_hi_chunks(n):
                    act.wait_ge(s_wraw[n % 2], raw_count(n))
                    for c in range(KC):
                        act.activation(whi[n][:, c, :], wraw[n % 2][:, c, :], ACT.Copy).then_inc(
                            s_whi if c == KC - 1 else s_whi_chunk, 1)

                ctx_hi_at(0, 0)
                for c in range(KC):
                    act.wait_ge(s_wk[c], 16)
                    act.activation(whi[WK][:, c, :], wraw[0][:, c, :], ACT.Copy).then_inc(s_wkhi, 1)
                act.wait_ge(s_biask, 16)
                k_evac(0, 0)
                w_hi_chunks(WQ)
                for m in range(1, 4):
                    k_evac(0, m)
                xt_hi(0)
                act.wait_ge(s_clast, 16)
                act.activation(othi[:, :, 0:B], craw[1][:, :, 0:B], ACT.Copy).then_inc(s_clhi, 1)
                w_hi_chunks(WV)
                ctx_hi_at(0, 1)
                w_hi(WO)
                qt_evac(0)
                act.wait_ge(s_maskin, 16)
                mask_bias(0, 0)

                def body(t, last=False):
                    for j in range(BT):
                        b = t * BT + j
                        more = not (last and j == BT - 1)
                        if more:
                            k_evac(b + 1, 0)
                        exp(b, 0)
                        if not (j == 0 and isinstance(t, int) and t == 0):
                            o_hi(b - 1, t if j > 0 else t - 1, (j + BT - 1) % BT)
                        if more:
                            k_evac(b + 1, 1)
                        exp(b, 1)
                        if j == 1:
                            xt_hi(t + 1)
                        if last and j == 3:
                            act.wait_ge(s_proj, B * 6)
                            w_hi(AV)
                        if more:
                            k_evac(b + 1, 2)
                        pt_evac(b, 0)
                        exp(b, 2)
                        if j == 3 and not last:
                            qt_evac(t + 1)
                        if more:
                            k_evac(b + 1, 3)
                            mask_bias(b + 1, j + 1)
                        pt_evac(b, 1)
                        exp(b, 3)
                        if not (last and j >= BT - 2):
                            ctx_hi_at(t, j + 2)
                        if last and j == 2:
                            act.wait_ge(s_proj, B * 6 - 2)
                            w_hi(AK)
                        pt_evac(b, 2)
                        pt_evac(b, 3)
                        if last and j == 0:
                            act.wait_ge(s_qmm, TILES)
                            w_hi(AQ)

                body(0)
                with act.Fori(1, TILES - 1) as t:
                    body(t)
                body(TILES - 1, last=True)
                o_hi(B - 1, TILES - 1, BT - 1)

            @block.vector
            def _(dve):
                def w_lo(n):
                    dve.wait_ge(s_whi, n)
                    dve.tensor_tensor(wlo[SLOT[n]][:], wraw[n % 2][:], whi[SLOT[n]][:].bitcast(F32),
                                      ALU.subtract).then_inc(s_wlo, 1)

                def ctx_lo(b, j):
                    dve.wait_ge(s_chi, b + 1)
                    dve.tensor_tensor(clo[j % 2][:], craw[j % 2][:], chi[j % 2][:].bitcast(F32),
                                      ALU.subtract).then_inc(s_clo, 1)

                def ln(t, xt):
                    ln_dve_stats(dve, t, xt)
                    dve.wait_ge(s_rstd, t + 1)
                    if not (isinstance(t, int) and t == 0):
                        dve.wait_ge(s_xtp, t)
                    dve.tensor_scalar(xn[:], xt, mv[:, 0:1], rstd[:, 0:1], ALU.subtract,
                                      ALU.mult).then_inc(s_xn, 1)

                def xt_lo(t):
                    dve.wait_ge(s_xthi, t + 1)
                    dve.tensor_tensor(xtlo[:], extra.rearrange("p (c n) -> p c n", c=KC), xthi[:].bitcast(F32),
                                      ALU.subtract).then_inc(s_xtlo, 1)

                def q_rope(t):
                    dve.wait_ge(s_qmm, t + 1)
                    if not (isinstance(t, int) and t == 0):
                        dve.wait_ge(s_qtp, t)
                    dve.tensor_tensor(qb[:], extra, bias[:, R_BQ, :], ALU.add).then_inc(s_qb, 1)
                    dve.wait_ge(s_qb, t + 1)
                    qv = qb[:].rearrange("p (a i) -> p a i", i=16)
                    dve.tensor_tensor(qcos[:].rearrange("p (a i) -> p a i", i=16), qv, cosq, ALU.mult)
                    dve.tensor_tensor(qsin[:].rearrange("p (a i) -> p a i", i=16), qv, sinq,
                                      ALU.mult).then_inc(s_qcos, 1)
                    dve.wait_ge(s_qcos, t + 1)
                    ev, od = slice(0, D // 2), slice(D // 2, D)
                    dve.tensor_tensor(qr[:, :, 0:64], qcos[:, ev].rearrange("p (g n) -> p g n", g=G),
                                      qsin[:, od].rearrange("p (g n) -> p g n", g=G), ALU.subtract)
                    dve.tensor_tensor(qr[:, :, 64:128], qsin[:, ev].rearrange("p (g n) -> p g n", g=G),
                                      qcos[:, od].rearrange("p (g n) -> p g n", g=G), ALU.add).then_inc(s_qr, 1)

                def k_cos(b):
                    dve.wait_ge(s_kev, (b + 1) * 4)
                    dve.tensor_tensor(kcos[:], kb[:], cosk, ALU.mult).then_inc(s_kcos, 1)

                def k_rotate(b, j):
                    dve.wait_ge(s_kcos, b + 1)
                    dve.wait_ge(s_ksin, b + 1)
                    if not (isinstance(b, int) and b < 2):
                        dve.wait_ge(s_sc, (b - 1) * G)
                    pairs = kr[j % 2][:].rearrange("p (a two) n -> p a two n", two=2)
                    for half in range(2):
                        rows = slice(half * 64, half * 64 + 64)
                        dve.tensor_tensor(pairs[0:64, :, half, :], kcos[rows, 0:2, :], ksin[rows, 2:4, :], ALU.subtract)
                        last = dve.tensor_tensor(pairs[64:128, :, half, :], ksin[rows, 0:2, :], kcos[rows, 2:4, :], ALU.add)
                    last.then_inc(s_kr, 1)

                def v_evac(b, j, c):
                    dve.wait_ge(s_proj, b * 6 + 4 + c + 1)
                    if c == 0 and not (isinstance(b, int) and b < 2):
                        dve.wait_ge(s_av, (b - 1) * G)
                    dve.tensor_tensor(v[j % 2][:, c, :], proj[(4 + c) % 3][:], bias[:, R_BV, :],
                                      ALU.add).then_inc(s_vev, 1)

                def masked(b, j, g):
                    n = b * G + g
                    dve.wait_ge(s_sc, n + 1)
                    if g == 0:
                        dve.wait_ge(s_mb, b + 1)
                    if not (isinstance(b, int) and n < 2):
                        dve.wait_ge(s_exp, n - 1)
                    dve.memset(tick[:, g:g + 1], 0.0)
                    dve.tensor_tensor_reduce(sm[g % 2][:], score[g % 2][:, 0:LK], mb[j % 2][:], -BLOW, 3.4e38,
                                             ALU.add, ALU.min, nmax[:, g:g + 1]).then_inc(s_sm, 1)

                def norm(b, g):
                    n = b * G + g
                    dve.wait_ge(s_exp, n + 1)
                    dve.reciprocal(rinv[:, g:g + 1], rsum[:, g:g + 1]).then_inc(s_rinv, 1)
                    dve.wait_ge(s_rinv, n + 1)
                    dve.tensor_scalar(pr[:, g, 0:LK], pr[:, g, 0:LK], rinv[:, g:g + 1], None,
                                      ALU.mult).then_inc(s_norm, 1)

                def o_sum(b):
                    dve.wait_ge(s_last, b + 1)
                    dve.tensor_tensor(olast[:], plast.rearrange("p (g q) -> p g q", g=G),
                                      vlast[:, :, b].unsqueeze(2).to_broadcast([P, G, S]), ALU.mult).then_inc(s_olast, 1)
                    dve.wait_ge(s_olast, b + 1)
                    dve.tensor_tensor(osum[:], av.rearrange("p (g q) -> p g q", g=G), olast[:], ALU.add).then_inc(s_osum, 1)

                def o_lo(b, j):
                    dve.wait_ge(s_ohi, b + 1)
                    dve.tensor_tensor(otlo[:, :, j * S:(j + 1) * S], osum[:],
                                      othi[:, :, j * S:(j + 1) * S].bitcast(F32), ALU.subtract).then_inc(s_olo, 1)

                def add_out(t):
                    dve.wait_ge(s_wo, t + 1)
                    dve.tensor_tensor(x[:, t, :], extra, x[:, t, :], ALU.add).then_inc(s_xwo, 1)
                    dve.wait_ge(s_xwo, t + 1)
                    dve.tensor_tensor(x[:, t, :], x[:, t, :], bias[:, R_BO, :], ALU.add).then_inc(s_xb, 1)

                def w_lo_chunks(n):
                    for c in range(KC):
                        if c < KC - 1:
                            dve.wait_ge(s_whi_chunk, (n - WQ) * (KC - 1) + c + 1)
                        else:
                            dve.wait_ge(s_whi, n)
                        lo = dve.tensor_tensor(wlo[n][:, c, :], wraw[n % 2][:, c, :], whi[n][:, c, :].bitcast(F32),
                                               ALU.subtract)
                    lo.then_inc(s_wlo, 1)

                ctx_lo(0, 0)
                for c in range(KC):
                    dve.wait_ge(s_wkhi, c + 1)
                    dve.tensor_tensor(wlo[WK][:, c, :], wraw[0][:, c, :], whi[WK][:, c, :].bitcast(F32),
                                      ALU.subtract).then_inc(s_wklo, 1)
                dve.wait_ge(s_x0, 16)
                dve.wait_ge(s_zero, 1)
                ln(0, x[:, 0, :])
                w_lo_chunks(WQ)
                dve.wait_ge(s_const, 16)
                xt_lo(0)
                k_cos(0)
                dve.wait_ge(s_clhi, 1)
                dve.tensor_tensor(othi[:, :, B:2 * B], craw[1][:, :, 0:B], othi[:, :, 0:B].bitcast(F32),
                                  ALU.subtract).then_inc(s_cllo, 1)
                w_lo_chunks(WV)
                dve.wait_ge(s_bias, 16)
                q_rope(0)
                dve.wait_ge(s_vl, 1)
                dve.wait_ge(s_biask, 16)
                sums = ptp[:, 0:G * 2 * B].rearrange("p (g s b) -> p g s b", g=G, s=2)
                dve.tensor_tensor(vlast[:], sums[:, :, 0, :], bias_cols[:, 4:4 + G].unsqueeze(2).to_broadcast([P, G, B]),
                                  ALU.add).then_inc(s_vlsb, 1)
                dve.wait_ge(s_vlsb, 1)
                dve.tensor_tensor(vlast[:], sums[:, :, 1, :], vlast[:], ALU.add).then_inc(s_vlsb, 1)
                ctx_lo(1, 1)
                k_rotate(0, 0)
                v_evac(0, 0, 0)
                v_evac(0, 0, 1)
                dve.wait_ge(s_x, 16 * (TILES - 1))

                def body(t, first=False, last=False):
                    for j in range(BT):
                        b = t * BT + j
                        more = not (last and j == BT - 1)
                        masked(b, j, 0)
                        if not (first and j == 0):
                            o_sum(b - 1)
                        masked(b, j, 1)
                        if not (first and j == 0):
                            o_lo(b - 1, (j + BT - 1) % BT)
                        norm(b, 0)
                        masked(b, j, 2)
                        norm(b, 1)
                        if j == 1:
                            xt_lo(t + 1)
                        if last and j == 3:
                            w_lo(AV)
                        if j == 0 and not first:
                            add_out(t - 1)
                        masked(b, j, 3)
                        norm(b, 2)
                        if more:
                            k_cos(b + 1)
                        norm(b, 3)
                        if more:
                            k_rotate(b + 1, j + 1)
                        if not (last and j >= BT - 2):
                            ctx_lo(b + 2, j)
                        if more:
                            v_evac(b + 1, j + 1, 0)
                        if j == 0:
                            ln(t + 1, x[:, 0 if last else t + 1, :])
                        if j == 2 and not last:
                            q_rope(t + 1)
                        if more:
                            v_evac(b + 1, j + 1, 1)
                        if last and j == 0:
                            w_lo(AQ)
                        if last and j == 2:
                            w_lo(AK)
                        if last and j == 3:
                            ln(TILES + 1, x[:, 1, :])

                body(0, first=True)
                with dve.Fori(1, TILES - 1) as t:
                    body(t)
                body(TILES - 1, last=True)
                dve.tensor_tensor(x[:, TILES - 1, :], x[:, TILES - 1, :], bias[:, R_BO, :], ALU.add).then_inc(s_xb, 1)
                o_sum(B - 1)
                o_lo(B - 1, BT - 1)

            @block.tensor
            def _(pe):
                def xn_transposed(t):
                    pe.wait_ge(s_xn, t + 1)
                    if not (isinstance(t, int) and t == 0):
                        pe.wait_ge(s_qt, t)
                    if not (isinstance(t, int) and t <= 1):
                        pe.wait_ge(s_xwo, t - 1)
                    for c in range(KC):
                        last = pe.transpose(extra[:, c * P:(c + 1) * P], xn[:, c * P:(c + 1) * P], ident)
                    last.then_inc(s_xtp, 1)

                def q_product(t):
                    pe.wait_ge(s_xtlo, t + 1)
                    mm3(pe, extra, lambda c: xthi[:, c, :], lambda c: xtlo[:, c, :],
                        lambda c: whi[WQ][:, c, :], lambda c: wlo[WQ][:, c, :]).then_inc(s_qmm, 1)

                def q_transposed(t):
                    pe.wait_ge(s_qr, t + 1)
                    for g in range(G):
                        last = pe.transpose(extra[:, g * P:(g + 1) * P], qr[:, g, :], ident)
                    last.then_inc(s_qtp, 1)

                def wk_chunk(c):
                    pe.wait_ge(s_wklo, c + 1)

                def k_product(b, j, m):
                    if m == 0:
                        pe.wait_ge(s_clo, b + 1)
                    if not (isinstance(b, int) and b == 0 and m < 3):
                        if m == 0:
                            pe.wait_ge(s_kev, b * 4)
                        elif m < 3:
                            pe.wait_ge(s_vev, b * 2 - 2 + m)
                        else:
                            pe.wait_ge(s_kev, b * 4 + 1)
                    mm3(pe, proj[m % 3][:, 0:LKP],
                        lambda c: whi[WK][:, c, m * P:(m + 1) * P], lambda c: wlo[WK][:, c, m * P:(m + 1) * P],
                        lambda c: chi[j % 2][:, c, :], lambda c: clo[j % 2][:, c, :],
                        before=wk_chunk if isinstance(b, int) and b == 0 and m == 0 else None).then_inc(s_proj, 1)

                def v_product(b, j, u, part):
                    psum = proj[(4 + u) % 3][:]
                    if part == 0:
                        pe.wait_ge(s_kev, b * 4 + 2 + u)
                    for c in (0, 1) if part == 0 else (2, 3):
                        hi, lo = (a[j % 2][:, c, u * P:(u + 1) * P] for a in (chi, clo))
                        pe.matmul(psum, hi, whi[WV][:, c, :], start=(c == 0), stop=False)
                        pe.matmul(psum, hi, wlo[WV][:, c, :], start=False, stop=False)
                        last = pe.matmul(psum, lo, whi[WV][:, c, :], start=False, stop=(c == KC - 1))
                    if part == 1:
                        last.then_inc(s_proj, 1)

                def scores(b, j, g):
                    n = b * G + g
                    if g == 0:
                        pe.wait_ge(s_kr, b + 1)
                        pe.wait_ge(s_qbd, b + 1)
                    if not (isinstance(b, int) and n < 2):
                        pe.wait_ge(s_sm, n - 1)
                    pe.matmul(score[g % 2][:, 0:LK], qbd[j % 2][:, g, :], kr[j % 2][:, g, 0:LK],
                              start=True, stop=True).then_inc(s_sc, 1)

                def probs_transposed(b, g):
                    n = b * G + g
                    pe.wait_ge(s_norm, n + 1)
                    if not (isinstance(b, int) and n == 0):
                        pe.wait_ge(s_pt, n)
                    for c in range(2):
                        last = pe.transpose(ptp[:, c * P:(c + 1) * P], pr[:, g, c * P:(c + 1) * P], ident)
                    last.then_inc(s_ptp, 1)

                def attend(b, t, j, g):
                    n = b * G + g
                    pe.wait_ge(s_pt, n + 1)
                    if g == 0:
                        pe.wait_ge(s_vev, b * 2 + 2)
                        if not (isinstance(b, int) and b == 0):
                            pe.wait_ge(s_osum, b)
                    for c in range(2):
                        for h in range(4):
                            cols = slice(h * HD, h * HD + HD)
                            last = pe.matmul(av[cols, g * S:(g + 1) * S],
                                             v[j % 2][:, c, g * P + h * HD:g * P + h * HD + HD],
                                             pt[g % 2][:, c * P + h * S:c * P + h * S + S], start=(c == 0), stop=(c == 1))
                    last.then_inc(s_av, 1)

                def last_spread(b):
                    pe.wait_ge(s_pdiag, b + 1)
                    pe.matmul(plast, const[:, C_SAME:C_SAME + P], pdiag[:].rearrange("p g q -> p (g q)"),
                              start=True, stop=True).then_inc(s_last, 1)

                def self_product(u):
                    if u == 0:
                        pe.wait_ge(s_xtlo, TILES + 1)
                    pe.wait_ge(s_wlo, AQ + u)
                    if u == 0:
                        pe.wait_ge(s_kev, B * 4)
                    else:
                        pe.wait_ge(s_vev, B * 2 - 2 + u)
                    w = SLOT[AQ + u]
                    mm3(pe, bank[u][:], lambda c: xthi[:, c, :], lambda c: xtlo[:, c, :],
                        lambda c: whi[w][:, c, :], lambda c: wlo[w][:, c, :]).then_inc((s_qp, s_kp, s_vp)[u], 1)

                def out_product(t):
                    pe.wait_ge(s_olo, t * BT + BT)
                    if isinstance(t, int) and t == TILES - 1:
                        pe.wait_ge(s_xtlo, TILES + 1)
                    else:
                        pe.wait_ge(s_qt, t + 2)
                    pe.wait_ge(s_wlo, WO)
                    mm3(pe, extra, lambda c: othi[:, c, :], lambda c: otlo[:, c, :],
                        lambda c: whi[WO][:, c, :], lambda c: wlo[WO][:, c, :]).then_inc(s_wo, 1)

                for m in range(4):
                    k_product(0, 0, m)
                pe.wait_ge(s_const, 16)
                xn_transposed(0)
                pe.wait_ge(s_wlo, WQ)
                q_product(0)
                pe.wait_ge(s_wlo, WV)
                pe.wait_ge(s_cllo, 1)
                for g in range(G):
                    for c in range(KC):
                        rows = slice(g * P, (g + 1) * P)
                        pe.matmul(ptp[:, g * 2 * B:(g + 1) * 2 * B], whi[WV][:, c, rows], othi[:, c, 0:2 * B],
                                  start=(c == 0), stop=False)
                        last = pe.matmul(ptp[:, g * 2 * B:g * 2 * B + B], wlo[WV][:, c, rows], othi[:, c, 0:B],
                                         start=False, stop=(c == KC - 1))
                last.then_inc(s_vl, 1)
                v_product(0, 0, 0, 0)
                v_product(0, 0, 0, 1)
                q_transposed(0)
                v_product(0, 0, 1, 0)
                v_product(0, 0, 1, 1)
                pe.wait_ge(s_vlsb, 2)

                def body(t, first=False, last=False):
                    for j in range(BT):
                        b = t * BT + j
                        more = not (last and j == BT - 1)
                        if more:
                            k_product(b + 1, j + 1, 0)
                        scores(b, j, 0)
                        if not (first and j == 0):
                            last_spread(b - 1)
                        if more:
                            k_product(b + 1, j + 1, 1)
                        scores(b, j, 1)
                        if j == 1:
                            xn_transposed(t + 1)
                        if more:
                            k_product(b + 1, j + 1, 2)
                        else:
                            self_product(0)
                        if j % 2 == 0:
                            probs_transposed(b, 0)
                        if j == 0 and not first:
                            out_product(t - 1)
                        scores(b, j, 2)
                        if j % 2 == 1:
                            probs_transposed(b, 0)
                        if j == 3 and not last:
                            q_transposed(t + 1)
                        if more:
                            k_product(b + 1, j + 1, 3)
                        if more:
                            probs_transposed(b, 1)
                        scores(b, j, 3)
                        if not more:
                            probs_transposed(b, 1)
                        if more:
                            v_product(b + 1, j + 1, 0, 0)
                        else:
                            self_product(1)
                        attend(b, t, j, 0)
                        attend(b, t, j, 1)
                        if more:
                            v_product(b + 1, j + 1, 0, 1)
                        probs_transposed(b, 2)
                        if more:
                            v_product(b + 1, j + 1, 1, 0)
                        probs_transposed(b, 3)
                        if more:
                            v_product(b + 1, j + 1, 1, 1)
                        if j == 1 and not last:
                            q_product(t + 1)
                        attend(b, t, j, 2)
                        attend(b, t, j, 3)

                body(0, first=True)
                with pe.Fori(1, TILES - 1) as t:
                    body(t)
                body(TILES - 1, last=True)
                last_spread(B - 1)
                self_product(2)
                out_product(TILES - 1)

        with ExitStack() as ph:
            def sb(name, shape, dt=F32):
                return sbuf(ph, name, shape, dt)

            bias = [craw[r // 2][:].rearrange("p c n -> p (c n)")[:, r % 2 * D:(r % 2 + 1) * D] for r in range(4)]
            qkv = [sb(f"{n}_self", [P, D]) for n in "qkv"]
            qt = sb("qt2", [P, H, S])
            kt = sb("kt2", [P, H, S])
            kbd = sb("kbd", [P, H, P])
            pbd = wraw[0][:].rearrange("p c (h n) -> p (c h) n", n=P)
            sm = sb("sm2", [P, G * BT, S])
            smax = sb("smax2", [P, G * BT])
            ssum = sb("ssum2", [P, G * BT])
            sinv = sb("sinv2", [P, G * BT])
            othi = sb("othi2", [P, G, P], F32R)
            otlo = sb("otlo2", [P, G, P], F32R)
            stats3 = sb("stats3", [P, 6])
            mv3 = sb("mv3", [P, 2])
            vareps3 = sb("vareps3", [P, 1])
            rstd3 = sb("rstd3", [P, 1])
            xn3 = sb("xn3", [P, D])
            expert_lo = sb("expert_lo", [P, NE, KC, D], F32R)
            route_c = wraw[0][:].rearrange("p c n -> p (c n)")[:, 0:R_ALL]
            gate_w = sb("gate_w", [P, KC, NE])
            x3t = sb("x3t", [P, KC, P])
            gate_b = sb("gate_b", [P, NE])
            expert_b = sm[0:NE].rearrange("p a k -> p (a k)")
            expert_b_hi, expert_b_lo = (b[0:NE].rearrange("p c n -> p (c n)") for b in (othi, otlo))
            logits = sb("logits", [P, TILES, NE])
            top8 = sb("top8", [P, TILES, 8])
            idx8 = sb("idx8", [P, TILES, 8], U32)
            expert_of = sb("expert_of", [P, SLOTS], I32)
            gather_row = sb("gather_row", [P, SLOTS], U32)
            add_row = sb("add_row", [P, SLOTS], U32)
            gather_at = [sb(f"gather_at{i}", [P, 1], U32) for i in range(AHEAD)]
            add_at = [sb(f"add_at{i}", [P, 1], U32) for i in range(2)]
            pool_tick = sb("pool_tick", [1, 8])

            used = [R_ALL, 0]

            def carve(*shape, raw=1):
                n = int(np.prod(shape))
                a = wraw[raw][:].rearrange("p c n -> p (c n)")[:, used[raw]:used[raw] + n]
                used[raw] += n
                return a.rearrange("p (a b) -> p a b", b=shape[1]) if len(shape) == 2 else a

            gap, gexp, gden = (carve(TILES, raw=0) for _ in range(3))
            gtop = carve(TILES, 2, raw=0)
            gates, gates_lo = carve(TILES, NE, raw=0), carve(TILES, NE, raw=0)
            gates_hi = sb("gates_hi", [P, TILES, NE], F32R)
            slot_gate = carve(SLOTS, raw=0)
            spare = carve(SLOTS, raw=0)

            K2 = 2 * TILES
            chosen = carve(K2, NE)
            kept = carve(TILES + 1, NE)
            prod = carve(K2, NE)
            rank, place, tile_of, whole = carve(K2), carve(K2), carve(K2), carve(K2)
            more = carve(NE, NE)
            tiles, upto, start = carve(NE), carve(NE, NE), carve(NE)
            cum = carve(NE)
            past = carve(SLOTS, NE)
            expert_f = carve(SLOTS)
            in_tile = carve(K2, SLOTS)
            payload = carve(K2, 2 * SLOTS)
            at_place = kbd
            gates_t_hi, gates_t_lo = xthi[0:NE], xtlo[0:NE]
            xg = [qkv[2], x3t[:].rearrange("p c n -> p (c n)"), xn, xn3]
            expert_raw = expert_lo[:].bitcast(F32)
            expert_hi = wparts
            eyhi, eylo = [xthi, othi], [xtlo, otlo]
            ysb = [qt[:].rearrange("p h q -> p (h q)"), kt[:].rearrange("p h k -> p (h k)")]

            (s_gw, s_gb, s_eb, s_qsb, s_ksb, s_vsb,
             s_qt, s_kt, s_kbd, s_sc, s_causal, s_max, s_msub, s_exp, s_sum, s_sinv, s_norm, s_ptp, s_pbd, s_av, s_ohi,
             s_olo, s_cp, s_xpb, s_xo) = (sem(n) for n in (
                 "gate_w_in", "gate_b_in", "expert_b_in", "self_q_in_sbuf", "self_k_in_sbuf",
                 "self_v_in_sbuf", "self_q_by_batch_d", "self_k_by_batch_d", "self_k_blocks_done", "self_scores_done",
                 "self_scores_masked", "self_max_done", "self_less_max", "self_exp_done", "self_sum_done",
                 "self_sum_inverted", "self_probs_normed", "self_probs_t_done", "self_probs_blocks_done",
                 "self_attn_done",
                 "self_attn_hi_done", "self_attn_lo_done", "self_out_proj_done", "self_x_with_bias",
                 "self_x_with_out_proj"))
            (s_stats3, s_mv3, s_var3, s_rstd3, s_xn3, s_x3t, s_x3d, s_ntp, s_lgp, s_lg, s_ew, s_route_c, s_padded) = (
                sem(n) for n in (
                    "ffn_ln_stats_done", "ffn_ln_mv_done", "ffn_ln_var_done", "ffn_ln_rstd_done", "ffn_ln_xn_done",
                    "ffn_xn_t_in_sbuf", "ffn_xn_stored", "ffn_xn_t_done", "logits_done", "logits_in_sbuf",
                    "expert_weights_in", "route_constants_in", "kept_padded"))
            (s_top, s_idx, s_rt, s_gexp, s_kept, s_rank, s_placed, s_quotient, s_at_place, s_gates, s_gsplit, s_gtp, s_gt, s_ebhi, s_eblo, s_bias, s_xbias,
             s_payload, s_table, s_experts, s_rows, s_init) = (sem(n) for n in (
                 "top_found", "top_index_found", "route_steps", "gate_exp_done", "kept_done", "ranks_done",
                 "places_done", "quotients_done", "place_onehots_done", "gates_done", "gates_split", "gates_t_done", "gates_t_in_sbuf", "expert_bias_hi_done", "expert_bias_lo_done",
                 "expert_bias_done", "x_with_expert_bias", "payload_done", "slot_table_done", "slot_experts_done",
                 "slot_rows_done", "out_initialised"))
            s_gather = [sem(f"slot_tokens_in{i}") for i in range(AHEAD)]
            (s_gcopy, s_acopy, s_ext, s_exhi, s_exlo, s_ewhi, s_ewlo, s_ewlo_pool, s_y, s_yev, s_add) = (sem(n) for n in (
                "gather_rows_copied", "add_rows_copied", "slot_t_done", "slot_t_hi_done", "slot_t_lo_done",
                "expert_hi_done", "expert_lo_by_dve", "expert_lo_by_pool", "slot_products_done", "slot_outputs_in_sbuf",
                "slot_outputs_added"))
            x3_d = nc.dram_tensor("ffn_xn_scratch", [B * S, D], F32, kind="Internal").ap()

            causal = const[:, C_CAUSAL:C_CAUSAL + S].unsqueeze(1).to_broadcast([P, G * BT, S])

            def over_k(a):
                return a.unsqueeze(2).to_broadcast([P, G * BT, S])

            def first(t):
                return isinstance(t, int) and t == 0

            ring = [bank[i][:] for i in range(4)] + [quad[:, i, :] for i in range(4)]
            b_q, b_k, b_v, b_xt, b_score, b_av, b_cp, b_x3 = ring
            bias_bank = (b_score, b_av, b_q, b_k, b_v, b_xt, b_x3, b_score)
            block = ph.enter_context(nc.Block())

            @block.sync
            def _(sp):
                sp.dma_start(gate_w[:], gate_w_in).then_inc(s_gw, 16)
                sp.dma_start(gate_b[:], gate_b_in.unsqueeze(0).partition_broadcast(P)).then_inc(s_gb, 16)
                for e in range(NE):
                    sp.dma_start(expert_raw[:, e, :, :], w_in[E0 + e]).then_inc(s_ew, 16)

                def store_xn3(t):
                    sp.wait_ge(s_xn3, t + 1)
                    sp.dma_start(x3_d[bass.ds(t * P, P), :], xn3[:]).then_inc(s_x3d, 16)

                with sp.Fori(0, TILES - 1) as t:
                    store_xn3(t)
                sp.wait_ge(s_ptp, TILES)
                sp.dma_start(expert_b, expert_b_in).then_inc(s_eb, 16)
                sp.wait_ge(s_av, TILES)
                sp.dma_start(route_c, route_in).then_inc(s_route_c, 16)
                store_xn3(TILES - 1)
                for t in range(TILES):
                    sp.wait_ge(s_xbias, t + 1)
                    sp.dma_start(out[t * P:(t + 1) * P, :], x[:, t, :]).then_inc(s_init, 16)
                sp.dma_start(out[B * S:B * S + P, :], x[:, 0, :]).then_inc(s_init, 16)
                sp.wait_ge(s_init, 16 * (TILES + 1))
                sp.wait_ge(s_add, 16 * SLOTS)

            @block.gpsimd
            def _(pool):
                pool.memset(pool_tick[:], 0.0).then_inc(s_padded, 1)

                def less_max(t):
                    pool.wait_ge(s_max, t + 1)
                    pool.tensor_tensor(sm[:], sm[:], over_k(smax[:]), ALU.subtract).then_inc(s_msub, 1)

                def norm(t):
                    pool.wait_ge(s_sinv, t + 1)
                    pool.tensor_tensor(sm[:], sm[:], over_k(sinv[:]), ALU.mult).then_inc(s_norm, 1)

                def ffn_ln(t):
                    pool.wait_ge(s_var3, t + 1)
                    pool.tensor_tensor(rstd3[:], vareps3[:], neghalf[:], ALU.pow).then_inc(s_rstd3, 1)

                def proj_bias(t):
                    pool.wait_ge(s_xn, TILES + t + 1)
                    pool.tensor_tensor(x[:, t, :], x[:, t, :], bias[R_AP - R_AQ], ALU.add).then_inc(s_xpb, 1)

                def body(t, depth=2, last=False):
                    if depth >= 1:
                        norm(t - 1)
                    if depth >= 2:
                        ffn_ln(t - 2)
                    if depth >= 1 and not last:
                        ln_pool(pool, TILES + t + 1)
                    proj_bias(t)
                    if not last:
                        less_max(t)

                pool.wait_ge(s_bias2, 32)
                body(0, depth=0)
                body(1, depth=1)
                with pool.Fori(2, TILES - 1) as t:
                    body(t)
                body(TILES - 1, last=True)
                pool.wait_ge(s_wlo, AP_)
                pool.memset(kept[:, TILES, :], 0.0).then_inc(s_padded, 1)
                ffn_ln(TILES - 2)

                def expert_lo_part(e):
                    pool.wait_ge(s_ewhi, e + 1)
                    pool.tensor_tensor(expert_lo[:, e, :, :], expert_raw[:, e, :, :],
                                       expert_hi[:, e, :, :].bitcast(F32), ALU.subtract).then_inc(s_ewlo_pool, 1)

                expert_lo_part(POOL_EXPERTS[0])
                ffn_ln(TILES - 1)
                for e in POOL_EXPERTS[1:]:
                    expert_lo_part(e)

                def tick(cell):
                    pool.tensor_tensor(pool_tick[:, cell:cell + 1], pool_tick[:, 7:8], pool_tick[:, 7:8], ALU.add)

                def gather(i, r):
                    if not (isinstance(i, int) and i < AHEAD):
                        pool.wait_ge(s_ext, i - AHEAD + 1)
                        tick(0)
                    pool.tensor_copy(gather_at[r][:], gather_row[:, bass.ds(i, 1)]).then_inc(s_gcopy, 1)
                    pool.wait_ge(s_gcopy, i + 1)
                    tick(1)
                    pool.indirect_dma_start(xg[r][:], None, x3_d, bass.IndirectOffsetOnAxis(ap=gather_at[r][:], axis=0)
                                            ).then_inc(s_gather[r], 16)

                def add(i, r):
                    pool.wait_ge(s_yev, i + 1)
                    tick(2)
                    pool.tensor_copy(add_at[r][:], add_row[:, bass.ds(i, 1)]).then_inc(s_acopy, 1)
                    pool.wait_ge(s_acopy, i + 1)
                    tick(3)
                    if not (isinstance(i, int) and i == 0):
                        pool.wait_ge(s_add, i * 16)
                        tick(4)
                    pool.indirect_dma_start(out, bass.IndirectOffsetOnAxis(ap=add_at[r][:], axis=0), ysb[r][:], None,
                                            compute_op=ALU.add).then_inc(s_add, 16)

                pool.wait_ge(s_rows, 1)
                pool.wait_ge(s_x3d, 16 * TILES)
                for i in range(AHEAD - 1):
                    gather(i, i)
                pool.wait_ge(s_rows, 3)
                pool.wait_ge(s_init, 16 * (TILES + 1))

                def expert_step(i, r):
                    gather(i + AHEAD - 1, (r + AHEAD - 1) % AHEAD)
                    add(i, r % 2)

                for i in range(AHEAD):
                    expert_step(i, i)
                with pool.Fori(1, LAST_ROUND) as k:
                    for r in range(AHEAD):
                        expert_step(k * AHEAD + r, r)
                for i in range(LAST_ROUND * AHEAD, SLOTS):
                    if i + AHEAD - 1 < SLOTS:
                        expert_step(i, i % AHEAD)
                    else:
                        add(i, i % 2)

            @block.scalar
            def _(act):
                def w_hi(n, slot, raw, uses):
                    act.wait_ge(s_wraw[raw], uses)
                    act.activation(whi[slot][:], wraw[raw][:], ACT.Copy).then_inc(s_whi, 1)

                def xt_hi(t):
                    act.wait_ge(s_xtp, TILES + t + 1)
                    act.wait_ge(s_vp, t)
                    act.activation(xthi[:], b_xt.rearrange("p (c n) -> p c n", c=KC), ACT.Copy).then_inc(s_xthi, 1)

                def blocks(dst, src):
                    for b in range(BT):
                        last = act.activation(dst[:].rearrange("p h (b n) -> p h b n", b=BT)[:, :, b, :], src, ACT.Copy,
                                              scale=const[:, C_HMS + b:C_HMS + b + 1])
                    return last

                def k_blocks(t):
                    act.wait_ge(s_kt, t + 1)
                    if not first(t):
                        act.wait_ge(s_sc, t)
                    blocks(kbd, kt[:]).then_inc(s_kbd, 1)

                def p_blocks(t):
                    act.wait_ge(s_ptp, t + 1)
                    if not first(t):
                        act.wait_ge(s_av, t)
                    blocks(pbd, b_xt.rearrange("p (h q) -> p h q", h=H)).then_inc(s_pbd, 1)

                def exp(t):
                    act.wait_ge(s_msub, t + 1)
                    act.activation(sm[:], sm[:], ACT.Exp, scale=A_SCALE).then_inc(s_exp, 1)

                def o_hi(t):
                    act.wait_ge(s_av, t + 1)
                    if not first(t):
                        act.wait_ge(s_cp, t)
                    act.activation(othi[:], b_av.rearrange("p (g n) -> p g n", g=G), ACT.Copy).then_inc(s_ohi, 1)

                def x3_evac(t):
                    act.wait_ge(s_ntp, t + 1)
                    if not first(t):
                        act.wait_ge(s_lgp, t)
                    act.activation(x3t[:], b_x3.rearrange("p (c n) -> p c n", c=KC), ACT.Copy).then_inc(s_x3t, 1)

                def body(t, depth=2, last=False):
                    if depth >= 1:
                        exp(t - 1)
                        p_blocks(t - 1)
                    if depth == 0:
                        xt_hi(t + 1)
                    k_blocks(t)
                    if depth == 0:
                        w_hi(AP_, SLOT[AP_], 1, raw_count(AP_))
                    if depth >= 1:
                        o_hi(t - 1)
                    if depth >= 1 and not last:
                        xt_hi(t + 1)
                    if depth >= 2:
                        x3_evac(t - 2)

                body(0, depth=0)
                body(1, depth=1)
                with act.Fori(2, TILES - 1) as t:
                    body(t)
                body(TILES - 1, last=True)
                exp(TILES - 1)
                p_blocks(TILES - 1)

                def expert_hi_part(e):
                    act.activation(expert_hi[:, e, :, :], expert_raw[:, e, :, :], ACT.Copy).then_inc(s_ewhi, 1)

                act.wait_ge(s_ew, 16 * NE)
                act.wait_ge(s_vp, TILES)
                expert_hi_part(0)
                o_hi(TILES - 1)
                x3_evac(TILES - 2)
                for e in range(1, 6):
                    expert_hi_part(e)
                act.wait_ge(s_cp, TILES)
                expert_hi_part(6)
                x3_evac(TILES - 1)
                expert_hi_part(7)
                act.wait_ge(s_eb, 16)
                act.activation(expert_b_hi, expert_b, ACT.Copy).then_inc(s_ebhi, 1)

                act.wait_ge(s_rt, 2)
                act.activation(gexp, gap, ACT.Exp).then_inc(s_gexp, 1)
                for i in range(4):
                    act.wait_ge(s_gtp, i + 1)
                    if i == 2:
                        act.wait_ge(s_bias, TILES // 2)
                    act.activation((gates_t_hi, gates_t_lo)[i % 2],
                                   (b_q, b_k, b_v, b_xt)[i][0:NE, :].rearrange("p (t n) -> p t n", n=P),
                                   ACT.Copy).then_inc(s_gt, 1)

                def slot_hi(i, r):
                    act.wait_ge(s_ext, i + 1)
                    act.activation(eyhi[r][:], (b_q, b_k)[r].rearrange("p (c n) -> p c n", c=KC),
                                   ACT.Copy).then_inc(s_exhi, 1)

                def gated(i, r):
                    act.wait_ge(s_y, i + 1)
                    if not (isinstance(i, int) and i < 2):
                        act.wait_ge(s_add, (i - 1) * 16)
                    act.activation(ysb[r][:], (b_x3, b_cp)[r], ACT.Copy,
                                   scale=slot_gate[:, bass.ds(i, 1)]).then_inc(s_yev, 1)

                slot_hi(0, 0)
                act.wait_ge(s_rows, 3)

                def expert_step(i, r):
                    slot_hi(i + 1, 1 - r)
                    gated(i, r)

                for r in range(2):
                    expert_step(r, r)
                with act.Fori(1, (SLOTS - 1) // 2) as k:
                    for r in range(2):
                        expert_step(k * 2 + r, r)
                gated(SLOTS - 1, 0)

            @block.vector
            def _(dve):
                def ln_apply(t):
                    dve.wait_ge(s_rstd, TILES + t + 1)
                    dve.wait_ge(s_xtp, TILES + t)
                    dve.tensor_scalar(xn[:], x[:, t, :], mv[:, 0:1], rstd[:, 0:1], ALU.subtract,
                                      ALU.mult).then_inc(s_xn, 1)

                def ffn_ln_stats(t):
                    dve.wait_ge(s_xo, t + 1)
                    dve.memset(tick[:, 0:1], 0.0)
                    dve.bn_stats(stats3[:], x[:, t, :]).then_inc(s_stats3, 1)
                    dve.wait_ge(s_stats3, t + 1)
                    dve.memset(tick[:, 1:2], 0.0)
                    dve.bn_aggr(mv3[:], stats3[:]).then_inc(s_mv3, 1)
                    dve.wait_ge(s_mv3, t + 1)
                    dve.tensor_scalar(vareps3[:], mv3[:, 1:2], EPS, None, ALU.add).then_inc(s_var3, 1)

                def ffn_ln_apply(t):
                    dve.wait_ge(s_rstd3, t + 1)
                    if not first(t):
                        dve.wait_ge(s_ntp, t)
                        dve.wait_ge(s_x3d, t * 16)
                    dve.tensor_scalar(xn3[:], x[:, t, :], mv3[:, 0:1], rstd3[:, 0:1], ALU.subtract,
                                      ALU.mult).then_inc(s_xn3, 1)

                def xt_lo(t):
                    dve.wait_ge(s_xthi, TILES + t + 1)
                    dve.tensor_tensor(xtlo[:], b_xt.rearrange("p (c n) -> p c n", c=KC), xthi[:].bitcast(F32),
                                      ALU.subtract).then_inc(s_xtlo, 1)

                def evac(t, u):
                    dve.wait_ge((s_qp, s_kp, s_vp)[u], t + 1)
                    if not first(t):
                        dve.wait_ge((s_qt, s_kt, s_av)[u], t)
                    dve.tensor_tensor(qkv[u][:], (b_q, b_k, b_v)[u], bias[u],
                                      ALU.add).then_inc((s_qsb, s_ksb, s_vsb)[u], 1)

                def q_by_batch(t):
                    dve.wait_ge(s_qsb, t + 1)
                    if not first(t):
                        dve.wait_ge(s_sc, t)
                    dve.transpose(qt[:].rearrange("p h q -> p (h q)"), qkv[0][:]).then_inc(s_qt, 1)

                def k_by_batch(t):
                    dve.wait_ge(s_ksb, t + 1)
                    if not first(t):
                        dve.wait_ge(s_kbd, t)
                    dve.transpose(kt[:].rearrange("p h k -> p (h k)"), qkv[1][:]).then_inc(s_kt, 1)

                def mask_and_max(t):
                    dve.wait_ge(s_sc, t + 1)
                    if not first(t):
                        dve.wait_ge(s_ptp, t)
                    dve.tensor_tensor(sm[:], b_score.rearrange("p (a k) -> p a k", k=S), causal,
                                      ALU.add).then_inc(s_causal, 1)
                    dve.wait_ge(s_causal, t + 1)
                    dve.tensor_reduce(smax[:], sm[:], AX.X, ALU.max).then_inc(s_max, 1)

                def less_max(t):
                    dve.wait_ge(s_max, t + 1)
                    dve.tensor_tensor(sm[:], sm[:], over_k(smax[:]), ALU.subtract).then_inc(s_msub, 1)

                def norm(t):
                    dve.wait_ge(s_sinv, t + 1)
                    dve.tensor_tensor(sm[:], sm[:], over_k(sinv[:]), ALU.mult).then_inc(s_norm, 1)

                def inverse_sum(t):
                    dve.wait_ge(s_exp, t + 1)
                    dve.tensor_reduce(ssum[:], sm[:], AX.X, ALU.add).then_inc(s_sum, 1)
                    dve.wait_ge(s_sum, t + 1)
                    dve.reciprocal(sinv[:], ssum[:]).then_inc(s_sinv, 1)

                def o_lo(t):
                    dve.wait_ge(s_ohi, t + 1)
                    dve.tensor_tensor(otlo[:], b_av.rearrange("p (g n) -> p g n", g=G), othi[:].bitcast(F32),
                                      ALU.subtract).then_inc(s_olo, 1)

                def add_out(t):
                    dve.wait_ge(s_cp, t + 1)
                    dve.wait_ge(s_xpb, t + 1)
                    dve.tensor_tensor(x[:, t, :], b_cp, x[:, t, :], ALU.add).then_inc(s_xo, 1)

                def logits_evac(t):
                    dve.wait_ge(s_lgp, t + 1)
                    dve.tensor_tensor(logits[:, t, :], b_x3[:, 0:NE], gate_b[:], ALU.add).then_inc(s_lg, 1)

                def cross_add_out():
                    dve.wait_ge(s_wo, TILES)
                    dve.wait_ge(s_xb, TILES)
                    dve.tensor_tensor(x[:, TILES - 1, :], b_cp, x[:, TILES - 1, :], ALU.add).then_inc(s_xwo, 1)

                dve.wait_ge(s_bias2, 32)

                def body(t, depth=2, last=False, before_mask=None):
                    if depth >= 2:
                        add_out(t - 2)
                    if depth >= 1:
                        inverse_sum(t - 1)
                    if depth >= 2:
                        ffn_ln_stats(t - 2)
                    if depth >= 3:
                        logits_evac(t - 3)
                    evac(t, 0)
                    if depth == 0:
                        xt_lo(t + 1)
                    q_by_batch(t)
                    if depth >= 2:
                        ffn_ln_apply(t - 2)
                    if depth >= 1 and not last:
                        ln_dve_stats(dve, TILES + t + 1, x[:, t + 1, :])
                    evac(t, 1)
                    k_by_batch(t)
                    if depth >= 1 and not last:
                        ln_apply(t + 1)
                    evac(t, 2)
                    if depth >= 1:
                        o_lo(t - 1)
                    if before_mask is not None:
                        before_mask()
                    mask_and_max(t)
                    if depth == 0:
                        dve.wait_ge(s_whi, AP_)
                        dve.tensor_tensor(wlo[SLOT[AP_]][:], wraw[AP_ % 2][:], whi[SLOT[AP_]][:].bitcast(F32),
                                          ALU.subtract).then_inc(s_wlo, 1)
                    if depth >= 1 and not last:
                        xt_lo(t + 1)

                body(0, depth=0, before_mask=cross_add_out)
                body(1, depth=1)
                body(2, depth=2)
                dve.wait_ge(s_gb, 16)
                with dve.Fori(3, TILES - 1) as t:
                    body(t, depth=3)
                body(TILES - 1, depth=3, last=True)
                T = TILES - 1

                def top(t):
                    dve.wait_ge(s_lg, t + 1)
                    dve.max(top8[:, t, :], logits[:, t, :]).then_inc(s_top, 1)
                    dve.wait_ge(s_top, t + 1)
                    dve.max_index(idx8[:, t, :], top8[:, t, :], logits[:, t, :]).then_inc(s_idx, 1)

                less_max(T)
                inverse_sum(T)
                norm(T)
                add_out(T - 1)
                ffn_ln_stats(T - 1)
                logits_evac(T - 2)
                ffn_ln_apply(T - 1)
                o_lo(T)
                for t in range(T - 1):
                    top(t)

                def expert_lo_part(e):
                    dve.wait_ge(s_ewhi, e + 1)
                    dve.tensor_tensor(expert_lo[:, e, :, :], expert_raw[:, e, :, :],
                                      expert_hi[:, e, :, :].bitcast(F32), ALU.subtract).then_inc(s_ewlo, 1)

                expert_lo_part(0)
                logits_evac(T - 1)
                expert_lo_part(1)
                add_out(T)
                ffn_ln_stats(T)
                ffn_ln_apply(T)
                top(T - 1)
                logits_evac(T)
                top(T)

                def rc(at, n):
                    return route_c[:, at:at + n]

                dve.wait_ge(s_idx, TILES)
                dve.tensor_copy(rank.rearrange("p (t k) -> p t k", k=2), idx8[:, :, 0:2]).then_inc(s_rt, 1)
                dve.tensor_tensor(gap, top8[:, :, 1], top8[:, :, 0], ALU.subtract).then_inc(s_rt, 1)
                dve.wait_ge(s_route_c, 16)
                dve.wait_ge(s_rt, 2)
                dve.tensor_tensor(chosen, rc(R_IOTA, NE).unsqueeze(1).to_broadcast([P, K2, NE]),
                                  rank.unsqueeze(2).to_broadcast([P, K2, NE]), ALU.is_equal).then_inc(s_rt, 1)
                dve.wait_ge(s_rt, 3)
                by_choice = chosen.rearrange("p (t k) e -> p t k e", k=2)
                dve.wait_ge(s_padded, 2)
                dve.tensor_tensor(kept[:, 0:TILES, :], by_choice[:, :, 0, :], by_choice[:, :, 1, :],
                                  ALU.add).then_inc(s_kept, 1)
                dve.wait_ge(s_gexp, 1)
                dve.tensor_scalar(gden, gexp, 1.0, None, ALU.add).then_inc(s_rt, 1)
                dve.wait_ge(s_rt, 4)
                dve.reciprocal(gtop[:, :, 0], gden).then_inc(s_rt, 1)
                dve.wait_ge(s_rt, 5)
                dve.tensor_tensor(gtop[:, :, 1], gexp, gtop[:, :, 0], ALU.mult).then_inc(s_rt, 1)
                dve.wait_ge(s_rt, 6)
                gate = gtop.rearrange("p t k -> p (t k)")
                dve.tensor_tensor(prod, chosen, gate.unsqueeze(2).to_broadcast([P, K2, NE]), ALU.mult).then_inc(s_rt, 1)
                dve.wait_ge(s_rt, 7)
                by_choice = prod.rearrange("p (t k) e -> p t k e", k=2)
                dve.tensor_tensor(gates, by_choice[:, :, 0, :], by_choice[:, :, 1, :], ALU.add).then_inc(s_gates, 1)
                dve.wait_ge(s_gates, 1)
                dve.tensor_copy(gates_hi[:], gates).then_inc(s_gsplit, 1)
                dve.wait_ge(s_gsplit, 1)
                dve.tensor_tensor(gates_lo, gates, gates_hi[:].bitcast(F32), ALU.subtract).then_inc(s_gsplit, 1)
                dve.wait_ge(s_ebhi, 1)
                dve.tensor_tensor(expert_b_lo, expert_b, expert_b_hi.bitcast(F32), ALU.subtract).then_inc(s_eblo, 1)
                ranks = b_x3[:, 0:(TILES + 1) * NE].rearrange("p (t e) -> p t e", e=NE)
                dve.wait_ge(s_rank, 1)
                dve.wait_ge(s_gates, 1)
                dve.tensor_tensor(prod.rearrange("p (t k) e -> p t k e", k=2),
                                  chosen.rearrange("p (t k) e -> p t k e", k=2),
                                  ranks[:, 0:TILES, :].unsqueeze(2).to_broadcast([P, TILES, 2, NE]),
                                  ALU.mult).then_inc(s_rt, 1)
                dve.tensor_tensor(more, ranks[:, TILES, :].unsqueeze(2).to_broadcast([P, NE, NE]),
                                  rc(R_TILE, NE).unsqueeze(1).to_broadcast([P, NE, NE]), ALU.is_gt).then_inc(s_rt, 1)
                dve.wait_ge(s_rt, 9)
                dve.tensor_reduce(rank, prod, AX.X, ALU.add).then_inc(s_rt, 1)
                dve.tensor_reduce(tiles, more, AX.X, ALU.add).then_inc(s_rt, 1)
                dve.wait_ge(s_rt, 11)
                dve.tensor_tensor(prod[:, :, 0:NE - 1], rank.unsqueeze(2).to_broadcast([P, K2, NE - 1]),
                                  rc(R_TILE + 1, NE - 1).unsqueeze(1).to_broadcast([P, K2, NE - 1]),
                                  ALU.is_ge).then_inc(s_quotient, 1)
                dve.wait_ge(s_quotient, 1)
                dve.tensor_reduce(whole, prod[:, :, 0:NE - 1], AX.X, ALU.add).then_inc(s_quotient, 1)
                dve.wait_ge(s_quotient, 2)
                dve.scalar_tensor_tensor(place, whole, -float(P), rank, ALU.mult, ALU.add).then_inc(s_placed, 1)
                dve.tensor_tensor(upto, rc(R_UPTO, NE * NE).rearrange("p (a b) -> p a b", b=NE),
                                  tiles.unsqueeze(1).to_broadcast([P, NE, NE]), ALU.mult).then_inc(s_rt, 1)
                dve.wait_ge(s_rt, 12)
                dve.tensor_reduce(cum, upto, AX.X, ALU.add).then_inc(s_rt, 1)
                dve.wait_ge(s_rt, 13)
                dve.tensor_tensor(start, cum, tiles, ALU.subtract).then_inc(s_rt, 1)
                dve.tensor_tensor(past, rc(R_IOTA, SLOTS).unsqueeze(2).to_broadcast([P, SLOTS, NE]),
                                  cum.unsqueeze(1).to_broadcast([P, SLOTS, NE]), ALU.is_ge).then_inc(s_rt, 1)
                dve.wait_ge(s_rt, 15)
                dve.tensor_tensor(prod, chosen, start.unsqueeze(1).to_broadcast([P, K2, NE]), ALU.mult).then_inc(s_rt, 1)
                dve.tensor_reduce(expert_f, past, AX.X, ALU.add).then_inc(s_rt, 1)
                dve.wait_ge(s_rt, 17)
                dve.tensor_reduce(tile_of, prod, AX.X, ALU.add).then_inc(s_rt, 1)
                dve.tensor_scalar(expert_of[:], expert_f, float(NE - 1), None, ALU.min).then_inc(s_experts, 1)
                dve.wait_ge(s_rt, 18)
                dve.tensor_tensor(tile_of, whole, tile_of, ALU.add).then_inc(s_rt, 1)
                dve.wait_ge(s_rt, 19)
                dve.tensor_tensor(in_tile, rc(R_IOTA, SLOTS).unsqueeze(1).to_broadcast([P, K2, SLOTS]),
                                  tile_of.unsqueeze(2).to_broadcast([P, K2, SLOTS]), ALU.is_equal).then_inc(s_rt, 1)
                dve.wait_ge(s_rt, 20)
                token = rc(R_TOKEN, TILES).unsqueeze(2).unsqueeze(3).to_broadcast([P, TILES, 2, SLOTS])
                dve.tensor_tensor(payload[:, :, 0:SLOTS].rearrange("p (t k) i -> p t k i", k=2),
                                  in_tile.rearrange("p (t k) i -> p t k i", k=2), token, ALU.mult).then_inc(s_payload, 1)
                dve.tensor_tensor(payload[:, :, SLOTS:2 * SLOTS], in_tile,
                                  gate.unsqueeze(2).to_broadcast([P, K2, SLOTS]), ALU.mult).then_inc(s_payload, 1)
                dve.wait_ge(s_sc, TILES)
                dve.wait_ge(s_placed, 1)
                for i in range(4):
                    part = slice(i * K2 // 4, (i + 1) * K2 // 4)
                    dve.tensor_tensor(at_place[:, part, :], place[:, part].unsqueeze(2).to_broadcast([P, K2 // 4, P]),
                                      rc(R_IOTA, P).unsqueeze(1).to_broadcast([P, K2 // 4, P]),
                                      ALU.is_equal).then_inc(s_at_place, 1)
                for e in range(POOL_EXPERTS[-1] + 1, NE):
                    expert_lo_part(e)

                number = b_cp[:, 0:SLOTS]
                dve.wait_ge(s_table, 1)
                dve.tensor_scalar(gather_row[:], number, 1.0, 1.0, ALU.max, ALU.subtract).then_inc(s_rows, 1)
                dve.tensor_copy(slot_gate, b_cp[:, SLOTS:2 * SLOTS]).then_inc(s_rows, 1)
                dve.tensor_scalar(spare, number, 0.0, rc(R_SPARE, 1), ALU.is_equal, ALU.mult).then_inc(s_rt, 1)
                dve.wait_ge(s_rt, 21)
                dve.scalar_tensor_tensor(add_row[:], number, -1.0, spare, ALU.add, ALU.add).then_inc(s_rows, 1)

                def slot_lo(i, r):
                    dve.wait_ge(s_exhi, i + 1)
                    dve.tensor_tensor(eylo[r][:], (b_q, b_k)[r].rearrange("p (c n) -> p c n", c=KC),
                                      eyhi[r][:].bitcast(F32), ALU.subtract).then_inc(s_exlo, 1)

                def expert_bias(t):
                    dve.wait_ge(s_bias, t + 1)
                    dve.tensor_tensor(x[:, t, :], bias_bank[t], x[:, t, :],
                                      ALU.add).then_inc(s_xbias, 1)

                for t in range(TILES):
                    expert_bias(t)
                slot_lo(0, 0)
                with dve.Fori(1, SLOTS // 2 + 1) as k:
                    for r in range(2):
                        slot_lo(k * 2 - 1 + r, 1 - r)

            @block.tensor
            def _(pe):
                def four_transposes(dst, src):
                    for c in range(KC):
                        last = pe.transpose(dst[:, c * P:(c + 1) * P], src[:, c * P:(c + 1) * P], ident)
                    return last

                def xn_transposed(t):
                    pe.wait_ge(s_xn, TILES + t + 1)
                    if not (isinstance(t, int) and t <= 1):
                        pe.wait_ge(s_pbd, t - 1)
                    four_transposes(b_xt, xn).then_inc(s_xtp, 1)

                def qkv_product(t, u):
                    if u == 0:
                        pe.wait_ge(s_xtlo, TILES + t + 1)
                    pe.wait_ge((s_qsb, s_ksb, s_vsb)[u], t)
                    w = SLOT[AQ + u]
                    mm3(pe, (b_q, b_k, b_v)[u], lambda c: xthi[:, c, :], lambda c: xtlo[:, c, :],
                        lambda c: whi[w][:, c, :], lambda c: wlo[w][:, c, :]).then_inc((s_qp, s_kp, s_vp)[u], 1)

                def scores(t):
                    pe.wait_ge(s_kbd, t + 1)
                    pe.wait_ge(s_qt, t + 1)
                    if not first(t):
                        pe.wait_ge(s_causal, t)
                    for h in range(H):
                        rows, cols = slice(h % 4 * S, h % 4 * S + S), slice(h // 4 * P, h // 4 * P + P)
                        last = pe.matmul(b_score[rows, cols], qt[:, h, :], kbd[:, h, :], start=True, stop=True)
                    last.then_inc(s_sc, 1)

                def probs_transposed(t):
                    pe.wait_ge(s_norm, t + 1)
                    four_transposes(b_xt, sm[:].rearrange("p a k -> p (a k)")).then_inc(s_ptp, 1)

                def attend(t):
                    pe.wait_ge(s_pbd, t + 1)
                    pe.wait_ge(s_vsb, t + 1)
                    if not first(t):
                        pe.wait_ge(s_olo, t)
                    for h in range(H):
                        rows, cols = slice(h % 4 * HD, h % 4 * HD + HD), slice(h // 4 * P, h // 4 * P + P)
                        last = pe.matmul(b_av[rows, cols], qkv[2][:, h * HD:(h + 1) * HD], pbd[:, h, :],
                                         start=True, stop=True)
                    last.then_inc(s_av, 1)

                def out_product(t):
                    pe.wait_ge(s_olo, t + 1)
                    if first(t):
                        pe.wait_ge(s_xwo, TILES)
                        pe.wait_ge(s_wlo, AP_)
                    else:
                        pe.wait_ge(s_xo, t)
                    mm3(pe, b_cp, lambda c: othi[:, c, :], lambda c: otlo[:, c, :],
                        lambda c: whi[3][:, c, :], lambda c: wlo[3][:, c, :]).then_inc(s_cp, 1)

                def x3_transposed(t):
                    pe.wait_ge(s_xn3, t + 1)
                    if not first(t):
                        pe.wait_ge(s_lg, t)
                    four_transposes(b_x3, xn3).then_inc(s_ntp, 1)

                def narrow(psum, a, b, start, stop):
                    for q in range(0, P, P // 4):
                        last = pe.matmul(psum[q:q + P // 4], a[:, q:q + P // 4], b, start=start, stop=stop)
                    return last

                def gate_logits(t):
                    pe.wait_ge(s_x3t, t + 1)
                    if first(t):
                        pe.wait_ge(s_gw, 16)
                    for c in range(KC):
                        last = narrow(b_x3[:, 0:NE], x3t[:, c, :], gate_w[:, c, :], c == 0, c == KC - 1)
                    last.then_inc(s_lgp, 1)

                def body(t, depth=2, last=False):
                    qkv_product(t, 0)
                    if depth >= 2:
                        probs_transposed(t - 1)
                    if depth == 1:
                        scores(t - 1)
                    qkv_product(t, 1)
                    qkv_product(t, 2)
                    if depth == 1:
                        probs_transposed(t - 1)
                    attend(t - 1)
                    if depth >= 2:
                        x3_transposed(t - 2)
                    scores(t)
                    if not last:
                        xn_transposed(t + 1)
                    out_product(t - 1)
                    if depth >= 2:
                        gate_logits(t - 2)

                xn_transposed(1)
                body(1, depth=1)
                body(2, depth=2)
                with pe.Fori(3, TILES - 1) as t:
                    body(t)
                body(TILES - 1, last=True)
                T = TILES - 1
                probs_transposed(T)
                x3_transposed(T - 1)
                attend(T)
                gate_logits(T - 1)
                out_product(T)
                x3_transposed(T)
                gate_logits(T)

                def rc(at, n):
                    return route_c[:, at:at + n]

                pe.wait_ge(s_kept, 1)
                pe.wait_ge(s_route_c, 16)
                ranks = b_x3[:, 0:(TILES + 1) * NE]
                narrow(ranks, rc(R_BEFORE, P), kept.rearrange("p t e -> p (t e)"), True, False)
                for t in range(TILES):
                    after = TILES - t
                    last = narrow(b_x3[:, (t + 1) * NE:(TILES + 1) * NE].rearrange("p (t e) -> p t e", e=NE),
                                  rc(R_ONES, P), kept[:, t, :].unsqueeze(1).to_broadcast([P, after, NE]),
                                  False, t == TILES - 1)
                last.then_inc(s_rank, 1)
                for i in range(4):
                    pe.wait_ge(s_gsplit, i % 2 + 1)
                    part = (gates_hi[:].bitcast(F32), gates_lo)[i % 2]
                    for t in range(4):
                        last = pe.transpose((b_q, b_k, b_v, b_xt)[i][0:NE, t * P:(t + 1) * P],
                                            part[:, i // 2 * 4 + t, :], ident)
                    last.then_inc(s_gtp, 1)

                def bias_product(t):
                    if t % 4 == 0:
                        pe.wait_ge(s_gt, t // 2 + 2)
                    if t == 6:
                        pe.wait_ge(s_rt, 9)
                    if t == 7:
                        pe.wait_ge(s_xbias, 1)
                    mm3(pe, bias_bank[t], lambda c: gates_t_hi[:, t % 4, :], lambda c: gates_t_lo[:, t % 4, :],
                        lambda c: expert_b_hi, lambda c: expert_b_lo, chunks=1).then_inc(s_bias, 1)

                pe.wait_ge(s_eblo, 1)
                for t in range(4):
                    bias_product(t)
                pe.wait_ge(s_payload, 2)
                pe.wait_ge(s_xo, TILES)
                for j in range(K2):
                    if j % (K2 // 4) == 0:
                        pe.wait_ge(s_at_place, j // (K2 // 4) + 1)
                    last = narrow(b_cp[:, 0:2 * SLOTS], at_place[:, j, :], payload[:, j, :], j == 0, j == K2 - 1)
                last.then_inc(s_table, 1)
                for t in range(4, TILES):
                    bias_product(t)

                def slot_transposed(i, r, g):
                    pe.wait_ge(s_gather[r], (g + 1) * 16)
                    if not (isinstance(i, int) and i < 2):
                        pe.wait_ge(s_exlo, i - 1)
                    four_transposes((b_q, b_k)[r % 2], xg[r]).then_inc(s_ext, 1)

                def slot_product(i, r):
                    e = pe.value_load(expert_of[0:1, bass.ds(i, 1)], min_val=0, max_val=NE - 1)
                    pe.wait_ge(s_exlo, i + 1)
                    if not (isinstance(i, int) and i < 2):
                        pe.wait_ge(s_yev, i - 1)
                    mm3(pe, (b_x3, b_cp)[r], lambda c: eyhi[r][:, c, :], lambda c: eylo[r][:, c, :],
                        lambda c: expert_hi[:, e, c, :], lambda c: expert_lo[:, e, c, :]).then_inc(s_y, 1)

                pe.wait_ge(s_xbias, 7)
                pe.wait_ge(s_rows, 3)
                pe.wait_ge(s_experts, 1)
                pe.wait_ge(s_ewlo_pool, len(POOL_EXPERTS))
                pe.wait_ge(s_ewlo, NE - len(POOL_EXPERTS))
                slot_transposed(0, 0, 0)

                def expert_step(i, r, g):
                    slot_transposed(i + 1, (r + 1) % AHEAD, g + (r + 1) // AHEAD)
                    slot_product(i, r % 2)

                for i in range(AHEAD):
                    expert_step(i, i, 0)
                with pe.Fori(1, LAST_ROUND) as k:
                    for r in range(AHEAD):
                        expert_step(k * AHEAD + r, r, k)
                for i in range(LAST_ROUND * AHEAD, SLOTS):
                    if i + 1 < SLOTS:
                        expert_step(i, i % AHEAD, i // AHEAD)
                    else:
                        slot_product(i, i % 2)


def kernel(**inputs):
    import numpy as _np
    import concourse.bacc as _bacc
    from concourse import mybir as _mybir
    from concourse.bass_utils import run_bass_kernel_spmd as _run

    a = {k: _np.asarray(v) for k, v in inputs.items()}

    def chunks(w):
        return w.reshape(KC, P, -1).transpose(1, 0, 2)

    def even_odd(w):
        return w.reshape(-1, H, HD // 2, 2).transpose(0, 3, 1, 2).reshape(w.shape)

    wkv, bkv = a["L0_xattn_Wkv"], a["L0_xattn_bkv"]
    wa, ba = a["L0_attn_c_attn_kernel"], a["L0_attn_c_attn_bias"]
    mats = [even_odd(wkv[:, :D]), even_odd(a["L0_xattn_Wq"]), wkv[:, D:], a["L0_xattn_Wo"],
            wa[:D].T, wa[D:2 * D].T, wa[2 * D:].T, a["L0_attn_c_proj_kernel"].T, *a["L0_ffn_expert_w"]]
    ctx = a["ctx_1024"]
    ctx_t = _np.zeros((B, P, KC, LKP), _np.float32)
    ctx_t[:, :, :, :LK] = ctx.reshape(B, LK, KC, P).transpose(0, 3, 2, 1)
    ctx_last = ctx[:, LK - 1, :].reshape(B, KC, P).transpose(2, 1, 0)
    arrays = {
        "x": a["x"].reshape(B * S, D),
        "ctx_t": ctx_t,
        "ctx_last": ctx_last,
        "mask": a["mask_BxS2_bf1"].view(_np.uint8),
        "weights": _np.stack([chunks(m) for m in mats]),
        "biases": _np.stack([even_odd(a["L0_xattn_bq"][None])[0], bkv[D:], a["L0_xattn_bo"], ba[:D], ba[D:2 * D],
                             ba[2 * D:], a["L0_attn_c_proj_bias"]]),
        "bias_cols": _np.concatenate([even_odd(bkv[None, :D])[0].reshape(4, P).T, bkv[D:].reshape(G, P).T], 1),
        "gate_w": chunks(a["L0_ffn_gate_w"].T),
        "gate_b": a["L0_ffn_gate_b"],
        "expert_b": a["L0_ffn_expert_b"],
        "constants": constants(),
        "route_constants": route_constants(),
    }
    arrays = {f"{k}_dram": _np.ascontiguousarray(v) for k, v in arrays.items()}
    nc = _bacc.Bacc("TRN2", target_bir_lowering=False, num_devices=1)
    args = [nc.dram_tensor(k, v.shape, _mybir.dt.from_np(v.dtype), kind="ExternalInput").ap() for k, v in arrays.items()]
    out = nc.dram_tensor("out_dram", [B * S + P, D], _mybir.dt.float32, kind="ExternalOutput").ap()
    perceiver(nc, *args, out)
    r = _run(nc, [arrays], core_ids=[0])
    return r.results[0]["out_dram"][:B * S].reshape(B, S, D)
```
